# Optimizing a Trainium2 kernel written in Bass

```python
import numpy as np
import jax
import jax.numpy as jnp

def _softmax(x, axis=-1):
    return jax.nn.softmax(x, axis=axis)

def _gelu(x):
    return jax.nn.gelu(x, approximate=True)

def _silu(x):
    return jax.nn.silu(x)

def _sigmoid(x):
    return jax.nn.sigmoid(x)

def _layernorm(x, axis=-1, eps=1e-05):
    m = jnp.mean(x, axis=axis, keepdims=True)
    v = jnp.var(x, axis=axis, keepdims=True)
    return (x - m) / jnp.sqrt(v + eps)

def _scatter_add(tgt, idx, src, axis=0):
    return tgt.at[idx].add(src)

def _segment_sum(src, seg, n):
    return jax.ops.segment_sum(src, seg, n)
kernel_name = 'mk_seq_preln_d1_jaxref_r4_605610'

def setup_inputs(seed: int=0):
    np.random.seed(seed)
    _w = jnp.asarray

    def _L0_attn_setup():
        import jax, jax.numpy as jnp
        import numpy as np
        HID, H, KV, D = (512, 16, 4, 128)
        ROPE_THETA = 10000.0
        GATE_NORM = 16.0

        def _rope_cos_sin(n, d, dtype=jnp.float32):
            inv_freq = 1.0 / ROPE_THETA ** (jnp.arange(0, d, 2, dtype=jnp.float32) / d)
            freqs = jnp.arange(n, dtype=jnp.float32)[:, None] * inv_freq[None, :]
            cos = jnp.cos(freqs).astype(dtype)[None, :, None, :]
            sin = jnp.sin(freqs).astype(dtype)[None, :, None, :]
            return (cos, sin)

        def _apply_rotary(x, cos, sin):
            x1, x2 = jnp.split(x, 2, axis=-1)
            return jnp.concatenate([x1 * cos - x2 * sin, x2 * cos + x1 * sin], axis=-1)

        def _forward(hidden_states, Wq, Wk, Wv, Wo):
            b, n, _ = hidden_states.shape
            groups = H // KV
            q = hidden_states @ Wq
            k = hidden_states @ Wk
            v = hidden_states @ Wv
            g = k
            q = q.reshape(b, n, H, D)
            k = k.reshape(b, n, KV, D)
            v = v.reshape(b, n, KV, D)
            g = g.reshape(b, n, KV, D)
            k = jnp.repeat(k, groups, axis=2)
            v = jnp.repeat(v, groups, axis=2)
            g = jnp.repeat(g, groups, axis=2)
            sq, sk, sv = (q, k, v)
            qs = jax.nn.softmax(q.astype(jnp.float32), axis=-1)
            ks = jax.nn.softmax(k.astype(jnp.float32), axis=-1)
            gl = jax.nn.log_sigmoid(g.astype(jnp.float32)) / GATE_NORM
            cos, sin = _rope_cos_sin(n, D)
            sq = _apply_rotary(sq, cos, sin)
            sk = _apply_rotary(sk, cos, sin)

            def step(S, inp):
                q_t, k_t, v_t, g_t = inp
                S = S * jnp.exp(g_t)[..., None] + k_t[..., None] * v_t[..., None, :]
                o_t = jnp.einsum('bhk,bhkv->bhv', q_t, S)
                return (S, o_t)
            xs = tuple((jnp.moveaxis(a, 1, 0) for a in (qs, ks, v, gl)))
            S0 = jnp.zeros((b, H, D, D), dtype=jnp.float32)
            _, o_gla = jax.lax.scan(step, S0, xs)
            o_gla = jnp.moveaxis(o_gla, 0, 1)
            scale = D ** (-0.5)
            scores = jnp.einsum('bqhd,bkhd->bhqk', sq, sk) * scale
            causal = jnp.tril(jnp.ones((n, n), dtype=bool))
            scores = jnp.where(causal[None, None], scores, jnp.finfo(scores.dtype).min)
            attn = jax.nn.softmax(scores, axis=-1)
            y = jnp.einsum('bhqk,bkhd->bqhd', attn, sv)
            o = 0.5 * y + 0.5 * o_gla
            o = o.reshape(b, n, H * D).astype(hidden_states.dtype)
            return o @ Wo
        key = jax.random.key(seed)
        k1, k2, k3, k4, k5 = jax.random.split(key, 5)
        s = 0.02
        return {'hidden_states': jax.random.normal(k1, (1, 512, HID), dtype=jnp.float32), 'Wq': jax.random.normal(k2, (HID, H * D), dtype=jnp.float32) * s, 'Wk': jax.random.normal(k3, (HID, KV * D), dtype=jnp.float32) * s, 'Wv': jax.random.normal(k4, (HID, KV * D), dtype=jnp.float32) * s, 'Wo': jax.random.normal(k5, (H * D, HID), dtype=jnp.float32) * s}
    _L0_attn_in = _L0_attn_setup()

    def _L0_ffn_setup():
        import math
        import jax, jax.numpy as jnp
        import numpy as np
        from jax import lax
        D = 512
        I = 256
        E = 32
        K = 4
        NG = 8
        TKG = 3
        NSH = 2
        SCALE = 2.5
        CF = 1.25
        B, S = (2, 512)

        def _router(x, router_w, e_bias):
            scores = jax.nn.sigmoid(x @ router_w.T)
            sc = scores + e_bias[None, :]
            T = x.shape[0]
            gs = sc.reshape(T, NG, E // NG)
            group_scores = lax.top_k(gs, 2)[0].sum(-1)
            _, gidx = lax.top_k(group_scores, TKG)
            gmask = jnp.zeros((T, NG), sc.dtype).at[jnp.arange(T)[:, None], gidx].set(1.0)
            smask = jnp.repeat(gmask, E // NG, axis=1)
            masked = jnp.where(smask > 0, sc, 0.0)
            _, topk_idx = lax.top_k(masked, K)
            topk_w = jnp.take_along_axis(scores, topk_idx, axis=1)
            topk_w = topk_w / (topk_w.sum(-1, keepdims=True) + 1e-20)
            topk_w = topk_w * SCALE
            return (topk_idx.astype(jnp.int32), topk_w)

        def _moe_forward(hidden_states, router_w, e_bias, W_gate, W_up, W_down, shared_gate, shared_up, shared_down):
            b, s, d = hidden_states.shape
            T = b * s
            C = int(math.ceil(CF * T / E))
            EC = E * C
            x = hidden_states.reshape(T, d)
            topk_idx, topk_w = _router(x, router_w, e_bias)
            expert_flat = topk_idx.reshape(-1)
            w_flat = topk_w.reshape(-1)
            tok_flat = jnp.repeat(jnp.arange(T, dtype=jnp.int32), K)
            sort_ix = jnp.argsort(expert_flat)
            e_sorted = expert_flat[sort_ix]
            tok_s = tok_flat[sort_ix]
            w_s = w_flat[sort_ix]
            counts = jnp.zeros(E, jnp.int32).at[e_sorted].add(1)
            group_start = jnp.concatenate([jnp.zeros(1, jnp.int32), jnp.cumsum(counts)[:-1].astype(jnp.int32)])
            pos = jnp.arange(T * K, dtype=jnp.int32) - group_start[e_sorted]
            valid = pos < C
            dest = e_sorted * C + jnp.where(valid, pos, 0)
            slots_token = jnp.zeros(EC, jnp.int32).at[dest].add(jnp.where(valid, tok_s, 0))
            slots_w = jnp.zeros(EC, w_s.dtype).at[dest].add(jnp.where(valid, w_s, 0.0))
            Xp = x[slots_token].reshape(E, C, d)
            G = jnp.einsum('ecd,edi->eci', Xp, W_gate)
            U = jnp.einsum('ecd,edi->eci', Xp, W_up)
            Y = jnp.einsum('eci,eid->ecd', jax.nn.silu(G) * U, W_down)
            Yf = Y.reshape(EC, d) * slots_w[:, None]
            out = jnp.zeros((T, d), x.dtype).at[slots_token].add(Yf)
            shared = jax.nn.silu(x @ shared_gate.T) * (x @ shared_up.T) @ shared_down.T
            return (out + shared).reshape(b, s, d)
        key = jax.random.key(seed)
        ks = jax.random.split(key, 8)

        def rn(k, shape, scale=0.02):
            return jax.random.normal(k, shape, jnp.float32) * scale
        return {'hidden_states': jax.random.normal(ks[0], (B, S, D), jnp.float32), 'router_w': rn(ks[1], (E, D)), 'e_bias': jnp.zeros((E,), jnp.float32), 'W_gate': rn(ks[2], (E, D, I)), 'W_up': rn(ks[3], (E, D, I)), 'W_down': rn(ks[4], (E, I, D)), 'shared_gate': rn(ks[5], (I * NSH, D)), 'shared_up': rn(ks[6], (I * NSH, D)), 'shared_down': rn(ks[7], (D, I * NSH))}
    _L0_ffn_in = _L0_ffn_setup()
    _d = {'L0_attn_hidden_states': _L0_attn_in['hidden_states'], 'L0_attn_Wq': _L0_attn_in['Wq'], 'L0_attn_Wk': _L0_attn_in['Wk'], 'L0_attn_Wv': _L0_attn_in['Wv'], 'L0_attn_Wo': _L0_attn_in['Wo'], 'L0_ffn_router_w': _L0_ffn_in['router_w'], 'L0_ffn_e_bias': _L0_ffn_in['e_bias'], 'L0_ffn_W_gate': _L0_ffn_in['W_gate'], 'L0_ffn_W_up': _L0_ffn_in['W_up'], 'L0_ffn_W_down': _L0_ffn_in['W_down'], 'L0_ffn_shared_gate': _L0_ffn_in['shared_gate'], 'L0_ffn_shared_up': _L0_ffn_in['shared_up'], 'L0_ffn_shared_down': _L0_ffn_in['shared_down']}
    _x0 = _d['L0_attn_hidden_states']
    _d['L0_attn_hidden_states'] = jax.random.normal(jax.random.fold_in(jax.random.key(seed), 1), (8, 512, 512), dtype=_x0.dtype)
    del _x0
    return _d

def reference(L0_attn_hidden_states, L0_attn_Wq, L0_attn_Wk, L0_attn_Wv, L0_attn_Wo, L0_ffn_router_w, L0_ffn_e_bias, L0_ffn_W_gate, L0_ffn_W_up, L0_ffn_W_down, L0_ffn_shared_gate, L0_ffn_shared_up, L0_ffn_shared_down):

    def _L0_attn_ref(hidden_states, Wq, Wk, Wv, Wo):
        import jax, jax.numpy as jnp
        import numpy as np
        HID, H, KV, D = (512, 16, 4, 128)
        ROPE_THETA = 10000.0
        GATE_NORM = 16.0

        def _rope_cos_sin(n, d, dtype=jnp.float32):
            inv_freq = 1.0 / ROPE_THETA ** (jnp.arange(0, d, 2, dtype=jnp.float32) / d)
            freqs = jnp.arange(n, dtype=jnp.float32)[:, None] * inv_freq[None, :]
            cos = jnp.cos(freqs).astype(dtype)[None, :, None, :]
            sin = jnp.sin(freqs).astype(dtype)[None, :, None, :]
            return (cos, sin)

        def _apply_rotary(x, cos, sin):
            x1, x2 = jnp.split(x, 2, axis=-1)
            return jnp.concatenate([x1 * cos - x2 * sin, x2 * cos + x1 * sin], axis=-1)

        def _forward(hidden_states, Wq, Wk, Wv, Wo):
            b, n, _ = hidden_states.shape
            groups = H // KV
            q = hidden_states @ Wq
            k = hidden_states @ Wk
            v = hidden_states @ Wv
            g = k
            q = q.reshape(b, n, H, D)
            k = k.reshape(b, n, KV, D)
            v = v.reshape(b, n, KV, D)
            g = g.reshape(b, n, KV, D)
            k = jnp.repeat(k, groups, axis=2)
            v = jnp.repeat(v, groups, axis=2)
            g = jnp.repeat(g, groups, axis=2)
            sq, sk, sv = (q, k, v)
            qs = jax.nn.softmax(q.astype(jnp.float32), axis=-1)
            ks = jax.nn.softmax(k.astype(jnp.float32), axis=-1)
            gl = jax.nn.log_sigmoid(g.astype(jnp.float32)) / GATE_NORM
            cos, sin = _rope_cos_sin(n, D)
            sq = _apply_rotary(sq, cos, sin)
            sk = _apply_rotary(sk, cos, sin)

            def step(S, inp):
                q_t, k_t, v_t, g_t = inp
                S = S * jnp.exp(g_t)[..., None] + k_t[..., None] * v_t[..., None, :]
                o_t = jnp.einsum('bhk,bhkv->bhv', q_t, S)
                return (S, o_t)
            xs = tuple((jnp.moveaxis(a, 1, 0) for a in (qs, ks, v, gl)))
            S0 = jnp.zeros((b, H, D, D), dtype=jnp.float32)
            _, o_gla = jax.lax.scan(step, S0, xs)
            o_gla = jnp.moveaxis(o_gla, 0, 1)
            scale = D ** (-0.5)
            scores = jnp.einsum('bqhd,bkhd->bhqk', sq, sk) * scale
            causal = jnp.tril(jnp.ones((n, n), dtype=bool))
            scores = jnp.where(causal[None, None], scores, jnp.finfo(scores.dtype).min)
            attn = jax.nn.softmax(scores, axis=-1)
            y = jnp.einsum('bhqk,bkhd->bqhd', attn, sv)
            o = 0.5 * y + 0.5 * o_gla
            o = o.reshape(b, n, H * D).astype(hidden_states.dtype)
            return o @ Wo
        return _forward(hidden_states, Wq, Wk, Wv, Wo)

    def _L0_ffn_ref(hidden_states, router_w, e_bias, W_gate, W_up, W_down, shared_gate, shared_up, shared_down):
        import math
        import jax, jax.numpy as jnp
        import numpy as np
        from jax import lax
        D = 512
        I = 256
        E = 32
        K = 4
        NG = 8
        TKG = 3
        NSH = 2
        SCALE = 2.5
        CF = 1.25
        B, S = (2, 512)

        def _router(x, router_w, e_bias):
            scores = jax.nn.sigmoid(x @ router_w.T)
            sc = scores + e_bias[None, :]
            T = x.shape[0]
            gs = sc.reshape(T, NG, E // NG)
            group_scores = lax.top_k(gs, 2)[0].sum(-1)
            _, gidx = lax.top_k(group_scores, TKG)
            gmask = jnp.zeros((T, NG), sc.dtype).at[jnp.arange(T)[:, None], gidx].set(1.0)
            smask = jnp.repeat(gmask, E // NG, axis=1)
            masked = jnp.where(smask > 0, sc, 0.0)
            _, topk_idx = lax.top_k(masked, K)
            topk_w = jnp.take_along_axis(scores, topk_idx, axis=1)
            topk_w = topk_w / (topk_w.sum(-1, keepdims=True) + 1e-20)
            topk_w = topk_w * SCALE
            return (topk_idx.astype(jnp.int32), topk_w)

        def _moe_forward(hidden_states, router_w, e_bias, W_gate, W_up, W_down, shared_gate, shared_up, shared_down):
            b, s, d = hidden_states.shape
            T = b * s
            C = int(math.ceil(CF * T / E))
            EC = E * C
            x = hidden_states.reshape(T, d)
            topk_idx, topk_w = _router(x, router_w, e_bias)
            expert_flat = topk_idx.reshape(-1)
            w_flat = topk_w.reshape(-1)
            tok_flat = jnp.repeat(jnp.arange(T, dtype=jnp.int32), K)
            sort_ix = jnp.argsort(expert_flat)
            e_sorted = expert_flat[sort_ix]
            tok_s = tok_flat[sort_ix]
            w_s = w_flat[sort_ix]
            counts = jnp.zeros(E, jnp.int32).at[e_sorted].add(1)
            group_start = jnp.concatenate([jnp.zeros(1, jnp.int32), jnp.cumsum(counts)[:-1].astype(jnp.int32)])
            pos = jnp.arange(T * K, dtype=jnp.int32) - group_start[e_sorted]
            valid = pos < C
            dest = e_sorted * C + jnp.where(valid, pos, 0)
            slots_token = jnp.zeros(EC, jnp.int32).at[dest].add(jnp.where(valid, tok_s, 0))
            slots_w = jnp.zeros(EC, w_s.dtype).at[dest].add(jnp.where(valid, w_s, 0.0))
            Xp = x[slots_token].reshape(E, C, d)
            G = jnp.einsum('ecd,edi->eci', Xp, W_gate)
            U = jnp.einsum('ecd,edi->eci', Xp, W_up)
            Y = jnp.einsum('eci,eid->ecd', jax.nn.silu(G) * U, W_down)
            Yf = Y.reshape(EC, d) * slots_w[:, None]
            out = jnp.zeros((T, d), x.dtype).at[slots_token].add(Yf)
            shared = jax.nn.silu(x @ shared_gate.T) * (x @ shared_up.T) @ shared_down.T
            return (out + shared).reshape(b, s, d)
        return _moe_forward(hidden_states, router_w, e_bias, W_gate, W_up, W_down, shared_gate, shared_up, shared_down)
    x = L0_attn_hidden_states
    x = x + _L0_attn_ref(_layernorm(x, axis=-1), L0_attn_Wq, L0_attn_Wk, L0_attn_Wv, L0_attn_Wo)
    x = x + _L0_ffn_ref(_layernorm(x, axis=-1), L0_ffn_router_w, L0_ffn_e_bias, L0_ffn_W_gate, L0_ffn_W_up, L0_ffn_W_down, L0_ffn_shared_gate, L0_ffn_shared_up, L0_ffn_shared_down)
    return x

_drawn_inputs = setup_inputs


def setup_inputs(seed=0):
    import zlib

    import numpy as np

    out = dict(_drawn_inputs(seed))
    spreads = {'L0_ffn_e_bias': (0.0, 0.324)}
    factors = {'L0_attn_Wq': 8.0,
     'L0_attn_Wk': 8.0,
     'L0_ffn_router_w': 2.976,
     'L0_ffn_W_gate': 2.787,
     'L0_ffn_W_up': 2.735,
     'L0_ffn_W_down': 2.732}
    for name, (base, spread) in spreads.items():
        noise = np.random.default_rng([zlib.crc32(name.encode()), seed]).standard_normal(out[name].shape)
        drawn = base * np.exp(spread * noise) if base else spread * noise
        out[name] = jnp.asarray(drawn.astype(out[name].dtype))
    for name, factor in factors.items():
        out[name] = (out[name] * factor).astype(out[name].dtype)
    return out
```

```python
from contextlib import ExitStack

import concourse.bass as bass
import numpy as np
from concourse import mybir

P = 128
F32 = mybir.dt.float32
BF16 = mybir.dt.bfloat16
I32 = mybir.dt.int32
U32 = mybir.dt.uint32
ALU = mybir.AluOpType
ACT = mybir.ActivationFunctionType
AX_X = mybir.AxisListType.X

DM = 512
DC = DM // P
HEADS = 16
KV = 4
G = HEADS // KV
DH = 128
HALF = DH // 2
SEQ = 512
NT = SEQ // P
SUB = 32
NSUB = P // SUB
EPS = 1e-5
GATE_NORM = 16.0
ROPE_THETA = 10000.0
HUGE = 3.0e38
NEG = -1.0e30


def attention_phase(nc, x, w_q, w_k, w_v, w_o, consts, x2):
    B = x.shape[0]
    QK = (G + 1) * DH
    with ExitStack() as ctx:
        def sb(name, shape, dt=F32):
            return ctx.enter_context(nc.sbuf_tensor(name, shape, dt))

        def sem(name):
            return ctx.enter_context(nc.semaphore(name))

        wq = sb("wq", [P, DC, HEADS * DH])
        wkv = sb("wkv", [P, DC, KV, 2 * DH])
        wo = sb("wo", [P, HEADS, DM])
        rope = sb("rope", [P, NT, 2, HALF])
        ident = sb("ident", [P, P])
        upto = sb("upto", [P, P])
        beyond = sb("beyond", [P, P])
        keep = sb("keep", [P, P])
        ident_b = sb("ident_b", [P, P], BF16)
        future_b = sb("future_b", [P, P], BF16)
        qr_t = [sb(f"qr_t{n}", [P, G, SEQ]) for n in range(2)]
        kr_t = [sb(f"kr_t{n}", [P, SEQ]) for n in range(2)]
        val = [sb(f"val{n}", [P, NT, DH]) for n in range(2)]
        q_in = [sb(f"q_in{n}", [P, G, SEQ - P]) for n in range(2)]
        local = [sb(f"local{n}", [P, NT, G, P]) for n in range(2)]
        state = [sb(f"state{n}", [P, NT - 1, DH]) for n in range(2)]
        o_t = sb("o_t", [P, G, SEQ])
        x_in = sb("x_in", [P, NT, DM])
        x_acc = sb("x_acc", [P, NT, DM])
        x_t = sb("x_t", [P, DC, SEQ])
        parts = sb("parts", [P, 2, QK])
        xn = parts[:, 0, 0:DM]
        qk = sb("qk", [P, QK])
        rot = sb("rot", [P, QK])
        soft = sb("soft", [P, QK])
        neg_top = sb("neg_top", [P, G + 1])
        tot = sb("tot", [P, G + 1])
        inv_tot = sb("inv_tot", [P, G + 1])
        logs = sb("logs", [P, DH])
        gate = sb("gate", [P, DH])
        decay = sb("decay", [P, (NSUB + 1) * P])
        keys = sb("keys", [P, 4 * P])
        span = sb("span", [P, 2 * P])
        k_dec = sb("k_dec", [P, NSUB, P])
        q_dec = sb("q_dec", [P, G, P])
        k_rest = sb("k_rest", [P, DH])
        prob = sb("prob", [P, 2, SEQ])
        prob_t = sb("prob_t", [P, NT, SEQ])
        neg_max = sb("neg_max", [P, G * NT])
        row_sum = sb("row_sum", [P, G * NT])
        inv_sum = sb("inv_sum", [P, G * NT])
        bn = sb("bn", [P, NT, 6])
        mv = sb("mv", [P, NT, 2])
        vpe = sb("vpe", [P, NT])
        rstd = sb("rstd", [P, NT])
        newton = sb("newton", [P, NT])

        qkv_ps = ctx.enter_context(nc.psum_tensor("qkv_ps", [P, 2 * 512], F32))
        tr_ps = [ctx.enter_context(nc.psum_tensor(f"tr_ps{n}", [P, 512], F32)) for n in range(2)]
        score_ps = [ctx.enter_context(nc.psum_tensor(f"score_ps{n}", [P, 512], F32)) for n in range(2)]
        prob_ps = ctx.enter_context(nc.psum_tensor("prob_ps", [P, 512], F32))
        out_ps = ctx.enter_context(nc.psum_tensor("out_ps", [P, 512], F32))

        loaded = sem("weights_loaded")
        masks_cast = sem("masks_cast")
        x_loaded = sem("x_loaded")
        x2_stored = sem("x2_stored")
        stats_step = sem("stats_step")
        root_step = sem("root_step")
        newton_step = sem("newton_step")
        xn_ready = sem("xn_ready")
        xn_turned = sem("xn_turned")
        x_t_ready = sem("x_t_ready")
        q_done = sem("q_done")
        kv_done = sem("kv_done")
        tops_ready = sem("tops_ready")
        parts_ready = sem("parts_ready")
        logs_step = sem("logs_step")
        gate_ready = sem("gate_ready")
        qk_ready = sem("qk_ready")
        val_ready = sem("val_ready")
        exps_ready = sem("exps_ready")
        inv_ready = sem("inv_ready")
        rot_ready = sem("rot_ready")
        soft_ready = sem("soft_ready")
        keys_turned = sem("keys_turned")
        kr_t_ready = sem("kr_t_ready")
        keys_copied = sem("keys_copied")
        span_ready = sem("span_ready")
        diffs_ready = sem("diffs_ready")
        decay_ready = sem("decay_ready")
        queries_turned = sem("queries_turned")
        qr_t_ready = sem("qr_t_ready")
        soft_turned = sem("soft_turned")
        k_dec_ready = sem("k_dec_ready")
        q_dec_ready = sem("q_dec_ready")
        q_in_ready = sem("q_in_ready")
        k_rest_ready = sem("k_rest_ready")
        update_done = sem("update_done")
        state_ready = sem("state_ready")
        local_done = sem("local_done")
        local_ready = sem("local_ready")
        scores_done = sem("scores_done")
        max_ready = sem("max_ready")
        exp_ready = [sem(f"exp_ready{n}") for n in range(2)]
        inv_sum_ready = sem("inv_sum_ready")
        prob_ready = sem("prob_ready")
        prob_turned = [sem(f"prob_turned{n}") for n in range(2)]
        past_copied = sem("past_copied")
        diag_ready = sem("diag_ready")
        attended = sem("attended")
        o_t_ready = sem("o_t_ready")
        projected = sem("projected")
        x2_added = [sem(f"x2_added{n}") for n in range(2)]

        ALL_LOADS = 16 * (2 * DC + 2 + 5)

        def each_sequence(eng, head, unit):
            head(0)
            unit(None, 0, 0, True)

            def sequence(b, last):
                for g in range(KV):
                    if g == KV - 1 and not last:
                        head(b + 1)
                    unit(KV * b + g, b, g, not (g == KV - 1 and last))
            if B > 1:
                with eng.Fori(0, B - 1) as b:
                    sequence(b, False)
            sequence(B - 1, True)

        def block_index(c, h, i):
            return G * NT * c + NT * h + i

        def use_index(c, h, i):
            return G * NT // 2 * c + NT // 2 * h + i // 2

        block = ctx.enter_context(nc.Block())

        @block.sync
        def _(sp):
            sp.dma_start(x_in[:], x[0].rearrange("(i p) d -> p i d", p=P)).then_inc(x_loaded, 16)
            sp.dma_start(rope[:], consts["rope"].rearrange("(i p) a d -> p i a d", p=P)).then_inc(loaded, 16)
            for to, name in ((ident, "ident"), (upto, "upto"), (beyond, "beyond"), (keep, "keep")):
                sp.dma_start(to[:], consts[name]).then_inc(loaded, 16)
            for n, w in enumerate((w_k, w_v)):
                for d in range(DC):
                    sp.dma_start(wkv[:, d, :, n * DH:(n + 1) * DH],
                                 w[d * P:(d + 1) * P, :].rearrange("p (g d) -> p g d", d=DH)).then_inc(loaded, 16)
            sp.dma_start(wq[:], w_q.rearrange("(c p) n -> p c n", p=P)).then_inc(loaded, 16)
            sp.dma_start(wo[:], w_o.rearrange("(h p) n -> p h n", p=P)).then_inc(loaded, 16)
            if B > 1:
                with sp.Fori(0, B - 1) as b:
                    for n in range(2):
                        sp.wait_ge(x2_added[n], KV * (NT // 2) * b + NT // 2)
                    sp.dma_start(x_in[:], x[b + 1].rearrange("(i p) d -> p i d", p=P)).then_inc(x_loaded, 16)
                    for n in range(2):
                        sp.wait_ge(x2_added[n], KV * (NT // 2) * (b + 1))
                    sp.dma_start(x2[b].rearrange("(i p) d -> p i d", p=P), x_acc[:]).then_inc(x2_stored, 16)
            for n in range(2):
                sp.wait_ge(x2_added[n], KV * (NT // 2) * B)
            sp.dma_start(x2[B - 1].rearrange("(i p) d -> p i d", p=P), x_acc[:]).then_inc(x2_stored, 16)
            sp.wait_ge(x2_stored, 16 * B)

        @block.gpsimd
        def _(pool):
            pool.wait_ge(loaded, ALL_LOADS)

            def normalise(c, h, i):
                n = block_index(c, h, i)
                j = NT * h + i
                pool.wait_ge(inv_sum_ready, n + 1)
                w = P * (i + 1)
                nc.gpsimd.tensor_tensor(prob[:, i % 2, 0:w], prob[:, i % 2, 0:w], inv_sum[:, j:j + 1].to_broadcast([P, w]),
                                        ALU.mult).then_inc(prob_ready, 1)

            def rotate(a):
                pool.wait_ge(parts_ready, a + 1)
                pool.wait_ge(keys_turned, a)
                pool.wait_ge(queries_turned, a)
                xc = parts[:, 0, :].rearrange("p (h s d) -> p h s d", s=2, d=HALF)
                xs = parts[:, 1, :].rearrange("p (h s d) -> p h s d", s=2, d=HALF)
                r = rot[:].rearrange("p (h s d) -> p h s d", s=2, d=HALF)
                nc.gpsimd.tensor_tensor(r[:, :, 0, :], xc[:, :, 0, :], xs[:, :, 1, :], ALU.subtract)
                nc.gpsimd.tensor_tensor(r[:, :, 1, :], xc[:, :, 1, :], xs[:, :, 0, :], ALU.add).then_inc(rot_ready, 1)

            def soften(a):
                pool.wait_ge(inv_ready, a + 1)
                s = soft[:].rearrange("p (h d) -> p h d", d=DH)
                nc.gpsimd.tensor_tensor(s, s, inv_tot[:].unsqueeze(2).to_broadcast([P, G + 1, DH]),
                                        ALU.mult).then_inc(soft_ready, 1)

            def differences(a):
                pool.wait_ge(keys_copied, a + 1)
                pool.wait_ge(q_dec_ready, a)
                run = keys[:, 2 * P:3 * P]
                runs = run.rearrange("p (c s) -> p c s", s=SUB)
                mid = runs[:, :, SUB // 2 - 1:SUB // 2]
                nc.gpsimd.tensor_tensor(decay[:, 0:NSUB * P].rearrange("p (c s) -> p c s", s=P),
                                        mid.to_broadcast([P, NSUB, P]),
                                        run.unsqueeze(1).to_broadcast([P, NSUB, P]), ALU.subtract)
                nc.gpsimd.tensor_tensor(decay[:, NSUB * P:(NSUB + 1) * P].rearrange("p (c s) -> p c s", s=SUB),
                                        runs, mid.to_broadcast([P, NSUB, SUB]), ALU.subtract).then_inc(diffs_ready, 1)

            def scaled_keys(a, p, i):
                nc.gpsimd.tensor_scalar(kr_t[p][:, i * P:(i + 1) * P], keys[:, 0:P], float(DH) ** -0.5, None,
                                        ALU.mult).then_inc(kr_t_ready, 1)

            def key_rest(ua, i):
                a, n = NT * ua + i, (NT - 1) * ua + i
                pool.wait_ge(span_ready, a + 1)
                pool.wait_ge(update_done, n)
                pool.wait_ge(soft_ready, a + 1)
                nc.gpsimd.tensor_tensor(k_rest[:], span[:, P:2 * P], soft[:, G * DH:QK], ALU.mult).then_inc(k_rest_ready, 1)

            def unit(c, b, g, prepare):
                ua, p = (0, 0) if c is None else (c + 1, (g + 1) % 2)
                if prepare and c is not None:
                    pool.wait_ge(attended, G * c)
                for s in range(NT):
                    if c is not None:
                        normalise(c, s, 0)
                        normalise(c, s, 1)
                    if prepare and s:
                        differences(NT * ua + s - 1)
                        scaled_keys(NT * ua + s - 1, p, s - 1)
                        key_rest(ua, s - 1)
                    if prepare:
                        rotate(NT * ua + s)
                    if c is not None:
                        normalise(c, s, 2)
                    if prepare:
                        soften(NT * ua + s)
                    if c is not None:
                        normalise(c, s, 3)
                if prepare:
                    differences(NT * ua + NT - 1)
                    scaled_keys(NT * ua + NT - 1, p, NT - 1)
            each_sequence(pool, lambda b: None, unit)

        @block.scalar
        def _(act):
            act.preload_act_table_set("natural_log_exp_and_others")
            act.wait_ge(loaded, ALL_LOADS)

            def head(b):
                act.wait_ge(stats_step, (2 * NT + 1) * (b + 1))
                nc.scalar.activation(rstd[:], vpe[:], ACT.Ln).then_inc(root_step, 1)
                act.wait_ge(root_step, 2 * b + 1)
                nc.scalar.activation(rstd[:], rstd[:], ACT.Exp, scale=-0.5).then_inc(root_step, 1)
                act.wait_ge(kv_done, KV * NT * b)
                for i in range(NT):
                    act.wait_ge(xn_turned, NT * b + i + 1)
                    nc.scalar.copy(x_t[:, :, i * P:(i + 1) * P],
                                   tr_ps[i % 2][:].rearrange("p (c t) -> p c t", c=DC)).then_inc(x_t_ready, 1)

            def exponent(c, h, i):
                n, k, j, w = block_index(c, h, i), use_index(c, h, i), NT * h + i, P * (i + 1)
                act.wait_ge(max_ready, n + 1)
                act.wait_ge(prob_turned[i % 2], k)
                nc.scalar.activation(prob[:, i % 2, 0:w], score_ps[i % 2][:, 0:w], ACT.Exp, bias=neg_max[:, j:j + 1],
                                     accum_out=row_sum[:, j:j + 1]).then_inc(exp_ready[i % 2], 1)

            def past(c, h, i):
                act.wait_ge(diag_ready, block_index(c, h, i) + 1)
                act.wait_ge(attended, G * c + h)
                nc.scalar.copy(prob_t[:, 0:i, i * P:(i + 1) * P],
                               prob_ps[:, 0:i * P].rearrange("p (j t) -> p j t", t=P)).then_inc(past_copied, 1)

            def out_copy(c, h):
                act.wait_ge(attended, G * c + h + 1)
                act.wait_ge(projected, NT * c)
                nc.scalar.copy(o_t[:, h, :], out_ps[:]).then_inc(o_t_ready, 1)

            def gates(a, p, i):
                act.wait_ge(q_done, a + 1)
                act.wait_ge(kv_done, a + 1)
                act.wait_ge(parts_ready, a)
                act.wait_ge(gate_ready, a)
                nc.scalar.copy(qk[:], qkv_ps[:, 0:QK]).then_inc(qk_ready, 1)
                nc.scalar.copy(val[p][:, i, :], qkv_ps[:, QK:QK + DH]).then_inc(val_ready, 1)
                act.wait_ge(qk_ready, a + 1)
                nc.scalar.activation(logs[:], qk[:, G * DH:QK], ACT.Abs).then_inc(logs_step, 1)
                act.wait_ge(logs_step, 3 * a + 1)
                nc.scalar.activation(logs[:], logs[:], ACT.Exp, scale=-1.0).then_inc(logs_step, 1)
                act.wait_ge(logs_step, 3 * a + 2)
                nc.scalar.activation(logs[:], logs[:], ACT.Ln, bias=1.0).then_inc(logs_step, 1)

            def feature_exps(a, ua, i):
                act.wait_ge(tops_ready, a + 1)
                act.wait_ge(soft_turned, a)
                act.wait_ge(k_rest_ready, (NT - 1) * ua + min(i, NT - 1))
                for h in range(G + 1):
                    ins = nc.scalar.activation(soft[:, h * DH:(h + 1) * DH], qk[:, h * DH:(h + 1) * DH], ACT.Exp,
                                               bias=neg_top[:, h:h + 1], accum_out=tot[:, h:h + 1])
                ins.then_inc(exps_ready, 1)

            def turned(a, ua, p, i):
                act.wait_ge(keys_copied, a + 1)
                act.wait_ge(k_rest_ready, (NT - 1) * ua + i)
                act.wait_ge(q_in_ready, (NT - 1) * ua + max(i - 1, 0))
                act.wait_ge(state_ready, (NT - 1) * ua + i)
                nc.scalar.activation(span[:], keys[:, 2 * P:4 * P], ACT.Exp).then_inc(span_ready, 1)
                act.wait_ge(queries_turned, a + 1)
                nc.scalar.copy(qr_t[p][:, :, i * P:(i + 1) * P],
                               tr_ps[1][:].rearrange("p (h t) -> p h t", t=P)).then_inc(qr_t_ready, 1)
                act.wait_ge(diffs_ready, a + 1)
                nc.scalar.activation(decay[:], decay[:], ACT.Exp).then_inc(decay_ready, 1)

            def unit(c, b, g, prepare):
                ua, p = (0, 0) if c is None else (c + 1, (g + 1) % 2)
                if prepare and c is not None:
                    act.wait_ge(attended, G * c)
                for s in range(NT):
                    if c is not None:
                        exponent(c, s, 0)
                        exponent(c, s, 1)
                        exponent(c, s, 2)
                    if prepare and s:
                        turned(NT * ua + s - 1, ua, p, s - 1)
                    if prepare:
                        gates(NT * ua + s, p, s)
                    if c is not None:
                        past(c, s, 1)
                        exponent(c, s, 3)
                    if prepare:
                        feature_exps(NT * ua + s, ua, s)
                    if c is not None:
                        past(c, s, 2)
                        past(c, s, 3)
                        out_copy(c, s)
                if prepare:
                    turned(NT * ua + NT - 1, ua, p, NT - 1)
            each_sequence(act, head, unit)

        @block.vector
        def _(dve):
            dve.wait_ge(loaded, ALL_LOADS)
            nc.vector.tensor_copy(ident_b[:], ident[:]).then_inc(masks_cast, 1)
            nc.vector.tensor_scalar(future_b[:], beyond[:], NEG * GATE_NORM, None, ALU.mult).then_inc(masks_cast, 1)

            def head(b):
                base = (2 * NT + 1) * b
                dve.wait_ge(x_loaded, 16 * (b + 1))
                for i in range(NT):
                    nc.vector.bn_stats(bn[:, i, :], x_in[:, i, :]).then_inc(stats_step, 1)
                dve.wait_ge(stats_step, base + NT)
                nc.vector.memset(newton[:], 0.0)
                for i in range(NT):
                    nc.vector.bn_aggr(mv[:, i, :], bn[:, i, :]).then_inc(stats_step, 1)
                dve.wait_ge(stats_step, base + 2 * NT)
                nc.vector.tensor_scalar(vpe[:], mv[:, :, 1], EPS, None, ALU.add).then_inc(stats_step, 1)
                dve.wait_ge(root_step, 2 * b + 2)
                dve.wait_ge(stats_step, base + 2 * NT + 1)
                for r in range(2):
                    n = 8 * b + 4 * r
                    if r:
                        dve.wait_ge(newton_step, n)
                    nc.vector.tensor_tensor(newton[:], rstd[:], rstd[:], ALU.mult).then_inc(newton_step, 1)
                    dve.wait_ge(newton_step, n + 1)
                    nc.vector.tensor_tensor(newton[:], newton[:], vpe[:], ALU.mult).then_inc(newton_step, 1)
                    dve.wait_ge(newton_step, n + 2)
                    nc.vector.tensor_scalar(newton[:], newton[:], -0.5, 1.5, ALU.mult, ALU.add).then_inc(newton_step, 1)
                    dve.wait_ge(newton_step, n + 3)
                    nc.vector.tensor_tensor(rstd[:], rstd[:], newton[:], ALU.mult).then_inc(newton_step, 1)
                dve.wait_ge(newton_step, 8 * b + 8)
                dve.wait_ge(rot_ready, KV * NT * b)
                for i in range(NT):
                    dve.wait_ge(xn_turned, NT * b + i)
                    nc.vector.tensor_scalar(xn, x_in[:, i, :], mv[:, i, 0:1], rstd[:, i:i + 1],
                                            ALU.subtract, ALU.mult).then_inc(xn_ready, 1)

            def row_max(c, h, i):
                n, j, w = block_index(c, h, i), NT * h + i, P * (i + 1)
                dve.wait_ge(scores_done, n + 1)
                nc.vector.tensor_reduce(neg_max[:, j:j + 1], score_ps[i % 2][:, 0:w], AX_X, ALU.max,
                                        negate=True).then_inc(max_ready, 1)

            def inverse(c, h, i):
                j = NT * h + i
                dve.wait_ge(exp_ready[i % 2], use_index(c, h, i) + 1)
                nc.vector.reciprocal(inv_sum[:, j:j + 1], row_sum[:, j:j + 1]).then_inc(inv_sum_ready, 1)

            def diagonal(c, h, i, p):
                dve.wait_ge(prob_turned[i % 2], use_index(c, h, i) + 1)
                dve.wait_ge(attended, G * c + h)
                dve.wait_ge(local_ready, NT * c + i + 1)
                nc.vector.tensor_tensor(prob_t[:, i, i * P:(i + 1) * P], prob_ps[:, i * P:(i + 1) * P],
                                        local[p][:, i, h, :], ALU.add).then_inc(diag_ready, 1)

            def features(a, i):
                dve.wait_ge(qk_ready, a + 1)
                dve.wait_ge(exps_ready, a)
                dve.wait_ge(rot_ready, a)
                nc.vector.tensor_reduce(neg_top[:], qk[:].rearrange("p (h d) -> p h d", d=DH), AX_X, ALU.max, negate=True).then_inc(tops_ready, 1)
                halves = qk[:].rearrange("p (h d) -> p h d", d=HALF)
                for r in range(2):
                    ins = nc.vector.tensor_tensor(parts[:, r, :].rearrange("p (h d) -> p h d", d=HALF), halves,
                                                  rope[:, i, r:r + 1, :].to_broadcast([P, 2 * (G + 1), HALF]), ALU.mult)
                ins.then_inc(parts_ready, 1)
                dve.wait_ge(logs_step, 3 * a + 3)
                dve.wait_ge(keys_turned, a)
                nc.vector.scalar_tensor_tensor(out=gate[:], in0=qk[:, G * DH:QK], scalar=0.0, in1=logs[:],
                                               op0=ALU.min, op1=ALU.subtract).then_inc(gate_ready, 1)

            def feature_inverse(a):
                dve.wait_ge(exps_ready, a + 1)
                nc.vector.reciprocal(inv_tot[:], tot[:]).then_inc(inv_ready, 1)

            def decays(a):
                dve.wait_ge(keys_turned, a + 1)
                dve.wait_ge(kr_t_ready, a)
                dve.wait_ge(span_ready, a)
                nc.vector.tensor_copy(keys[:], tr_ps[0][:]).then_inc(keys_copied, 1)

            def apply_decays(a, ua, i, p):
                dve.wait_ge(decay_ready, a + 1)
                dve.wait_ge(keys_copied, a + 1)
                dve.wait_ge(local_done, a)
                nc.vector.tensor_tensor(k_dec[:], decay[:, 0:NSUB * P].rearrange("p (c s) -> p c s", s=P),
                                        keys[:, P:2 * P].unsqueeze(1).to_broadcast([P, NSUB, P]), ALU.mult).then_inc(k_dec_ready, 1)
                dve.wait_ge(soft_turned, a + 1)
                qs = tr_ps[0][:].rearrange("p (h t) -> p h t", t=P)
                nc.vector.tensor_tensor(q_dec[:], qs, decay[:, NSUB * P:(NSUB + 1) * P].unsqueeze(1)
                                        .to_broadcast([P, G, P]), ALU.mult).then_inc(q_dec_ready, 1)
                dve.wait_ge(span_ready, a + 1)
                if i:
                    nc.vector.tensor_tensor(q_in[p][:, :, (i - 1) * P:i * P], qs, span[:, 0:P].unsqueeze(1)
                                            .to_broadcast([P, G, P]), ALU.mult).then_inc(q_in_ready, 1)
                if i < NT - 1:
                    n = (NT - 1) * ua + i
                    dve.wait_ge(update_done, n + 1)
                    if i:
                        dve.wait_ge(state_ready, n)
                        nc.vector.scalar_tensor_tensor(out=state[p][:, i, :], in0=state[p][:, i - 1, :],
                                                       scalar=span[:, P - 1:P],
                                                       in1=tr_ps[1][:, 0:DH], op0=ALU.mult, op1=ALU.add).then_inc(state_ready, 1)
                    else:
                        nc.vector.tensor_copy(state[p][:, 0, :], tr_ps[1][:, 0:DH]).then_inc(state_ready, 1)
                dve.wait_ge(local_done, a + 1)
                nc.vector.scalar_tensor_tensor(out=local[p][:, i, :, :], in0=tr_ps[0][:].rearrange("p (h t) -> p h t", t=P),
                                               scalar=HUGE, in1=keep[:].unsqueeze(1).to_broadcast([P, G, P]),
                                               op0=ALU.min, op1=ALU.mult).then_inc(local_ready, 1)

            def residual(c, b, g):
                for i in range(NT):
                    dve.wait_ge(projected, NT * c + i + 1)
                    if g:
                        dve.wait_ge(x2_added[i % 2], NT // 2 * c)
                        base = x_acc
                    else:
                        dve.wait_ge(x2_stored, 16 * b)
                        base = x_in
                    nc.vector.scalar_tensor_tensor(out=x_acc[:, i, :], in0=score_ps[i % 2][:], scalar=0.5,
                                                   in1=base[:, i, :], op0=ALU.mult, op1=ALU.add).then_inc(x2_added[i % 2], 1)

            def unit(c, b, g, prepare):
                ua, p = (0, 0) if c is None else (c + 1, (g + 1) % 2)
                if prepare and c is not None:
                    dve.wait_ge(attended, G * c)
                for s in range(NT):
                    if c is not None:
                        row_max(c, s, 0)
                        row_max(c, s, 1)
                        inverse(c, s, 0)
                        inverse(c, s, 1)
                        diagonal(c, s, 0, g % 2)
                        row_max(c, s, 2)
                    if prepare and s:
                        decays(NT * ua + s - 1)
                    if prepare:
                        features(NT * ua + s, s)
                    if c is not None:
                        inverse(c, s, 2)
                        diagonal(c, s, 1, g % 2)
                        row_max(c, s, 3)
                    if prepare and s:
                        apply_decays(NT * ua + s - 1, ua, s - 1, p)
                    if prepare:
                        feature_inverse(NT * ua + s)
                    if c is not None:
                        inverse(c, s, 3)
                        diagonal(c, s, 2, g % 2)
                        diagonal(c, s, 3, g % 2)
                if prepare:
                    decays(NT * ua + NT - 1)
                    apply_decays(NT * ua + NT - 1, ua, NT - 1, p)
                if c is not None:
                    residual(c, b, g)
            each_sequence(dve, head, unit)

        @block.tensor
        def _(pe):
            pe.wait_ge(loaded, ALL_LOADS)
            pe.wait_ge(masks_cast, 2)

            def head(b):
                pe.wait_ge(local_ready, KV * NT * b)
                pe.wait_ge(qr_t_ready, KV * NT * b)
                for i in range(NT):
                    pe.wait_ge(xn_ready, NT * b + i + 1)
                    if i >= 2:
                        pe.wait_ge(x_t_ready, NT * b + i - 1)
                    for d in range(DC):
                        ins = nc.tensor.transpose(tr_ps[i % 2][:, d * P:(d + 1) * P], parts[:, 0, d * P:(d + 1) * P], ident[:])
                    ins.then_inc(xn_turned, 1)

            def scores(c, h, i, p):
                k, w = use_index(c, h, i), P * (i + 1)
                pe.wait_ge(exp_ready[i % 2], k)
                pe.wait_ge(x2_added[i % 2], NT // 2 * c)
                nc.tensor.matmul(score_ps[i % 2][:, 0:w], qr_t[p][:, h, i * P:(i + 1) * P], kr_t[p][:, 0:w],
                                 start=True, stop=False)
                nc.tensor.matmul(score_ps[i % 2][:, i * P:w], future_b[:], ident_b[:], start=False,
                                 stop=True).then_inc(scores_done, 1)

            def turn_probs(c, h, i):
                n = block_index(c, h, i)
                pe.wait_ge(prob_ready, n + 1)
                pe.wait_ge(diag_ready, n)
                pe.wait_ge(past_copied, (NT - 1) * (G * c + h) + max(i - 1, 0))
                for j in range(i + 1):
                    ins = nc.tensor.transpose(prob_ps[:, j * P:(j + 1) * P], prob[:, i % 2, j * P:(j + 1) * P], ident[:])
                ins.then_inc(prob_turned[i % 2], 1)

            def attend(c, h, p):
                pe.wait_ge(past_copied, (NT - 1) * (G * c + h + 1))
                pe.wait_ge(diag_ready, NT * (G * c + h + 1))
                pe.wait_ge(o_t_ready, G * c + h)
                pe.wait_ge(val_ready, NT * (c + 1))
                pe.wait_ge(q_in_ready, (NT - 1) * (c + 1))
                pe.wait_ge(state_ready, (NT - 1) * (c + 1))
                for j in range(NT):
                    nc.tensor.matmul(out_ps[:, j * P:SEQ], val[p][:, j, :], prob_t[:, j, j * P:SEQ],
                                     start=(j == 0), stop=False, skip_group_check=True)
                for i in range(1, NT):
                    ins = nc.tensor.matmul(out_ps[:, i * P:(i + 1) * P], state[p][:, i - 1, :],
                                           q_in[p][:, h, (i - 1) * P:i * P], start=False, stop=(i == NT - 1),
                                           skip_group_check=True)
                ins.then_inc(attended, 1)

            def project(c, b, g):
                for i in range(NT):
                    pe.wait_ge(o_t_ready, G * (c + 1))
                    pe.wait_ge(exp_ready[i % 2], G * NT // 2 * (c + 1))
                    pe.wait_ge(x2_added[i % 2], NT // 2 * c + i // 2)
                    for h in range(G):
                        ins = nc.tensor.matmul(score_ps[i % 2][:], o_t[:, h, i * P:(i + 1) * P], wo[:, G * g + h, :],
                                               start=(h == 0), stop=(h == G - 1))
                    ins.then_inc(projected, 1)

            def products(a, ub, i, gn):
                pe.wait_ge(x_t_ready, NT * (ub + 1))
                pe.wait_ge(val_ready, a)
                for d in range(DC):
                    ins = nc.tensor.matmul(qkv_ps[:, 0:G * DH], x_t[:, d, i * P:(i + 1) * P],
                                           wq[:, d, gn * G * DH:(gn + 1) * G * DH], start=(d == 0), stop=(d == DC - 1))
                ins.then_inc(q_done, 1)
                for d in range(DC):
                    ins = nc.tensor.matmul(qkv_ps[:, G * DH:G * DH + 2 * DH], x_t[:, d, i * P:(i + 1) * P],
                                           wkv[:, d, gn, :], start=(d == 0), stop=(d == DC - 1))
                ins.then_inc(kv_done, 1)

            def turn_features(a):
                pe.wait_ge(rot_ready, a + 1)
                pe.wait_ge(soft_ready, a + 1)
                pe.wait_ge(gate_ready, a + 1)
                pe.wait_ge(local_ready, a)
                nc.tensor.transpose(tr_ps[0][:, 0:P], rot[:, G * DH:QK], ident[:])
                nc.tensor.transpose(tr_ps[0][:, P:2 * P], soft[:, G * DH:QK], ident[:])
                nc.tensor.matmul(tr_ps[0][:, 2 * P:3 * P], gate[:], upto[:], start=True, stop=True)
                nc.tensor.matmul(tr_ps[0][:, 3 * P:4 * P], beyond[:], gate[:], start=True, stop=True).then_inc(keys_turned, 1)

            def turn_queries(a, ua, i):
                pe.wait_ge(state_ready, (NT - 1) * ua + min(i, NT - 1))
                pe.wait_ge(qr_t_ready, a)
                for h in range(G):
                    ins = nc.tensor.transpose(tr_ps[1][:, h * P:(h + 1) * P], rot[:, h * P:(h + 1) * P], ident[:])
                ins.then_inc(queries_turned, 1)

            def linear(a, ua, i, p):
                pe.wait_ge(keys_copied, a + 1)
                for h in range(G):
                    ins = nc.tensor.transpose(tr_ps[0][:, h * P:(h + 1) * P], soft[:, h * P:(h + 1) * P], ident[:])
                ins.then_inc(soft_turned, 1)
                if i < NT - 1:
                    pe.wait_ge(qr_t_ready, a + 1)
                    pe.wait_ge(k_rest_ready, (NT - 1) * ua + i + 1)
                    pe.wait_ge(val_ready, a + 1)
                    nc.tensor.matmul(tr_ps[1][:, 0:DH], k_rest[:], val[p][:, i, :], start=True, stop=True).then_inc(update_done, 1)
                pe.wait_ge(k_dec_ready, a + 1)
                pe.wait_ge(q_dec_ready, a + 1)
                pe.wait_ge(q_in_ready, (NT - 1) * ua + i)
                for s in range(NSUB):
                    m = SUB * (s + 1)
                    ins = nc.tensor.matmul(tr_ps[0][0:m, :].rearrange("p (h t) -> p h t", t=P)[:, :, m - SUB:m],
                                           k_dec[:, s, 0:m], q_dec[:, :, m - SUB:m], start=True, stop=True)
                ins.then_inc(local_done, 1)

            def unit(c, b, g, prepare):
                ua, p = (0, 0) if c is None else (c + 1, (g + 1) % 2)
                gn = 0 if c is None else (g + 1) % KV
                ub = 0 if c is None else b + (g + 1) // KV
                if c is not None:
                    pe.wait_ge(kr_t_ready, NT * (c + 1))
                    pe.wait_ge(qr_t_ready, NT * (c + 1))
                for s in range(NT):
                    if c is not None:
                        scores(c, s, 0, g % 2)
                        scores(c, s, 1, g % 2)
                    if prepare:
                        products(NT * ua + s, ub, s, gn)
                    if c is not None:
                        turn_probs(c, s, 0)
                        scores(c, s, 2, g % 2)
                    if prepare and s:
                        turn_features(NT * ua + s - 1)
                        turn_queries(NT * ua + s - 1, ua, s - 1)
                    if c is not None:
                        turn_probs(c, s, 1)
                        scores(c, s, 3, g % 2)
                    if prepare and s:
                        linear(NT * ua + s - 1, ua, s - 1, p)
                    if c is not None:
                        turn_probs(c, s, 2)
                        turn_probs(c, s, 3)
                        attend(c, s, g % 2)
                if prepare:
                    turn_features(NT * ua + NT - 1)
                    turn_queries(NT * ua + NT - 1, ua, NT - 1)
                    linear(NT * ua + NT - 1, ua, NT - 1, p)
                if c is not None:
                    project(c, b, g)
            each_sequence(pe, head, unit)


E_ = 32
GROUPS = 8
TOP_GROUPS = 3
K = 4
FF = 256
FC = FF // P
SH = 512
SC = SH // P
ROUTE_SCALE = 2.5
FAR = 1.0e6
PICKED = -1.0e30


def capacity(tokens):
    return -(-5 * tokens // (4 * E_))


def slot_tiles(cap):
    n = -(-cap // P)
    assert cap % n == 0
    return n, cap // n


def routing_phase(nc, x2, router_w, e_bias, consts, y, slots_dram, weights_dram, tokens_dram):
    B = x2.shape[0]
    T = B * SEQ
    cap = capacity(T)
    ROUTE_STEPS = 58
    GE = E_ // GROUPS
    with ExitStack() as ctx:
        def sb(name, shape, dt=F32):
            return ctx.enter_context(nc.sbuf_tensor("r_" + name, shape, dt))

        def sem(name):
            return ctx.enter_context(nc.semaphore("r_" + name))

        ident = sb("ident", [P, P])
        before = sb("before", [P, P])
        before_b = sb("before_b", [P, P], BF16)
        ones_b = sb("ones_b", [P, P], BF16)
        rw = sb("rw", [E_, DM])
        rw_t = sb("rw_t", [P, DC, E_])
        bias = sb("bias", [P, E_])
        first = sb("first", [P, E_])
        order = sb("order", [P, E_])
        lower = sb("lower", [P, GROUPS, GROUPS])
        token = sb("token", [P, T // P, K])
        no_token = sb("no_token", [E_, cap])
        xb = sb("xb", [P, NT, DM])
        yn = sb("yn", [P, NT, DM])
        y_t = sb("y_t", [P, DC, SEQ])
        bn = sb("bn", [P, NT, 6])
        mv = sb("mv", [P, NT, 2])
        vpe = sb("vpe", [P, NT])
        rstd = sb("rstd", [P, NT])
        newton = sb("newton", [P, NT])
        ex = sb("ex", [P, NT, E_])
        score = sb("score", [P, NT, E_])
        biased = sb("biased", [P, NT, E_])
        hi = sb("hi", [P, NT * GROUPS, 2])
        lo = sb("lo", [P, NT * GROUPS, 2])
        gs = sb("gs", [P, NT, GROUPS])
        g2 = sb("g2", [P, NT * GROUPS])
        g3 = sb("g3", [P, NT * GROUPS])
        beats = sb("beats", [P, NT * GROUPS, GROUPS])
        ties = sb("ties", [P, NT * GROUPS, GROUPS])
        rank = sb("rank", [P, NT * GROUPS])
        v = sb("v", [P, NT, E_])
        cand = sb("cand", [P, NT, E_])
        top = sb("top", [P, NT])
        hot = sb("hot", [P, NT, K, E_])
        picked = sb("picked", [P, NT, E_], BF16)
        seen = sb("seen", [P, E_])
        seen_b = sb("seen_b", [P, NT, E_], BF16)
        over = sb("over", [P, NT, E_])
        slot = sb("slot", [P, NT, E_])
        prod = sb("prod", [P, NT, K, E_])
        wk = sb("wk", [P, NT, K])
        sk = sb("sk", [P, NT, K])
        ok = sb("ok", [P, NT, K])
        token_now = sb("token_now", [P, NT, K])
        sk_i = sb("sk_i", [P, NT, K], I32)
        wsum = sb("wsum", [P, NT])
        tr_ps = [ctx.enter_context(nc.psum_tensor(f"r_tr_ps{n}", [P, 512], F32)) for n in range(2)]
        lg_ps = ctx.enter_context(nc.psum_tensor("r_lg_ps", [P, NT, E_], F32))
        pos_ps = ctx.enter_context(nc.psum_tensor("r_pos_ps", [P, NT, E_], F32))

        loaded = sem("loaded")
        table_cleared = sem("table_cleared")
        cast = sem("cast")
        rw_turned = sem("rw_turned")
        rw_ready = sem("rw_ready")
        x_loaded = sem("x_loaded")
        y_stored = sem("y_stored")
        stats_step = sem("stats_step")
        root_step = sem("root_step")
        newton_step = sem("newton_step")
        yn_ready = sem("yn_ready")
        yn_turned = sem("yn_turned")
        y_t_ready = sem("y_t_ready")
        logits_done = sem("logits_done")
        ex_ready = sem("ex_ready")
        route_step = sem("route_step")
        picks_ready = sem("picks_ready")
        places_done = sem("places_done")
        slots_ready = sem("slots_ready")
        token_copied = sem("token_copied")
        slots_stored = sem("slots_stored")
        scattered = sem("scattered")
        ALL_LOADS = 16 * 9

        block = ctx.enter_context(nc.Block())

        @block.sync
        def _(sp):
            sp.dma_start(no_token[:], consts["no_token"]).then_inc(loaded, 16)
            for to, name in ((ident, "ident"), (before, "before")):
                sp.dma_start(to[:], consts[name]).then_inc(loaded, 16)
            sp.dma_start(rw[:], router_w).then_inc(loaded, 16)
            sp.dma_start(bias[:], e_bias.partition_broadcast(P)).then_inc(loaded, 16)
            sp.dma_start(first[:], consts["first"].partition_broadcast(P)).then_inc(loaded, 16)
            sp.dma_start(order[:], consts["order"].partition_broadcast(P)).then_inc(loaded, 16)
            sp.dma_start(lower[:], consts["lower"].partition_broadcast(P)).then_inc(loaded, 16)
            sp.dma_start(token[:], consts["token"]).then_inc(loaded, 16)
            sp.wait_ge(loaded, ALL_LOADS)
            sp.dma_start(tokens_dram.rearrange("(e c) o -> e (c o)", e=E_), no_token[:]).then_inc(table_cleared, 16)
            with sp.Fori(0, B) as b:
                sp.wait_ge(yn_ready, NT * b)
                sp.dma_start(xb[:], x2[b].rearrange("(i p) d -> p i d", p=P)).then_inc(x_loaded, 16)
                sp.wait_ge(yn_ready, NT * (b + 1))
                sp.dma_start(y[b].rearrange("(i p) d -> p i d", p=P), yn[:]).then_inc(y_stored, 16)
            sp.wait_ge(y_stored, 16 * B)

        @block.gpsimd
        def _(pool):
            pool.wait_ge(loaded, ALL_LOADS)
            pool.wait_ge(table_cleared, 16)
            with pool.Fori(0, B) as b:
                pool.wait_ge(loaded, ALL_LOADS)
                pool.wait_ge(scattered, 16 * NT * K * b)
                nc.gpsimd.tensor_copy(token_now[:], token[:, bass.ts(b, NT), :]).then_inc(token_copied, 1)
                pool.wait_ge(token_copied, b + 1)
                pool.wait_ge(slots_ready, b + 1)
                pool.dma_start(slots_dram[b], sk_i[:].rearrange("p i k -> p (i k)")).then_inc(slots_stored, 16)
                pool.dma_start(weights_dram[b], wk[:].rearrange("p i k -> p (i k)")).then_inc(slots_stored, 16)
                for i in range(NT):
                    for k in range(K):
                        pool.indirect_dma_start(tokens_dram, bass.IndirectOffsetOnAxis(ap=sk_i[:, i, k:k + 1], axis=0),
                                                token_now[:, i, k:k + 1], None, bounds_check=E_ * cap - 1,
                                                oob_is_err=False).then_inc(scattered, 16)
            pool.wait_ge(slots_stored, 32 * B)
            pool.wait_ge(scattered, 16 * NT * K * B)

        @block.scalar
        def _(act):
            act.preload_act_table_set("natural_log_exp_and_others")
            act.wait_ge(rw_turned, 1)
            nc.scalar.copy(rw_t[:], tr_ps[0][:, 0:DC * E_].rearrange("p (c e) -> p c e", e=E_)).then_inc(rw_ready, 1)
            with act.Fori(0, B) as b:
                act.wait_ge(stats_step, (2 * NT + 1) * (b + 1))
                nc.scalar.activation(rstd[:], vpe[:], ACT.Ln).then_inc(root_step, 1)
                act.wait_ge(root_step, 2 * b + 1)
                nc.scalar.activation(rstd[:], rstd[:], ACT.Exp, scale=-0.5).then_inc(root_step, 1)
                for i in range(NT):
                    act.wait_ge(yn_turned, NT * b + i + 1)
                    act.wait_ge(logits_done, b)
                    nc.scalar.copy(y_t[:, :, i * P:(i + 1) * P],
                                   tr_ps[i % 2][:].rearrange("p (c t) -> p c t", c=DC)).then_inc(y_t_ready, 1)
                act.wait_ge(logits_done, b + 1)
                nc.scalar.activation(ex[:], lg_ps[:], ACT.Exp, scale=-1.0).then_inc(ex_ready, 1)

        @block.tensor
        def _(pe):
            pe.wait_ge(loaded, ALL_LOADS)
            pe.wait_ge(cast, 3)
            for d in range(DC):
                ins = nc.tensor.transpose(tr_ps[0][:, d * E_:(d + 1) * E_], rw[:, d * P:(d + 1) * P], ident[0:E_, 0:E_])
            ins.then_inc(rw_turned, 1)
            pe.wait_ge(rw_ready, 1)
            with pe.Fori(0, B) as b:
                for i in range(NT):
                    pe.wait_ge(yn_ready, NT * b + i + 1)
                    pe.wait_ge(y_t_ready, NT * b + (i - 1 if i >= 2 else 0))
                    for d in range(DC):
                        ins = nc.tensor.transpose(tr_ps[i % 2][:, d * P:(d + 1) * P], yn[:, i, d * P:(d + 1) * P], ident[:])
                    ins.then_inc(yn_turned, 1)
                pe.wait_ge(y_t_ready, NT * (b + 1))
                pe.wait_ge(ex_ready, b)
                for i in range(NT):
                    for d in range(DC):
                        ins = nc.tensor.matmul(lg_ps[:, i, :], y_t[:, d, i * P:(i + 1) * P], rw_t[:, d, :],
                                               start=(d == 0), stop=(d == DC - 1))
                ins.then_inc(logits_done, 1)
                pe.wait_ge(picks_ready, b + 1)
                for i in range(NT):
                    nc.tensor.matmul(pos_ps[:, i, :], before_b[:], picked[:, i, :], start=True, stop=False)
                    ins = nc.tensor.matmul(pos_ps[:, i, :], ones_b[:], seen_b[:, i, :], start=False, stop=True)
                ins.then_inc(places_done, 1)

        @block.vector
        def _(dve):
            dve.wait_ge(loaded, ALL_LOADS)
            nc.vector.tensor_copy(before_b[:], before[:]).then_inc(cast, 1)
            nc.vector.memset(ones_b[:], 1.0).then_inc(cast, 1)
            nc.vector.memset(seen[:], 0.0).then_inc(cast, 1)
            dve.wait_ge(cast, 3)
            with dve.Fori(0, B) as b:
                base = (2 * NT + 1) * b
                dve.wait_ge(x_loaded, 16 * (b + 1))
                for i in range(NT):
                    nc.vector.bn_stats(bn[:, i, :], xb[:, i, :]).then_inc(stats_step, 1)
                dve.wait_ge(stats_step, base + NT)
                nc.vector.memset(newton[:], 0.0)
                for i in range(NT):
                    nc.vector.bn_aggr(mv[:, i, :], bn[:, i, :]).then_inc(stats_step, 1)
                dve.wait_ge(stats_step, base + 2 * NT)
                nc.vector.tensor_scalar(vpe[:], mv[:, :, 1], EPS, None, ALU.add).then_inc(stats_step, 1)
                dve.wait_ge(root_step, 2 * b + 2)
                dve.wait_ge(stats_step, base + 2 * NT + 1)
                for r in range(2):
                    n = 8 * b + 4 * r
                    dve.wait_ge(newton_step, n)
                    nc.vector.tensor_tensor(newton[:], rstd[:], rstd[:], ALU.mult).then_inc(newton_step, 1)
                    dve.wait_ge(newton_step, n + 1)
                    nc.vector.tensor_tensor(newton[:], newton[:], vpe[:], ALU.mult).then_inc(newton_step, 1)
                    dve.wait_ge(newton_step, n + 2)
                    nc.vector.tensor_scalar(newton[:], newton[:], -0.5, 1.5, ALU.mult, ALU.add).then_inc(newton_step, 1)
                    dve.wait_ge(newton_step, n + 3)
                    nc.vector.tensor_tensor(rstd[:], rstd[:], newton[:], ALU.mult).then_inc(newton_step, 1)
                dve.wait_ge(newton_step, 8 * b + 8)
                dve.wait_ge(y_stored, 16 * b)
                dve.wait_ge(yn_turned, NT * b)
                for i in range(NT):
                    nc.vector.tensor_scalar(yn[:, i, :], xb[:, i, :], mv[:, i, 0:1], rstd[:, i:i + 1],
                                            ALU.subtract, ALU.mult).then_inc(yn_ready, 1)
                steps = 0

                def step(ins):
                    nonlocal steps
                    steps += 1
                    ins.then_inc(route_step, 1)
                    dve.wait_ge(route_step, ROUTE_STEPS * b + steps)

                def tt(out, a, c, op):
                    return nc.vector.tensor_tensor(out, a, c, op)

                def over_experts(t):
                    return t.unsqueeze(2).to_broadcast([P, NT, E_])

                def over_tiles(t):
                    return t.unsqueeze(1).to_broadcast([P, NT, E_])

                dve.wait_ge(ex_ready, b + 1)
                step(nc.vector.tensor_scalar(score[:], ex[:], 1.0, None, ALU.add))
                step(nc.vector.reciprocal(score[:], score[:]))
                step(tt(biased[:], score[:], over_tiles(bias[:]), ALU.add))
                pairs = biased[:].rearrange("p i (g q r) -> p (i g) q r", q=GE // 2, r=2)
                step(tt(hi[:], pairs[:, :, :, 0], pairs[:, :, :, 1], ALU.max))
                step(tt(lo[:], pairs[:, :, :, 0], pairs[:, :, :, 1], ALU.min))
                gsf = gs[:].rearrange("p i g -> p (i g)")
                step(tt(gsf, hi[:, :, 0], hi[:, :, 1], ALU.max))
                step(tt(g2[:], hi[:, :, 0], hi[:, :, 1], ALU.min))
                step(tt(g3[:], lo[:, :, 0], lo[:, :, 1], ALU.max))
                step(tt(g2[:], g2[:], g3[:], ALU.max))
                step(tt(gsf, gsf, g2[:], ALU.add))
                for i in range(NT):
                    r = slice(i * GROUPS, (i + 1) * GROUPS)
                    other = gs[:, i, :].unsqueeze(1).to_broadcast([P, GROUPS, GROUPS])
                    own = gs[:, i, :].unsqueeze(2).to_broadcast([P, GROUPS, GROUPS])
                    tt(beats[:, r, :], other, own, ALU.is_gt)
                    ins = tt(ties[:, r, :], other, own, ALU.is_equal)
                step(ins)
                for i in range(NT):
                    r = slice(i * GROUPS, (i + 1) * GROUPS)
                    ins = tt(ties[:, r, :], ties[:, r, :], lower[:], ALU.mult)
                step(ins)
                step(tt(beats[:], beats[:], ties[:], ALU.add))
                step(nc.vector.tensor_reduce(rank[:], beats[:], AX_X, ALU.add))
                step(nc.vector.tensor_scalar(rank[:], rank[:], float(TOP_GROUPS), None, ALU.is_lt))
                step(tt(v[:].rearrange("p i (g q) -> p (i g) q", q=GE), biased[:].rearrange("p i (g q) -> p (i g) q", q=GE),
                        rank[:].unsqueeze(2).to_broadcast([P, NT * GROUPS, GE]), ALU.mult))
                for k in range(K):
                    step(nc.vector.tensor_reduce(top[:], v[:], AX_X, ALU.max))
                    step(tt(cand[:], v[:], over_experts(top[:]), ALU.is_equal))
                    step(tt(cand[:], cand[:], over_tiles(order[:]), ALU.mult))
                    step(nc.vector.tensor_reduce(top[:], cand[:], AX_X, ALU.max))
                    step(tt(hot[:, :, k, :], cand[:], over_experts(top[:]), ALU.is_equal))
                    step(nc.vector.scalar_tensor_tensor(out=v[:], in0=hot[:, :, k, :], scalar=PICKED, in1=v[:],
                                                        op0=ALU.mult, op1=ALU.add))
                dve.wait_ge(places_done, b)
                step(nc.vector.tensor_scalar(cand[:], v[:], 0.5 * PICKED, None, ALU.is_lt))
                for i in range(NT):
                    nc.vector.tensor_copy(seen_b[:, i, :], seen[:])
                    step(tt(seen[:], seen[:], cand[:, i, :], ALU.add))
                nc.vector.tensor_copy(picked[:], cand[:]).then_inc(picks_ready, 1)
                dve.wait_ge(slots_stored, 32 * b)
                dve.wait_ge(scattered, 16 * NT * K * b)
                step(tt(prod[:], hot[:], score[:].unsqueeze(2).to_broadcast([P, NT, K, E_]), ALU.mult))
                step(nc.vector.tensor_reduce(wk[:], prod[:], AX_X, ALU.add))
                step(nc.vector.tensor_reduce(wsum[:], wk[:], AX_X, ALU.add))
                step(nc.vector.tensor_scalar(wsum[:], wsum[:], 1e-20, None, ALU.add))
                step(nc.vector.reciprocal(wsum[:], wsum[:]))
                step(tt(wk[:], wk[:], wsum[:].unsqueeze(2).to_broadcast([P, NT, K]), ALU.mult))
                dve.wait_ge(places_done, b + 1)
                step(nc.vector.tensor_scalar(over[:], pos_ps[:], float(cap), FAR, ALU.is_ge, ALU.mult))
                step(tt(slot[:], pos_ps[:], over_tiles(first[:]), ALU.add))
                step(tt(slot[:], slot[:], over[:], ALU.add))
                step(tt(prod[:], hot[:], slot[:].unsqueeze(2).to_broadcast([P, NT, K, E_]), ALU.mult))
                step(nc.vector.tensor_reduce(sk[:], prod[:], AX_X, ALU.add))
                step(nc.vector.tensor_scalar(ok[:], sk[:], FAR, ROUTE_SCALE, ALU.is_lt, ALU.mult))
                step(tt(wk[:], wk[:], ok[:], ALU.mult))
                nc.vector.tensor_copy(sk_i[:], sk[:]).then_inc(slots_ready, 1)
                assert steps == ROUTE_STEPS, steps


def expert_phase(nc, y, w_gate, w_up, w_down, consts, tokens_dram, y_out):
    T = y.shape[0] * SEQ
    cap = capacity(T)
    n_ct, ct = slot_tiles(cap)
    yf = y.rearrange("b t d -> (b t) d")
    with ExitStack() as ctx:
        def sb(name, shape, dt=F32):
            return ctx.enter_context(nc.sbuf_tensor("e_" + name, shape, dt))

        def sem(name):
            return ctx.enter_context(nc.semaphore("e_" + name))

        ident = sb("ident", [P, P])
        spare = sb("spare", [P, 3])
        who = sb("who", [E_, cap])
        who_i = sb("who_i", [ct, n_ct, E_], I32)
        now = [sb(f"now{n}", [ct, n_ct], I32) for n in range(2)]
        wg = [sb(f"wg{n}", [P, DC, FF]) for n in range(2)]
        wu = [sb(f"wu{n}", [P, DC, FF]) for n in range(2)]
        wd = [sb(f"wd{n}", [P, FC, DM]) for n in range(2)]
        xg = [[sb(f"xg{n}_{j}", [ct, DM]) for j in range(n_ct)] for n in range(2)]
        xp_t = [sb(f"xp_t{n}", [P, DC, cap]) for n in range(2)]
        ex = sb("ex", [P, FC, cap])
        h = [sb(f"h{n}", [P, FC, cap]) for n in range(2)]
        yo = [sb(f"yo{n}", [ct, n_ct, DM]) for n in range(2)]
        tr_ps = [ctx.enter_context(nc.psum_tensor(f"e_tr_ps{n}", [P, 512], F32)) for n in range(2)]
        gate_ps = ctx.enter_context(nc.psum_tensor("e_gate_ps", [P, 512], F32))
        up_ps = ctx.enter_context(nc.psum_tensor("e_up_ps", [P, 512], F32))
        down_ps = [ctx.enter_context(nc.psum_tensor(f"e_down_ps{n}", [P, 512], F32)) for n in range(2)]

        loaded = sem("loaded")
        cleared = sem("cleared")
        who_turned = sem("who_turned")
        who_ready = sem("who_ready")
        now_ready = [sem(f"now_ready{n}") for n in range(2)]
        up_loaded = [sem(f"up_loaded{n}") for n in range(2)]
        down_loaded = [sem(f"down_loaded{n}") for n in range(2)]
        gathered = [sem(f"gathered{n}") for n in range(2)]
        turned = sem("turned")
        xp_ready = sem("xp_ready")
        gate_done = sem("gate_done")
        up_done = sem("up_done")
        ex_ready = sem("ex_ready")
        h_step = sem("h_step")
        down_done = sem("down_done")
        yo_ready = sem("yo_ready")
        stored = [sem(f"stored{n}") for n in range(2)]

        block = ctx.enter_context(nc.Block())

        @block.sync
        def _(sp):
            sp.dma_start(who[:], tokens_dram.rearrange("(e c) o -> e (c o)", e=E_)).then_inc(loaded, 16)
            sp.dma_start(ident[:], consts["ident"]).then_inc(loaded, 16)
            with sp.Fori(0, E_ // 2) as r:
                for n in range(2):
                    e = 2 * r + n
                    sp.wait_ge(up_done, 2 * r)
                    sp.dma_start(wg[n][:], w_gate[e].rearrange("(c p) i -> p c i", p=P)).then_inc(up_loaded[n], 16)
                    sp.dma_start(wu[n][:], w_up[e].rearrange("(c p) i -> p c i", p=P)).then_inc(up_loaded[n], 16)
                    sp.wait_ge(down_done, 2 * n_ct * r)
                    sp.dma_start(wd[n][:], w_down[e].rearrange("(c p) d -> p c d", p=P)).then_inc(down_loaded[n], 16)

        @block.gpsimd
        def _(pool):
            for n in range(2):
                for j in range(n_ct):
                    nc.gpsimd.memset(xg[n][j][:], 0.0)
            nc.gpsimd.memset(spare[:], 0.0).then_inc(cleared, 1)
            pool.wait_ge(cleared, 1)
            pool.wait_ge(who_ready, 1)
            with pool.Fori(0, E_ // 2) as r:
                for n in range(2):
                    pool.wait_ge(who_ready, 1)
                    pool.wait_ge(gathered[n], 16 * n_ct * r)
                    nc.gpsimd.tensor_copy(now[n][:], who_i[:, :, bass.ds(2 * r + n, 1)].rearrange("p j e -> p (j e)")).then_inc(now_ready[n], 1)
                for n in range(2):
                    pool.wait_ge(now_ready[n], r + 1)
                    pool.wait_ge(turned, 2 * n_ct * r)
                    nc.gpsimd.tensor_tensor(spare[:, 1 + n:2 + n], spare[:, 0:1], spare[:, 0:1], ALU.add)
                    for j in range(n_ct):
                        pool.indirect_dma_start(xg[n][j][:], None, yf, bass.IndirectOffsetOnAxis(ap=now[n][:, j:j + 1], axis=0),
                                                bounds_check=T - 1, oob_is_err=False).then_inc(gathered[n], 16)

        @block.scalar
        def _(act):
            act.preload_act_table_set("natural_log_exp_and_others")
            with act.Fori(0, E_ // 2) as r:
                for n in range(2):
                    e = 2 * r + n
                    for j in range(n_ct):
                        act.wait_ge(turned, n_ct * e + j + 1)
                        act.wait_ge(up_done, 2 * r)
                        nc.scalar.copy(xp_t[n][:, :, j * ct:(j + 1) * ct],
                                       tr_ps[j % 2][:, 0:DC * ct].rearrange("p (c t) -> p c t", c=DC)).then_inc(xp_ready, 1)
                    act.wait_ge(gate_done, e + 1)
                    act.wait_ge(h_step, 4 * e)
                    nc.scalar.activation(ex[:], gate_ps[:, 0:FC * cap].rearrange("p (c t) -> p c t", c=FC), ACT.Exp,
                                         scale=-1.0).then_inc(ex_ready, 1)
                    act.wait_ge(stored[n], 16 * r)
                    for j in range(n_ct):
                        act.wait_ge(down_done, n_ct * e + j + 1)
                        nc.scalar.copy(yo[n][:, j, :], down_ps[j % 2][0:ct, :]).then_inc(yo_ready, 1)
                    act.wait_ge(yo_ready, n_ct * (e + 1))
                    act.dma_start(y_out[e].rearrange("(j p) d -> p j d", p=ct), yo[n][:]).then_inc(stored[n], 16)
            for n in range(2):
                act.wait_ge(stored[n], 16 * (E_ // 2))

        @block.vector
        def _(dve):
            dve.wait_ge(who_turned, 1)
            nc.vector.tensor_copy(who_i[:], gate_ps[0:ct, 0:n_ct * E_].rearrange("p (j e) -> p j e", e=E_)).then_inc(who_ready, 1)
            with dve.Fori(0, E_ // 2) as r:
                for n in range(2):
                    e = 2 * r + n
                    dve.wait_ge(ex_ready, e + 1)
                    nc.vector.tensor_scalar(ex[:], ex[:], 1.0, None, ALU.add).then_inc(h_step, 1)
                    dve.wait_ge(h_step, 4 * e + 1)
                    nc.vector.reciprocal(ex[:], ex[:]).then_inc(h_step, 1)
                    dve.wait_ge(h_step, 4 * e + 2)
                    nc.vector.tensor_tensor(ex[:], ex[:], gate_ps[:, 0:FC * cap].rearrange("p (c t) -> p c t", c=FC),
                                            ALU.mult).then_inc(h_step, 1)
                    dve.wait_ge(h_step, 4 * e + 3)
                    dve.wait_ge(up_done, e + 1)
                    dve.wait_ge(down_done, 2 * n_ct * r)
                    nc.vector.tensor_tensor(h[n][:], ex[:], up_ps[:, 0:FC * cap].rearrange("p (c t) -> p c t", c=FC),
                                            ALU.mult).then_inc(h_step, 1)

        @block.tensor
        def _(pe):
            pe.wait_ge(loaded, 32)
            for j in range(n_ct):
                ins = nc.tensor.transpose(gate_ps[0:ct, j * E_:(j + 1) * E_], who[:, j * ct:(j + 1) * ct], ident[0:E_, 0:E_])
            ins.then_inc(who_turned, 1)
            pe.wait_ge(who_ready, 1)
            with pe.Fori(0, E_ // 2) as r:
                for n in range(2):
                    e = 2 * r + n
                    pe.wait_ge(gathered[n], 16 * n_ct * (r + 1))
                    for j in range(n_ct):
                        pe.wait_ge(xp_ready, n_ct * e + max(j - 1, 0))
                        for d in range(DC):
                            ins = nc.tensor.transpose(tr_ps[j % 2][:, d * ct:(d + 1) * ct], xg[n][j][:, d * P:(d + 1) * P],
                                                      ident[0:ct, 0:ct])
                        ins.then_inc(turned, 1)
                    pe.wait_ge(xp_ready, n_ct * (e + 1))
                    pe.wait_ge(up_loaded[n], 32 * (r + 1))
                    pe.wait_ge(h_step, 4 * e)
                    for w, ps, done in ((wg, gate_ps, gate_done), (wu, up_ps, up_done)):
                        for f in range(FC):
                            for d in range(DC):
                                ins = nc.tensor.matmul(ps[:, f * cap:(f + 1) * cap], w[n][:, d, f * P:(f + 1) * P],
                                                       xp_t[n][:, d, :], start=(d == 0), stop=(d == DC - 1))
                        ins.then_inc(done, 1)
                    pe.wait_ge(h_step, 4 * (e + 1))
                    pe.wait_ge(down_loaded[n], 16 * (r + 1))
                    for j in range(n_ct):
                        pe.wait_ge(yo_ready, n_ct * e + max(j - 1, 0))
                        for f in range(FC):
                            ins = nc.tensor.matmul(down_ps[j % 2][0:ct, :], h[n][:, f, j * ct:(j + 1) * ct], wd[n][:, f, :],
                                                   start=(f == 0), stop=(f == FC - 1))
                        ins.then_inc(down_done, 1)


def combine_phase(nc, x2, y, shared_gate, shared_up, shared_down, consts, slots_dram, weights_dram, y_out, out):
    B = x2.shape[0]
    T = B * SEQ
    cap = capacity(T)
    rows = y_out.rearrange("e c d -> (e c) d")
    with ExitStack() as ctx:
        def sb(name, shape, dt=F32):
            return ctx.enter_context(nc.sbuf_tensor("c_" + name, shape, dt))

        def sem(name):
            return ctx.enter_context(nc.semaphore("c_" + name))

        ident = sb("ident", [P, P])
        raw = [sb(f"raw{n}", [P, 4, DM]) for n in range(3)]
        turned_w = [sb(f"w_t{n}", [P, 4, DM]) for n in range(3)]
        sg, su, sd = turned_w
        yb = sb("yb", [P, NT, DM])
        xb = sb("xb", [P, NT, DM])
        y_t = sb("y_t", [P, DC, SEQ])
        ex = sb("ex", [P, SEQ])
        h = sb("h", [P, SC, SEQ])
        acc = sb("acc", [P, NT, DM])
        spare = sb("spare", [P, 3])
        part = sb("part", [P, NT, K, DM])
        si = sb("si", [P, NT * K], I32)
        wk = sb("wk", [P, NT * K])
        tr_ps = [ctx.enter_context(nc.psum_tensor(f"c_tr_ps{n}", [P, 512], F32)) for n in range(2)]
        gate_ps = [ctx.enter_context(nc.psum_tensor(f"c_gate_ps{n}", [P, 512], F32)) for n in range(2)]
        up_ps = [ctx.enter_context(nc.psum_tensor(f"c_up_ps{n}", [P, 512], F32)) for n in range(2)]
        down_ps = [ctx.enter_context(nc.psum_tensor(f"c_down_ps{n}", [P, 512], F32)) for n in range(2)]

        loaded = sem("loaded")
        w_turned = sem("w_turned")
        w_ready = sem("w_ready")
        cleared = sem("cleared")
        y_loaded = sem("y_loaded")
        x_loaded = sem("x_loaded")
        carried = sem("carried")
        slots_loaded = sem("slots_loaded")
        gathered = sem("gathered")
        y_turned = sem("y_turned")
        y_t_ready = sem("y_t_ready")
        gate_done = sem("gate_done")
        up_done = sem("up_done")
        ex_ready = sem("ex_ready")
        h_step = sem("h_step")
        down_done = sem("down_done")
        acc_step = sem("acc_step")
        stored = sem("stored")
        STEPS = K + 1
        block = ctx.enter_context(nc.Block())

        @block.sync
        def _(sp):
            sp.dma_start(ident[:], consts["ident"]).then_inc(loaded, 16)
            for to, w in zip(raw, (shared_gate, shared_up, shared_down)):
                sp.dma_start(to[:], w.rearrange("(r p) n -> p r n", p=P)).then_inc(loaded, 16)
            with sp.Fori(0, B) as b:
                sp.wait_ge(y_turned, NT * b)
                sp.dma_start(yb[:], y[b].rearrange("(i p) d -> p i d", p=P)).then_inc(y_loaded, 16)
                sp.wait_ge(acc_step, STEPS * NT * b)
                sp.dma_start(xb[:], x2[b].rearrange("(i p) d -> p i d", p=P)).then_inc(x_loaded, 16)
                sp.dma_start(wk[:], weights_dram[b]).then_inc(x_loaded, 16)
                sp.wait_ge(gathered, 16 * NT * K * b)
                sp.dma_start(si[:], slots_dram[b]).then_inc(slots_loaded, 16)

        @block.gpsimd
        def _(pool):
            nc.gpsimd.memset(part[:], 0.0)
            nc.gpsimd.memset(spare[:], 0.0).then_inc(cleared, 1)
            pool.wait_ge(cleared, 1)
            with pool.Fori(0, B) as b:
                pool.wait_ge(slots_loaded, 16 * (b + 1))
                pool.wait_ge(acc_step, STEPS * NT * b)
                pool.wait_ge(carried, b)
                nc.gpsimd.tensor_tensor(spare[:, 1:2], spare[:, 0:1], spare[:, 0:1], ALU.add).then_inc(carried, 1)
                for i in range(NT):
                    for k in range(K):
                        j = K * i + k
                        pool.indirect_dma_start(part[:, i, k, :], None, rows, bass.IndirectOffsetOnAxis(ap=si[:, j:j + 1], axis=0),
                                                bounds_check=E_ * cap - 1, oob_is_err=False).then_inc(gathered, 16)

        @block.scalar
        def _(act):
            act.preload_act_table_set("natural_log_exp_and_others")
            for n in range(3):
                for r in range(4):
                    m = 4 * n + r
                    act.wait_ge(w_turned, m + 1)
                    nc.scalar.copy(turned_w[n][:, :, r * P:(r + 1) * P], tr_ps[m % 2][:].rearrange("p (c t) -> p c t", c=4)).then_inc(w_ready, 1)
            with act.Fori(0, B) as b:
                for i in range(NT):
                    act.wait_ge(y_turned, NT * b + i + 1)
                    act.wait_ge(up_done, SC * b)
                    nc.scalar.copy(y_t[:, :, i * P:(i + 1) * P],
                                   tr_ps[i % 2][:].rearrange("p (c t) -> p c t", c=DC)).then_inc(y_t_ready, 1)
                for f in range(SC):
                    m = SC * b + f
                    act.wait_ge(gate_done, m + 1)
                    act.wait_ge(h_step, 4 * m)
                    nc.scalar.activation(ex[:], gate_ps[f % 2][:], ACT.Exp, scale=-1.0).then_inc(ex_ready, 1)
                for i in range(NT):
                    act.wait_ge(acc_step, STEPS * (NT * b + i + 1))
                    act.dma_start(out[b, i * P:(i + 1) * P, :], acc[:, i, :]).then_inc(stored, 16)
            act.wait_ge(stored, 16 * NT * B)

        @block.vector
        def _(dve):
            with dve.Fori(0, B) as b:
                for f in range(SC):
                    m = SC * b + f
                    dve.wait_ge(ex_ready, m + 1)
                    nc.vector.tensor_scalar(ex[:], ex[:], 1.0, None, ALU.add).then_inc(h_step, 1)
                    dve.wait_ge(h_step, 4 * m + 1)
                    nc.vector.reciprocal(ex[:], ex[:]).then_inc(h_step, 1)
                    dve.wait_ge(h_step, 4 * m + 2)
                    nc.vector.tensor_tensor(ex[:], ex[:], gate_ps[f % 2][:], ALU.mult).then_inc(h_step, 1)
                    dve.wait_ge(h_step, 4 * m + 3)
                    dve.wait_ge(up_done, m + 1)
                    dve.wait_ge(down_done, NT * b)
                    nc.vector.tensor_tensor(h[:, f, :], ex[:], up_ps[f % 2][:], ALU.mult).then_inc(h_step, 1)
                dve.wait_ge(x_loaded, 32 * (b + 1))
                dve.wait_ge(stored, 16 * NT * b)
                dve.wait_ge(gathered, 16 * NT * K * (b + 1))
                for i in range(NT):
                    m = NT * b + i
                    dve.wait_ge(down_done, m + 1)
                    nc.vector.tensor_tensor(acc[:, i, :], down_ps[i % 2][:], xb[:, i, :], ALU.add).then_inc(acc_step, 1)
                    for k in range(K):
                        dve.wait_ge(acc_step, STEPS * m + k + 1)
                        nc.vector.scalar_tensor_tensor(out=acc[:, i, :], in0=part[:, i, k, :], scalar=wk[:, K * i + k:K * i + k + 1],
                                                       in1=acc[:, i, :], op0=ALU.mult, op1=ALU.add).then_inc(acc_step, 1)

        @block.tensor
        def _(pe):
            pe.wait_ge(loaded, 16 * 4)
            for n in range(3):
                for r in range(4):
                    m = 4 * n + r
                    if m >= 2:
                        pe.wait_ge(w_ready, m - 1)
                    for q in range(4):
                        ins = nc.tensor.transpose(tr_ps[m % 2][:, q * P:(q + 1) * P], raw[n][:, r, q * P:(q + 1) * P], ident[:])
                    ins.then_inc(w_turned, 1)
            pe.wait_ge(w_ready, 12)
            with pe.Fori(0, B) as b:
                pe.wait_ge(y_loaded, 16 * (b + 1))
                for i in range(NT):
                    pe.wait_ge(y_t_ready, NT * b + (i - 1 if i >= 2 else 0))
                    for d in range(DC):
                        ins = nc.tensor.transpose(tr_ps[i % 2][:, d * P:(d + 1) * P], yb[:, i, d * P:(d + 1) * P], ident[:])
                    ins.then_inc(y_turned, 1)
                pe.wait_ge(y_t_ready, NT * (b + 1))
                for f in range(SC):
                    m = SC * b + f
                    pe.wait_ge(h_step, 4 * (SC * b + (f - 1 if f >= 2 else 0)))
                    for w, ps, done in ((sg, gate_ps, gate_done), (su, up_ps, up_done)):
                        for d in range(DC):
                            ins = nc.tensor.matmul(ps[f % 2][:], w[:, d, f * P:(f + 1) * P], y_t[:, d, :],
                                                   start=(d == 0), stop=(d == DC - 1))
                        ins.then_inc(done, 1)
                pe.wait_ge(h_step, 4 * SC * (b + 1))
                for i in range(NT):
                    pe.wait_ge(acc_step, STEPS * (NT * b + (i - 1 if i >= 2 else 0)))
                    for f in range(SC):
                        ins = nc.tensor.matmul(down_ps[i % 2][:], h[:, f, i * P:(i + 1) * P], sd[:, f, :],
                                               start=(f == 0), stop=(f == SC - 1))
                    ins.then_inc(down_done, 1)


def host_constants():
    inv = (1.0 / np.float32(ROPE_THETA) ** (np.arange(0, DH, 2, dtype=np.float32) / np.float32(DH))).astype(np.float32)
    ang = (np.arange(SEQ, dtype=np.float32)[:, None] * inv[None, :]).astype(np.float32)
    at = np.arange(P)
    return {
        "rope": np.stack([np.cos(ang), np.sin(ang)], 1).astype(np.float32),
        "ident": np.eye(P, dtype=np.float32),
        "upto": (at[:, None] <= at[None, :]).astype(np.float32) / np.float32(GATE_NORM),
        "beyond": (at[:, None] > at[None, :]).astype(np.float32) / np.float32(GATE_NORM),
        "keep": (at[:, None] <= at[None, :]).astype(np.float32),
    }


def host_constants2(T):
    cap = capacity(T)
    at = np.arange(P)
    c = host_constants()
    c["before"] = (at[:, None] < at[None, :]).astype(np.float32)
    c["first"] = (np.arange(E_) * cap).astype(np.float32)
    c["order"] = (E_ - np.arange(E_)).astype(np.float32)
    g = np.arange(GROUPS)
    c["lower"] = (g[None, :] < g[:, None]).astype(np.float32)
    c["token"] = np.repeat((np.arange(T // P)[None, :] * P + at[:, None])[:, :, None], K, 2).astype(np.float32)
    c["no_token"] = np.full((E_, cap), T, np.float32)
    return c


def block_kernel(nc, a, consts, out):
    x = a["L0_attn_hidden_states"]
    B = x.shape[0]
    cap = capacity(B * SEQ)

    def scratch(name, shape, dt=F32):
        return nc.dram_tensor(name, shape, dt, kind="Internal").ap()

    x2 = scratch("x2", [B, SEQ, DM])
    y = scratch("y", [B, SEQ, DM])
    slots = scratch("slots", [B, P, NT * K], I32)
    weights = scratch("weights", [B, P, NT * K])
    tokens = scratch("tokens", [E_ * cap, 1])
    y_out = scratch("y_out", [E_, cap, DM])
    attention_phase(nc, x, a["L0_attn_Wq"], a["L0_attn_Wk"], a["L0_attn_Wv"], a["L0_attn_Wo"], consts, x2)
    routing_phase(nc, x2, a["L0_ffn_router_w"], a["L0_ffn_e_bias"], consts, y, slots, weights, tokens)
    expert_phase(nc, y, a["L0_ffn_W_gate"], a["L0_ffn_W_up"], a["L0_ffn_W_down"], consts, tokens, y_out)
    combine_phase(nc, x2, y, a["L0_ffn_shared_gate"], a["L0_ffn_shared_up"], a["L0_ffn_shared_down"], consts, slots,
                  weights, y_out, out)


_INS = ["L0_attn_hidden_states", "L0_attn_Wq", "L0_attn_Wk", "L0_attn_Wv", "L0_attn_Wo", "L0_ffn_router_w",
        "L0_ffn_e_bias", "L0_ffn_W_gate", "L0_ffn_W_up", "L0_ffn_W_down", "L0_ffn_shared_gate", "L0_ffn_shared_up",
        "L0_ffn_shared_down"]


def kernel(**inputs):
    import concourse.bacc as _bacc
    from concourse.bass_utils import run_bass_kernel_spmd as _run

    nc = _bacc.Bacc("TRN2", target_bir_lowering=False, num_devices=1)
    arrays, ins, consts = {}, {}, {}
    for name in _INS:
        a = np.ascontiguousarray(inputs[name])
        arrays[f"in_{name}_dram"] = a
        ins[name] = nc.dram_tensor(f"in_{name}_dram", a.shape, mybir.dt.from_np(a.dtype), kind="ExternalInput").ap()
    shape = inputs["L0_attn_hidden_states"].shape
    for name, a in host_constants2(shape[0] * shape[1]).items():
        arrays[f"const_{name}_dram"] = a
        consts[name] = nc.dram_tensor(f"const_{name}_dram", a.shape, mybir.dt.from_np(a.dtype), kind="ExternalInput").ap()
    out = nc.dram_tensor("out_0_dram", shape, F32, kind="ExternalOutput").ap()
    block_kernel(nc, ins, consts, out)
    r = _run(nc, [arrays], core_ids=[0])
    return r.results[0]["out_0_dram"]
```

```python
from contextlib import ExitStack

import concourse.bass as bass
import numpy as np
from concourse import mybir

P = 128
F32 = mybir.dt.float32
BF16 = mybir.dt.bfloat16
I32 = mybir.dt.int32
U32 = mybir.dt.uint32
ALU = mybir.AluOpType
ACT = mybir.ActivationFunctionType
AX_X = mybir.AxisListType.X

DM = 512
DC = DM // P
HEADS = 16
KV = 4
G = HEADS // KV
DH = 128
HALF = DH // 2
SEQ = 512
NT = SEQ // P
SUB = 32
NSUB = P // SUB
EPS = 1e-5
GATE_NORM = 16.0
ROPE_THETA = 10000.0
HUGE = 3.0e38
NEG = -1.0e30


def attention_phase(nc, x, w_q, w_k, w_v, w_o, consts, x2):
    B = x.shape[0]
    QK = (G + 1) * DH
    with ExitStack() as ctx:
        def sb(name, shape, dt=F32):
            return ctx.enter_context(nc.sbuf_tensor(name, shape, dt))

        def sem(name):
            return ctx.enter_context(nc.semaphore(name))

        wq = sb("wq", [P, DC, HEADS * DH])
        wkv = sb("wkv", [P, DC, KV, 2 * DH])
        wo = sb("wo", [P, HEADS, DM])
        rope = sb("rope", [P, NT, 2, HALF])
        ident = sb("ident", [P, P])
        upto = sb("upto", [P, P])
        beyond = sb("beyond", [P, P])
        keep = sb("keep", [P, P])
        ident_b = sb("ident_b", [P, P], BF16)
        future_b = sb("future_b", [P, P], BF16)
        qr_t = [sb(f"qr_t{n}", [P, G, SEQ]) for n in range(2)]
        kr_t = [sb(f"kr_t{n}", [P, SEQ]) for n in range(2)]
        val = [sb(f"val{n}", [P, NT, DH]) for n in range(2)]
        q_in = [sb(f"q_in{n}", [P, G, SEQ - P]) for n in range(2)]
        local = [sb(f"local{n}", [P, NT, G, P]) for n in range(2)]
        state = [sb(f"state{n}", [P, NT - 1, DH]) for n in range(2)]
        o_t = sb("o_t", [P, G, SEQ])
        x_in = sb("x_in", [P, NT, DM])
        x_acc = sb("x_acc", [P, NT, DM])
        x_t = sb("x_t", [P, DC, SEQ])
        parts = sb("parts", [P, 2, QK])
        xn = [parts[:, n, 0:DM] for n in range(2)]
        qk = sb("qk", [P, QK])
        rot = sb("rot", [P, QK])
        soft = sb("soft", [P, QK])
        neg_top = sb("neg_top", [P, G + 1])
        tot = sb("tot", [P, G + 1])
        inv_tot = sb("inv_tot", [P, G + 1])
        logs = sb("logs", [P, DH])
        gate = sb("gate", [P, DH])
        decay = sb("decay", [P, (NSUB + 1) * P])
        keys = sb("keys", [P, 4 * P])
        span = sb("span", [P, 2 * P])
        k_dec = sb("k_dec", [P, NSUB, P])
        q_dec = sb("q_dec", [P, G, P])
        k_rest = sb("k_rest", [P, DH])
        prob = sb("prob", [P, 2, SEQ])
        prob_t = sb("prob_t", [P, NT, SEQ])
        neg_max = sb("neg_max", [P, G * NT])
        row_sum = sb("row_sum", [P, G * NT])
        inv_sum = sb("inv_sum", [P, G * NT])
        bn = sb("bn", [P, NT, 6])
        mv = sb("mv", [P, NT, 2])
        vpe = sb("vpe", [P, NT])
        rstd = sb("rstd", [P, NT])
        newton = sb("newton", [P, NT])

        qkv_ps = ctx.enter_context(nc.psum_tensor("qkv_ps", [P, 2 * 512], F32))
        tr_ps = [ctx.enter_context(nc.psum_tensor(f"tr_ps{n}", [P, 512], F32)) for n in range(2)]
        score_ps = [ctx.enter_context(nc.psum_tensor(f"score_ps{n}", [P, 512], F32)) for n in range(2)]
        out_ps = ctx.enter_context(nc.psum_tensor("out_ps", [P, 512], F32))
        prob_ps = [out_ps, ctx.enter_context(nc.psum_tensor("prob_ps", [P, 512], F32))]

        loaded = sem("weights_loaded")
        masks_cast = sem("masks_cast")
        x_loaded = sem("x_loaded")
        x2_stored = sem("x2_stored")
        stats_step = sem("stats_step")
        root_step = sem("root_step")
        newton_step = sem("newton_step")
        xn_ready = sem("xn_ready")
        xn_turned = sem("xn_turned")
        x_t_ready = sem("x_t_ready")
        q_done = sem("q_done")
        kv_done = sem("kv_done")
        tops_ready = sem("tops_ready")
        parts_ready = sem("parts_ready")
        logs_step = sem("logs_step")
        gate_ready = sem("gate_ready")
        qk_ready = sem("qk_ready")
        val_ready = sem("val_ready")
        exps_ready = sem("exps_ready")
        inv_ready = sem("inv_ready")
        rot_ready = sem("rot_ready")
        soft_ready = sem("soft_ready")
        keys_turned = sem("keys_turned")
        kr_t_ready = sem("kr_t_ready")
        keys_copied = sem("keys_copied")
        span_ready = sem("span_ready")
        diffs_ready = sem("diffs_ready")
        decay_ready = sem("decay_ready")
        queries_turned = sem("queries_turned")
        qr_t_ready = sem("qr_t_ready")
        soft_turned = sem("soft_turned")
        k_dec_ready = sem("k_dec_ready")
        q_dec_ready = sem("q_dec_ready")
        q_in_ready = sem("q_in_ready")
        k_rest_ready = sem("k_rest_ready")
        update_done = sem("update_done")
        state_ready = sem("state_ready")
        local_done = sem("local_done")
        local_ready = sem("local_ready")
        scores_done = sem("scores_done")
        max_ready = sem("max_ready")
        exp_ready = [sem(f"exp_ready{n}") for n in range(2)]
        inv_sum_ready = sem("inv_sum_ready")
        prob_ready = sem("prob_ready")
        prob_turned = [sem(f"prob_turned{n}") for n in range(2)]
        past_copied = sem("past_copied")
        diag_ready = sem("diag_ready")
        attended = sem("attended")
        o_t_ready = sem("o_t_ready")
        projected = sem("projected")
        x2_added = [sem(f"x2_added{n}") for n in range(2)]

        PROJECTION = (0, 1, 3, 2)
        ALL_LOADS = 16 * (2 * DC + 2 + 5)

        def each_sequence(eng, head, unit):
            head()
            unit(None, 0, 0, True, False)

            def sequence(b, last):
                for g in range(KV):
                    unit(KV * b + g, b, g, not (g == KV - 1 and last), not last)
            if B > 1:
                with eng.Fori(0, B - 1) as b:
                    sequence(b, False)
            sequence(B - 1, True)

        def block_index(c, h, i):
            return G * NT * c + NT * h + NT - 1 - i

        def use_index(c, h, i):
            return G * NT // 2 * c + NT // 2 * h + (NT - 1 - i) // 2

        block = ctx.enter_context(nc.Block())

        @block.sync
        def _(sp):
            sp.dma_start(x_in[:], x[0].rearrange("(i p) d -> p i d", p=P)).then_inc(x_loaded, 16)
            sp.dma_start(rope[:], consts["rope"].rearrange("(i p) a d -> p i a d", p=P)).then_inc(loaded, 16)
            for to, name in ((ident, "ident"), (upto, "upto"), (beyond, "beyond"), (keep, "keep")):
                sp.dma_start(to[:], consts[name]).then_inc(loaded, 16)
            for n, w in enumerate((w_k, w_v)):
                for d in range(DC):
                    sp.dma_start(wkv[:, d, :, n * DH:(n + 1) * DH],
                                 w[d * P:(d + 1) * P, :].rearrange("p (g d) -> p g d", d=DH)).then_inc(loaded, 16)
            sp.dma_start(wq[:], w_q.rearrange("(c p) n -> p c n", p=P)).then_inc(loaded, 16)
            sp.dma_start(wo[:], w_o.rearrange("(h p) n -> p h n", p=P)).then_inc(loaded, 16)
            if B > 1:
                with sp.Fori(0, B - 1) as b:
                    for n in range(2):
                        sp.wait_ge(x2_added[n], KV * (NT // 2) * b + NT // 2)
                    sp.dma_start(x_in[:], x[b + 1].rearrange("(i p) d -> p i d", p=P)).then_inc(x_loaded, 16)
                    for n in range(2):
                        sp.wait_ge(x2_added[n], KV * (NT // 2) * (b + 1))
                    sp.dma_start(x2[b].rearrange("(i p) d -> p i d", p=P), x_acc[:]).then_inc(x2_stored, 16)
            for n in range(2):
                sp.wait_ge(x2_added[n], KV * (NT // 2) * B)
            sp.dma_start(x2[B - 1].rearrange("(i p) d -> p i d", p=P), x_acc[:]).then_inc(x2_stored, 16)
            sp.wait_ge(x2_stored, 16 * B)

        @block.gpsimd
        def _(pool):
            pool.wait_ge(loaded, ALL_LOADS)

            def rotate(a):
                pool.wait_ge(parts_ready, a + 1)
                pool.wait_ge(keys_turned, a)
                pool.wait_ge(queries_turned, a)
                xc = parts[:, 0, :].rearrange("p (h s d) -> p h s d", s=2, d=HALF)
                xs = parts[:, 1, :].rearrange("p (h s d) -> p h s d", s=2, d=HALF)
                r = rot[:].rearrange("p (h s d) -> p h s d", s=2, d=HALF)
                nc.gpsimd.tensor_tensor(r[:, :, 0, :], xc[:, :, 0, :], xs[:, :, 1, :], ALU.subtract)
                nc.gpsimd.tensor_tensor(r[:, :, 1, :], xc[:, :, 1, :], xs[:, :, 0, :], ALU.add).then_inc(rot_ready, 1)

            def differences(a):
                pool.wait_ge(keys_copied, a + 1)
                pool.wait_ge(q_dec_ready, a)
                run = keys[:, 2 * P:3 * P]
                runs = run.rearrange("p (c s) -> p c s", s=SUB)
                mid = runs[:, :, SUB // 2 - 1:SUB // 2]
                nc.gpsimd.tensor_tensor(decay[:, 0:NSUB * P].rearrange("p (c s) -> p c s", s=P),
                                        mid.to_broadcast([P, NSUB, P]),
                                        run.unsqueeze(1).to_broadcast([P, NSUB, P]), ALU.subtract)
                nc.gpsimd.tensor_tensor(decay[:, NSUB * P:(NSUB + 1) * P].rearrange("p (c s) -> p c s", s=SUB),
                                        runs, mid.to_broadcast([P, NSUB, SUB]), ALU.subtract).then_inc(diffs_ready, 1)

            def scaled_keys(a, p, i):
                nc.gpsimd.tensor_scalar(kr_t[p][:, i * P:(i + 1) * P], keys[:, 0:P], float(DH) ** -0.5, None,
                                        ALU.mult).then_inc(kr_t_ready, 1)

            def key_rest(ua, i):
                a, n = NT * ua + i, (NT - 1) * ua + i
                pool.wait_ge(span_ready, a + 1)
                pool.wait_ge(update_done, n)
                pool.wait_ge(soft_ready, a + 1)
                nc.gpsimd.tensor_tensor(k_rest[:], span[:, P:2 * P], soft[:, G * DH:QK], ALU.mult).then_inc(k_rest_ready, 1)

            def unit(c, b, g, prepare, more):
                ua, p = (0, 0) if c is None else (c + 1, (g + 1) % 2)
                if prepare and c is not None:
                    pool.wait_ge(attended, G * c)
                for s in range(NT):
                    if prepare and s:
                        differences(NT * ua + s - 1)
                        scaled_keys(NT * ua + s - 1, p, s - 1)
                        key_rest(ua, s - 1)
                    if prepare:
                        rotate(NT * ua + s)
                if prepare:
                    differences(NT * ua + NT - 1)
                    scaled_keys(NT * ua + NT - 1, p, NT - 1)
            each_sequence(pool, lambda: None, unit)

        @block.scalar
        def _(act):
            act.preload_act_table_set("natural_log_exp_and_others")
            act.wait_ge(loaded, ALL_LOADS)

            def root(b):
                act.wait_ge(stats_step, (2 * NT + 1) * (b + 1))
                nc.scalar.activation(rstd[:], vpe[:], ACT.Ln).then_inc(root_step, 1)
                act.wait_ge(root_step, 2 * b + 1)
                nc.scalar.activation(rstd[:], rstd[:], ACT.Exp, scale=-0.5).then_inc(root_step, 1)

            def turned_x(b):
                act.wait_ge(kv_done, KV * NT * b)
                for i in range(NT):
                    act.wait_ge(xn_turned, NT * b + i + 1)
                    nc.scalar.copy(x_t[:, :, i * P:(i + 1) * P],
                                   tr_ps[i % 2][:].rearrange("p (c t) -> p c t", c=DC)).then_inc(x_t_ready, 1)

            def head():
                root(0)
                turned_x(0)

            def exponent(c, h, i):
                n, k, j, w = block_index(c, h, i), use_index(c, h, i), NT * h + i, P * (i + 1)
                act.wait_ge(max_ready, n + 1)
                act.wait_ge(prob_turned[i % 2], k)
                nc.scalar.activation(prob[:, i % 2, 0:w], score_ps[i % 2][:, 0:w], ACT.Exp, bias=neg_max[:, j:j + 1],
                                     accum_out=row_sum[:, j:j + 1]).then_inc(exp_ready[i % 2], 1)

            def past(c, h, i):
                act.wait_ge(diag_ready, block_index(c, h, i) + 1)
                act.wait_ge(attended, G * c + h)
                nc.scalar.copy(prob_t[:, 0:i, i * P:(i + 1) * P],
                               prob_ps[i % 2][:, 0:i * P].rearrange("p (j t) -> p j t", t=P)).then_inc(past_copied, 1)

            def out_copy(c, h):
                act.wait_ge(attended, G * c + h + 1)
                act.wait_ge(projected, NT * c)
                nc.scalar.copy(o_t[:, h, :], out_ps[:]).then_inc(o_t_ready, 1)

            def take_products(a, p, i):
                act.wait_ge(q_done, a + 1)
                act.wait_ge(kv_done, a + 1)
                act.wait_ge(parts_ready, a)
                act.wait_ge(gate_ready, a)
                nc.scalar.copy(qk[:], qkv_ps[:, 0:QK]).then_inc(qk_ready, 1)
                nc.scalar.copy(val[p][:, i, :], qkv_ps[:, QK:QK + DH]).then_inc(val_ready, 1)
                act.wait_ge(qk_ready, a + 1)
                nc.scalar.activation(logs[:], qk[:, G * DH:QK], ACT.Abs).then_inc(logs_step, 1)

            def gates(a):
                act.wait_ge(logs_step, 3 * a + 1)
                nc.scalar.activation(logs[:], logs[:], ACT.Exp, scale=-1.0).then_inc(logs_step, 1)
                act.wait_ge(logs_step, 3 * a + 2)
                nc.scalar.activation(logs[:], logs[:], ACT.Ln, bias=1.0).then_inc(logs_step, 1)

            def feature_exps(a, ua, i):
                act.wait_ge(tops_ready, a + 1)
                act.wait_ge(soft_turned, a)
                act.wait_ge(k_rest_ready, (NT - 1) * ua + min(i, NT - 1))
                for h in range(G + 1):
                    ins = nc.scalar.activation(soft[:, h * DH:(h + 1) * DH], qk[:, h * DH:(h + 1) * DH], ACT.Exp,
                                               bias=neg_top[:, h:h + 1], accum_out=tot[:, h:h + 1])
                ins.then_inc(exps_ready, 1)

            def turned(a, ua, p, i):
                act.wait_ge(keys_copied, a + 1)
                act.wait_ge(k_rest_ready, (NT - 1) * ua + i)
                act.wait_ge(q_in_ready, (NT - 1) * ua + max(i - 1, 0))
                act.wait_ge(state_ready, (NT - 1) * ua + i)
                nc.scalar.activation(span[:], keys[:, 2 * P:4 * P], ACT.Exp).then_inc(span_ready, 1)
                act.wait_ge(queries_turned, a + 1)
                nc.scalar.copy(qr_t[p][:, :, i * P:(i + 1) * P],
                               tr_ps[1][:].rearrange("p (h t) -> p h t", t=P)).then_inc(qr_t_ready, 1)
                act.wait_ge(diffs_ready, a + 1)
                nc.scalar.activation(decay[:], decay[:], ACT.Exp).then_inc(decay_ready, 1)

            def unit(c, b, g, prepare, more):
                ua, p = (0, 0) if c is None else (c + 1, (g + 1) % 2)
                if prepare and c is not None:
                    act.wait_ge(attended, G * c)
                if c is not None:
                    exponent(c, 0, 3)
                    exponent(c, 0, 2)
                if more and g == KV - 1:
                    turned_x(b + 1)
                for s in range(NT):
                    if more and g == KV - 2 and s == 2:
                        root(b + 1)
                    if c is not None:
                        past(c, s, 3)
                        exponent(c, s, 1)
                        past(c, s, 2)
                        exponent(c, s, 0)
                    if prepare and s:
                        turned(NT * ua + s - 1, ua, p, s - 1)
                    if prepare:
                        take_products(NT * ua + s, p, s)
                    if c is not None:
                        if s < G - 1:
                            exponent(c, s + 1, 3)
                        past(c, s, 1)
                        if s < G - 1:
                            exponent(c, s + 1, 2)
                    if prepare:
                        gates(NT * ua + s)
                        feature_exps(NT * ua + s, ua, s)
                    if c is not None:
                        out_copy(c, s)
                if prepare:
                    turned(NT * ua + NT - 1, ua, p, NT - 1)
            each_sequence(act, head, unit)

        @block.vector
        def _(dve):
            dve.wait_ge(loaded, ALL_LOADS)
            nc.vector.tensor_copy(ident_b[:], ident[:]).then_inc(masks_cast, 1)
            nc.vector.tensor_scalar(future_b[:], beyond[:], NEG * GATE_NORM, None, ALU.mult).then_inc(masks_cast, 1)

            def statistics(b):
                base = (2 * NT + 1) * b
                dve.wait_ge(x_loaded, 16 * (b + 1))
                for i in range(NT):
                    nc.vector.bn_stats(bn[:, i, :], x_in[:, i, :]).then_inc(stats_step, 1)
                dve.wait_ge(stats_step, base + NT)
                nc.vector.memset(newton[:], 0.0)
                for i in range(NT):
                    nc.vector.bn_aggr(mv[:, i, :], bn[:, i, :]).then_inc(stats_step, 1)
                dve.wait_ge(stats_step, base + 2 * NT)
                nc.vector.tensor_scalar(vpe[:], mv[:, :, 1], EPS, None, ALU.add).then_inc(stats_step, 1)

            def refine(b):
                dve.wait_ge(root_step, 2 * b + 2)
                dve.wait_ge(stats_step, (2 * NT + 1) * (b + 1))
                for r in range(2):
                    n = 8 * b + 4 * r
                    if r:
                        dve.wait_ge(newton_step, n)
                    nc.vector.tensor_tensor(newton[:], rstd[:], rstd[:], ALU.mult).then_inc(newton_step, 1)
                    dve.wait_ge(newton_step, n + 1)
                    nc.vector.tensor_tensor(newton[:], newton[:], vpe[:], ALU.mult).then_inc(newton_step, 1)
                    dve.wait_ge(newton_step, n + 2)
                    nc.vector.tensor_scalar(newton[:], newton[:], -0.5, 1.5, ALU.mult, ALU.add).then_inc(newton_step, 1)
                    dve.wait_ge(newton_step, n + 3)
                    nc.vector.tensor_tensor(rstd[:], rstd[:], newton[:], ALU.mult).then_inc(newton_step, 1)

            def norm(b):
                dve.wait_ge(newton_step, 8 * b + 8)
                dve.wait_ge(rot_ready, KV * NT * b)
                for i in range(NT):
                    if i >= 2:
                        dve.wait_ge(xn_turned, NT * b + i - 1)
                    nc.vector.tensor_scalar(xn[i % 2], x_in[:, i, :], mv[:, i, 0:1], rstd[:, i:i + 1],
                                            ALU.subtract, ALU.mult).then_inc(xn_ready, 1)

            def head():
                statistics(0)
                refine(0)
                norm(0)

            def row_max(c, h, i):
                n, j, w = block_index(c, h, i), NT * h + i, P * (i + 1)
                dve.wait_ge(scores_done, n + 1)
                nc.vector.tensor_reduce(neg_max[:, j:j + 1], score_ps[i % 2][:, 0:w], AX_X, ALU.max,
                                        negate=True).then_inc(max_ready, 1)

            def normalise(c, h, i):
                n, j, w = block_index(c, h, i), NT * h + i, P * (i + 1)
                dve.wait_ge(exp_ready[i % 2], use_index(c, h, i) + 1)
                nc.vector.reciprocal(inv_sum[:, j:j + 1], row_sum[:, j:j + 1]).then_inc(inv_sum_ready, 1)
                dve.wait_ge(inv_sum_ready, n + 1)
                nc.vector.tensor_scalar(prob[:, i % 2, 0:w], prob[:, i % 2, 0:w], inv_sum[:, j:j + 1], None,
                                        ALU.mult).then_inc(prob_ready, 1)

            def diagonal(c, h, i, p):
                dve.wait_ge(prob_turned[i % 2], use_index(c, h, i) + 1)
                dve.wait_ge(attended, G * c + h)
                dve.wait_ge(local_ready, NT * c + i + 1)
                nc.vector.tensor_tensor(prob_t[:, i, i * P:(i + 1) * P], prob_ps[i % 2][:, i * P:(i + 1) * P],
                                        local[p][:, i, h, :], ALU.add).then_inc(diag_ready, 1)

            def feature_max(a):
                dve.wait_ge(qk_ready, a + 1)
                dve.wait_ge(exps_ready, a)
                nc.vector.tensor_reduce(neg_top[:], qk[:].rearrange("p (h d) -> p h d", d=DH), AX_X, ALU.max,
                                        negate=True).then_inc(tops_ready, 1)

            def rope_parts(a, i):
                dve.wait_ge(rot_ready, a)
                halves = qk[:].rearrange("p (h d) -> p h d", d=HALF)
                for r in range(2):
                    ins = nc.vector.tensor_tensor(parts[:, r, :].rearrange("p (h d) -> p h d", d=HALF), halves,
                                                  rope[:, i, r:r + 1, :].to_broadcast([P, 2 * (G + 1), HALF]), ALU.mult)
                ins.then_inc(parts_ready, 1)

            def gate_logs(a):
                dve.wait_ge(logs_step, 3 * a + 3)
                dve.wait_ge(keys_turned, a)
                nc.vector.scalar_tensor_tensor(out=gate[:], in0=qk[:, G * DH:QK], scalar=0.0, in1=logs[:],
                                               op0=ALU.min, op1=ALU.subtract).then_inc(gate_ready, 1)

            def soften(a):
                dve.wait_ge(exps_ready, a + 1)
                nc.vector.reciprocal(inv_tot[:], tot[:]).then_inc(inv_ready, 1)
                dve.wait_ge(inv_ready, a + 1)
                s = soft[:].rearrange("p (h d) -> p h d", d=DH)
                nc.vector.tensor_tensor(s, s, inv_tot[:].unsqueeze(2).to_broadcast([P, G + 1, DH]),
                                        ALU.mult).then_inc(soft_ready, 1)

            def decays(a):
                dve.wait_ge(keys_turned, a + 1)
                dve.wait_ge(kr_t_ready, a)
                dve.wait_ge(span_ready, a)
                nc.vector.tensor_copy(keys[:], tr_ps[0][:]).then_inc(keys_copied, 1)

            def apply_decays(a, ua, i, p):
                dve.wait_ge(decay_ready, a + 1)
                dve.wait_ge(keys_copied, a + 1)
                dve.wait_ge(local_done, a)
                nc.vector.tensor_tensor(k_dec[:], decay[:, 0:NSUB * P].rearrange("p (c s) -> p c s", s=P),
                                        keys[:, P:2 * P].unsqueeze(1).to_broadcast([P, NSUB, P]), ALU.mult).then_inc(k_dec_ready, 1)
                dve.wait_ge(soft_turned, a + 1)
                qs = tr_ps[0][:].rearrange("p (h t) -> p h t", t=P)
                nc.vector.tensor_tensor(q_dec[:], qs, decay[:, NSUB * P:(NSUB + 1) * P].unsqueeze(1)
                                        .to_broadcast([P, G, P]), ALU.mult).then_inc(q_dec_ready, 1)
                dve.wait_ge(span_ready, a + 1)
                if i:
                    nc.vector.tensor_tensor(q_in[p][:, :, (i - 1) * P:i * P], qs, span[:, 0:P].unsqueeze(1)
                                            .to_broadcast([P, G, P]), ALU.mult).then_inc(q_in_ready, 1)
                if i < NT - 1:
                    n = (NT - 1) * ua + i
                    dve.wait_ge(update_done, n + 1)
                    if i:
                        dve.wait_ge(state_ready, n)
                        nc.vector.scalar_tensor_tensor(out=state[p][:, i, :], in0=state[p][:, i - 1, :],
                                                       scalar=span[:, P - 1:P],
                                                       in1=tr_ps[1][:, 0:DH], op0=ALU.mult, op1=ALU.add).then_inc(state_ready, 1)
                    else:
                        nc.vector.tensor_copy(state[p][:, 0, :], tr_ps[1][:, 0:DH]).then_inc(state_ready, 1)

            def keep_local(a, i, p):
                dve.wait_ge(local_done, a + 1)
                nc.vector.scalar_tensor_tensor(out=local[p][:, i, :, :], in0=tr_ps[0][:].rearrange("p (h t) -> p h t", t=P),
                                               scalar=HUGE, in1=keep[:].unsqueeze(1).to_broadcast([P, G, P]),
                                               op0=ALU.min, op1=ALU.mult).then_inc(local_ready, 1)

            def residual(c, b, g, tiles):
                for i in tiles:
                    dve.wait_ge(projected, NT * c + PROJECTION.index(i) + 1)
                    if g:
                        dve.wait_ge(x2_added[i % 2], NT // 2 * c)
                        base = x_acc
                    else:
                        dve.wait_ge(x2_stored, 16 * b)
                        base = x_in
                    nc.vector.scalar_tensor_tensor(out=x_acc[:, i, :], in0=score_ps[i % 2][:], scalar=0.5,
                                                   in1=base[:, i, :], op0=ALU.mult, op1=ALU.add).then_inc(x2_added[i % 2], 1)

            def unit(c, b, g, prepare, more):
                ua, p = (0, 0) if c is None else (c + 1, (g + 1) % 2)
                if prepare and c is not None:
                    dve.wait_ge(attended, G * c)
                if c is not None:
                    row_max(c, 0, 3)
                    row_max(c, 0, 2)
                if more and g == KV - 1:
                    norm(b + 1)
                if c is not None:
                    normalise(c, 0, 3)
                    normalise(c, 0, 2)
                for s in range(NT):
                    if more and g == KV - 2 and s == 2:
                        statistics(b + 1)
                    if more and g == KV - 2 and s == 3:
                        refine(b + 1)
                    if c is not None:
                        diagonal(c, s, 3, g % 2)
                        row_max(c, s, 1)
                        normalise(c, s, 1)
                        diagonal(c, s, 2, g % 2)
                        row_max(c, s, 0)
                        normalise(c, s, 0)
                    if prepare and s:
                        decays(NT * ua + s - 1)
                        apply_decays(NT * ua + s - 1, ua, s - 1, p)
                    if c is not None:
                        if s < G - 1:
                            row_max(c, s + 1, 3)
                            row_max(c, s + 1, 2)
                        diagonal(c, s, 1, g % 2)
                        diagonal(c, s, 0, g % 2)
                    if prepare:
                        feature_max(NT * ua + s)
                    if prepare and s:
                        keep_local(NT * ua + s - 1, s - 1, p)
                    if c is not None and s < G - 1:
                        normalise(c, s + 1, 3)
                        normalise(c, s + 1, 2)
                    if prepare:
                        rope_parts(NT * ua + s, s)
                        gate_logs(NT * ua + s)
                        soften(NT * ua + s)
                if prepare:
                    decays(NT * ua + NT - 1)
                if c is not None:
                    residual(c, b, g, PROJECTION[:2])
                if prepare:
                    apply_decays(NT * ua + NT - 1, ua, NT - 1, p)
                if c is not None:
                    residual(c, b, g, PROJECTION[2:3])
                if prepare:
                    keep_local(NT * ua + NT - 1, NT - 1, p)
                if c is not None:
                    residual(c, b, g, PROJECTION[3:])
            each_sequence(dve, head, unit)

        @block.tensor
        def _(pe):
            pe.wait_ge(loaded, ALL_LOADS)
            pe.wait_ge(masks_cast, 2)

            def turn_x(b):
                pe.wait_ge(local_ready, KV * NT * b)
                pe.wait_ge(qr_t_ready, KV * NT * b)
                for i in range(NT):
                    pe.wait_ge(xn_ready, NT * b + i + 1)
                    if i >= 2:
                        pe.wait_ge(x_t_ready, NT * b + i - 1)
                    for d in range(DC):
                        ins = nc.tensor.transpose(tr_ps[i % 2][:, d * P:(d + 1) * P], xn[i % 2][:, d * P:(d + 1) * P], ident[:])
                    ins.then_inc(xn_turned, 1)

            def head():
                turn_x(0)

            def scores(c, h, i, p):
                k, w = use_index(c, h, i), P * (i + 1)
                pe.wait_ge(exp_ready[i % 2], k)
                pe.wait_ge(x2_added[i % 2], NT // 2 * c)
                nc.tensor.matmul(score_ps[i % 2][:, 0:w], qr_t[p][:, h, i * P:(i + 1) * P], kr_t[p][:, 0:w],
                                 start=True, stop=False)
                nc.tensor.matmul(score_ps[i % 2][:, i * P:w], future_b[:], ident_b[:], start=False,
                                 stop=True).then_inc(scores_done, 1)

            def turn_probs(c, h, i):
                n = block_index(c, h, i)
                pe.wait_ge(prob_ready, n + 1)
                if i == 2:
                    pe.wait_ge(o_t_ready, G * c + h)
                else:
                    pe.wait_ge(past_copied, (NT - 1) * (G * c + h) + max(NT - 2 - i, 0))
                for j in range(i + 1):
                    ins = nc.tensor.transpose(prob_ps[i % 2][:, j * P:(j + 1) * P], prob[:, i % 2, j * P:(j + 1) * P], ident[:])
                ins.then_inc(prob_turned[i % 2], 1)

            def attend(c, h, p):
                pe.wait_ge(past_copied, (NT - 1) * (G * c + h + 1))
                pe.wait_ge(diag_ready, NT * (G * c + h + 1))
                pe.wait_ge(o_t_ready, G * c + h)
                pe.wait_ge(val_ready, NT * (c + 1))
                pe.wait_ge(q_in_ready, (NT - 1) * (c + 1))
                pe.wait_ge(state_ready, (NT - 1) * (c + 1))
                for j in range(NT):
                    nc.tensor.matmul(out_ps[:, j * P:SEQ], val[p][:, j, :], prob_t[:, j, j * P:SEQ],
                                     start=(j == 0), stop=False, skip_group_check=True)
                for i in range(1, NT):
                    ins = nc.tensor.matmul(out_ps[:, i * P:(i + 1) * P], state[p][:, i - 1, :],
                                           q_in[p][:, h, (i - 1) * P:i * P], start=False, stop=(i == NT - 1),
                                           skip_group_check=True)
                ins.then_inc(attended, 1)

            def project_first(c, g, tiles):
                for i in tiles:
                    pe.wait_ge(o_t_ready, G * (c + 1) - 1)
                    pe.wait_ge(exp_ready[i % 2], G * NT // 2 * (c + 1))
                    pe.wait_ge(x2_added[i % 2], NT // 2 * c + i // 2)
                    for h in range(G - 1):
                        nc.tensor.matmul(score_ps[i % 2][:], o_t[:, h, i * P:(i + 1) * P], wo[:, G * g + h, :],
                                         start=(h == 0), stop=False)

            def project_last(c, g, tiles):
                for i in tiles:
                    pe.wait_ge(o_t_ready, G * (c + 1))
                    nc.tensor.matmul(score_ps[i % 2][:], o_t[:, G - 1, i * P:(i + 1) * P], wo[:, G * g + G - 1, :],
                                     start=False, stop=True).then_inc(projected, 1)

            def products(a, ub, i, gn):
                pe.wait_ge(x_t_ready, NT * (ub + 1))
                pe.wait_ge(val_ready, a)
                for d in range(DC):
                    ins = nc.tensor.matmul(qkv_ps[:, 0:G * DH], x_t[:, d, i * P:(i + 1) * P],
                                           wq[:, d, gn * G * DH:(gn + 1) * G * DH], start=(d == 0), stop=(d == DC - 1))
                ins.then_inc(q_done, 1)
                for d in range(DC):
                    ins = nc.tensor.matmul(qkv_ps[:, G * DH:G * DH + 2 * DH], x_t[:, d, i * P:(i + 1) * P],
                                           wkv[:, d, gn, :], start=(d == 0), stop=(d == DC - 1))
                ins.then_inc(kv_done, 1)

            def turn_features(a):
                pe.wait_ge(rot_ready, a + 1)
                pe.wait_ge(soft_ready, a + 1)
                pe.wait_ge(gate_ready, a + 1)
                pe.wait_ge(local_ready, a)
                nc.tensor.transpose(tr_ps[0][:, 0:P], rot[:, G * DH:QK], ident[:])
                nc.tensor.transpose(tr_ps[0][:, P:2 * P], soft[:, G * DH:QK], ident[:])
                nc.tensor.matmul(tr_ps[0][:, 2 * P:3 * P], gate[:], upto[:], start=True, stop=True)
                nc.tensor.matmul(tr_ps[0][:, 3 * P:4 * P], beyond[:], gate[:], start=True, stop=True).then_inc(keys_turned, 1)

            def turn_queries(a, ua, i):
                pe.wait_ge(state_ready, (NT - 1) * ua + min(i, NT - 1))
                pe.wait_ge(qr_t_ready, a)
                for h in range(G):
                    ins = nc.tensor.transpose(tr_ps[1][:, h * P:(h + 1) * P], rot[:, h * P:(h + 1) * P], ident[:])
                ins.then_inc(queries_turned, 1)

            def linear(a, ua, i, p):
                pe.wait_ge(keys_copied, a + 1)
                for h in range(G):
                    ins = nc.tensor.transpose(tr_ps[0][:, h * P:(h + 1) * P], soft[:, h * P:(h + 1) * P], ident[:])
                ins.then_inc(soft_turned, 1)
                if i < NT - 1:
                    pe.wait_ge(qr_t_ready, a + 1)
                    pe.wait_ge(k_rest_ready, (NT - 1) * ua + i + 1)
                    pe.wait_ge(val_ready, a + 1)
                    nc.tensor.matmul(tr_ps[1][:, 0:DH], k_rest[:], val[p][:, i, :], start=True, stop=True).then_inc(update_done, 1)

            def chunk_local(a, ua, i):
                pe.wait_ge(k_dec_ready, a + 1)
                pe.wait_ge(q_dec_ready, a + 1)
                pe.wait_ge(q_in_ready, (NT - 1) * ua + i)
                for s in range(NSUB):
                    m = SUB * (s + 1)
                    ins = nc.tensor.matmul(tr_ps[0][0:m, :].rearrange("p (h t) -> p h t", t=P)[:, :, m - SUB:m],
                                           k_dec[:, s, 0:m], q_dec[:, :, m - SUB:m], start=True, stop=True)
                ins.then_inc(local_done, 1)

            def unit(c, b, g, prepare, more):
                ua, p = (0, 0) if c is None else (c + 1, (g + 1) % 2)
                gn = 0 if c is None else (g + 1) % KV
                ub = 0 if c is None else b + (g + 1) // KV
                if c is not None:
                    pe.wait_ge(kr_t_ready, NT * (c + 1))
                    pe.wait_ge(qr_t_ready, NT * (c + 1))
                if c is not None:
                    scores(c, 0, 3, g % 2)
                    scores(c, 0, 2, g % 2)
                if more and g == KV - 1:
                    turn_x(b + 1)
                for s in range(NT):
                    if prepare and s == 0:
                        products(NT * ua, ub, 0, gn)
                    if c is not None:
                        turn_probs(c, s, 3)
                        scores(c, s, 1, g % 2)
                        turn_probs(c, s, 2)
                        scores(c, s, 0, g % 2)
                    if prepare and s:
                        turn_features(NT * ua + s - 1)
                        turn_queries(NT * ua + s - 1, ua, s - 1)
                        products(NT * ua + s, ub, s, gn)
                        linear(NT * ua + s - 1, ua, s - 1, p)
                    if c is not None:
                        if s < G - 1:
                            scores(c, s + 1, 3, g % 2)
                            scores(c, s + 1, 2, g % 2)
                        turn_probs(c, s, 1)
                        turn_probs(c, s, 0)
                    if prepare and s:
                        chunk_local(NT * ua + s - 1, ua, s - 1)
                    if c is not None:
                        attend(c, s, g % 2)
                if c is not None:
                    project_first(c, g, PROJECTION[:2])
                if prepare:
                    turn_features(NT * ua + NT - 1)
                    turn_queries(NT * ua + NT - 1, ua, NT - 1)
                if c is not None:
                    project_last(c, g, PROJECTION[:2])
                if prepare:
                    linear(NT * ua + NT - 1, ua, NT - 1, p)
                if c is not None:
                    project_first(c, g, PROJECTION[2:3])
                    project_last(c, g, PROJECTION[2:3])
                if prepare:
                    chunk_local(NT * ua + NT - 1, ua, NT - 1)
                if c is not None:
                    project_first(c, g, PROJECTION[3:])
                    project_last(c, g, PROJECTION[3:])
            each_sequence(pe, head, unit)


E_ = 32
GROUPS = 8
TOP_GROUPS = 3
K = 4
FF = 256
FC = FF // P
SH = 512
SC = SH // P
ROUTE_SCALE = 2.5
FAR = 1.0e6
PICKED = -1.0e30


def capacity(tokens):
    return -(-5 * tokens // (4 * E_))


def slot_tiles(cap):
    n = -(-cap // P)
    assert cap % n == 0
    return n, cap // n


def routing_phase(nc, x2, router_w, e_bias, shared_gate, shared_up, shared_down, consts, y, base_dram, slots_dram,
                  weights_dram, tokens_dram):
    B = x2.shape[0]
    T = B * SEQ
    cap = capacity(T)
    ROUTE_STEPS = 56
    GE = E_ // GROUPS
    with ExitStack() as ctx:
        def sb(name, shape, dt=F32):
            return ctx.enter_context(nc.sbuf_tensor("r_" + name, shape, dt))

        def sem(name):
            return ctx.enter_context(nc.semaphore("r_" + name))

        ident = sb("ident", [P, P])
        before = sb("before", [P, P])
        before_b = sb("before_b", [P, P], BF16)
        ones_b = sb("ones_b", [P, P], BF16)
        rw = sb("rw", [E_, DM])
        rw_t = sb("rw_t", [P, DC, E_])
        bias = sb("bias", [P, E_])
        first = sb("first", [P, E_])
        order = sb("order", [P, E_])
        lower = sb("lower", [P, GROUPS, GROUPS])
        token = sb("token", [P, T // P, K])
        no_token = sb("no_token", [E_, cap])
        raw = [sb(f"raw{n}", [P, 4, DM]) for n in range(3)]
        turned_w = [sb(f"w_t{n}", [P, 4, DM]) for n in range(3)]
        sg, su, sd = turned_w
        xb = sb("xb", [P, NT, DM])
        xr = sb("xr", [P, NT, DM])
        sig = sb("sig", [P, 2, SEQ])
        h = sb("h", [P, SC, SEQ])
        yn = sb("yn", [P, NT, DM])
        y_t = sb("y_t", [P, DC, SEQ])
        bn = sb("bn", [P, NT, 6])
        mv = sb("mv", [P, NT, 2])
        vpe = sb("vpe", [P, NT])
        rstd = sb("rstd", [P, NT])
        newton = sb("newton", [P, NT])
        score = sb("score", [P, NT, E_])
        biased = sb("biased", [P, NT, E_])
        hi = sb("hi", [P, NT * GROUPS, 2])
        lo = sb("lo", [P, NT * GROUPS, 2])
        gs = sb("gs", [P, NT, GROUPS])
        g2 = sb("g2", [P, NT * GROUPS])
        g3 = sb("g3", [P, NT * GROUPS])
        beats = sb("beats", [P, NT * GROUPS, GROUPS])
        ties = sb("ties", [P, NT * GROUPS, GROUPS])
        rank = sb("rank", [P, NT * GROUPS])
        v = sb("v", [P, NT, E_])
        cand = sb("cand", [P, NT, E_])
        top = sb("top", [P, NT])
        hot = sb("hot", [P, NT, K, E_])
        picked = sb("picked", [P, NT, E_], BF16)
        seen = sb("seen", [P, E_])
        seen_b = sb("seen_b", [P, NT, E_], BF16)
        over = sb("over", [P, NT, E_])
        slot = sb("slot", [P, NT, E_])
        prod = sb("prod", [P, NT, K, E_])
        wk = sb("wk", [P, NT, K])
        sk = sb("sk", [P, NT, K])
        ok = sb("ok", [P, NT, K])
        token_now = sb("token_now", [P, NT, K])
        sk_i = sb("sk_i", [P, NT, K], I32)
        wsum = sb("wsum", [P, NT])
        tr_ps = [ctx.enter_context(nc.psum_tensor(f"r_tr_ps{n}", [P, 512], F32)) for n in range(2)]
        gate_ps = [ctx.enter_context(nc.psum_tensor(f"r_gate_ps{n}", [P, 512], F32)) for n in range(2)]
        up_ps = [ctx.enter_context(nc.psum_tensor(f"r_up_ps{n}", [P, 512], F32)) for n in range(2)]
        down_ps = gate_ps
        lg_ps = ctx.enter_context(nc.psum_tensor("r_lg_ps", [P, NT, E_], F32))
        pos_ps = ctx.enter_context(nc.psum_tensor("r_pos_ps", [P, NT, E_], F32))

        loaded = sem("loaded")
        table_cleared = sem("table_cleared")
        cast = sem("cast")
        rw_turned = sem("rw_turned")
        rw_ready = sem("rw_ready")
        shared_loaded = sem("shared_loaded")
        w_turned = sem("w_turned")
        w_ready = sem("w_ready")
        x_loaded = sem("x_loaded")
        xr_loaded = sem("xr_loaded")
        gate_done = sem("gate_done")
        up_done = sem("up_done")
        sig_ready = sem("sig_ready")
        h_step = sem("h_step")
        down_done = sem("down_done")
        summed = sem("summed")
        base_stored = sem("base_stored")
        y_stored = sem("y_stored")
        stats_step = sem("stats_step")
        root_step = sem("root_step")
        newton_step = sem("newton_step")
        yn_ready = sem("yn_ready")
        yn_turned = sem("yn_turned")
        y_t_ready = sem("y_t_ready")
        logits_done = sem("logits_done")
        score_ready = sem("score_ready")
        route_step = sem("route_step")
        picks_ready = sem("picks_ready")
        places_done = sem("places_done")
        slots_ready = sem("slots_ready")
        token_copied = sem("token_copied")
        slots_stored = sem("slots_stored")
        scattered = sem("scattered")
        ALL_LOADS = 16 * 9

        def each_sequence(eng, head, sequence):
            if head is not None:
                head(0)
            if B > 1:
                with eng.Fori(0, B - 1) as b:
                    sequence(b, False)
            sequence(B - 1, True)

        block = ctx.enter_context(nc.Block())

        @block.sync
        def _(sp):
            sp.dma_start(xb[:], x2[0].rearrange("(i p) d -> p i d", p=P)).then_inc(x_loaded, 16)
            sp.dma_start(no_token[:], consts["no_token"]).then_inc(loaded, 16)
            for to, name in ((ident, "ident"), (before, "before")):
                sp.dma_start(to[:], consts[name]).then_inc(loaded, 16)
            sp.dma_start(rw[:], router_w).then_inc(loaded, 16)
            sp.dma_start(bias[:], e_bias.partition_broadcast(P)).then_inc(loaded, 16)
            sp.dma_start(first[:], consts["first"].partition_broadcast(P)).then_inc(loaded, 16)
            sp.dma_start(order[:], consts["order"].partition_broadcast(P)).then_inc(loaded, 16)
            sp.dma_start(lower[:], consts["lower"].partition_broadcast(P)).then_inc(loaded, 16)
            sp.dma_start(token[:], consts["token"]).then_inc(loaded, 16)
            for to, w in zip(raw, (shared_gate, shared_up, shared_down)):
                sp.dma_start(to[:], w.rearrange("(r p) n -> p r n", p=P)).then_inc(shared_loaded, 16)
            sp.dma_start(xr[:], x2[0].rearrange("(i p) d -> p i d", p=P)).then_inc(xr_loaded, 16)
            sp.wait_ge(loaded, ALL_LOADS)
            sp.dma_start(tokens_dram.rearrange("(e c) o -> e (c o)", e=E_), no_token[:]).then_inc(table_cleared, 16)

            def sequence(b, last):
                sp.wait_ge(yn_ready, NT * (b + 1))
                if not last:
                    sp.dma_start(xb[:], x2[b + 1].rearrange("(i p) d -> p i d", p=P)).then_inc(x_loaded, 16)
                sp.dma_start(y[b].rearrange("(i p) d -> p i d", p=P), yn[:]).then_inc(y_stored, 16)
                sp.wait_ge(summed, NT * (b + 1))
                sp.dma_start(base_dram[b].rearrange("(i p) d -> p i d", p=P), xr[:]).then_inc(base_stored, 16)
                if not last:
                    sp.wait_ge(base_stored, 16 * (b + 1))
                    sp.dma_start(xr[:], x2[b + 1].rearrange("(i p) d -> p i d", p=P)).then_inc(xr_loaded, 16)
            each_sequence(sp, None, sequence)
            sp.wait_ge(y_stored, 16 * B)
            sp.wait_ge(base_stored, 16 * B)

        @block.gpsimd
        def _(pool):
            pool.wait_ge(loaded, ALL_LOADS)
            pool.wait_ge(table_cleared, 16)
            with pool.Fori(0, B) as b:
                pool.wait_ge(loaded, ALL_LOADS)
                pool.wait_ge(scattered, 16 * NT * K * b)
                nc.gpsimd.tensor_copy(token_now[:], token[:, bass.ts(b, NT), :]).then_inc(token_copied, 1)
                pool.wait_ge(token_copied, b + 1)
                pool.wait_ge(slots_ready, b + 1)
                pool.dma_start(slots_dram[b], sk_i[:].rearrange("p i k -> p (i k)")).then_inc(slots_stored, 16)
                pool.dma_start(weights_dram[b], wk[:].rearrange("p i k -> p (i k)")).then_inc(slots_stored, 16)
                for i in range(NT):
                    for k in range(K):
                        pool.indirect_dma_start(tokens_dram, bass.IndirectOffsetOnAxis(ap=sk_i[:, i, k:k + 1], axis=0),
                                                token_now[:, i, k:k + 1], None, bounds_check=E_ * cap - 1,
                                                oob_is_err=False).then_inc(scattered, 16)
            pool.wait_ge(slots_stored, 32 * B)
            pool.wait_ge(scattered, 16 * NT * K * B)

        @block.scalar
        def _(act):
            act.preload_act_table_set("sigmoid_and_others")
            act.wait_ge(rw_turned, 1)
            nc.scalar.copy(rw_t[:], tr_ps[0][:, 0:DC * E_].rearrange("p (c e) -> p c e", e=E_)).then_inc(rw_ready, 1)
            for n in range(3):
                for q in range(4):
                    m = 4 * n + q
                    act.wait_ge(w_turned, m + 1)
                    nc.scalar.copy(turned_w[n][:, :, q * P:(q + 1) * P], gate_ps[m % 2][:].rearrange("p (c t) -> p c t", c=4)).then_inc(w_ready, 1)

            def root(b):
                act.preload_act_table_set("natural_log_exp_and_others")
                act.wait_ge(stats_step, (2 * NT + 1) * (b + 1))
                nc.scalar.activation(rstd[:], vpe[:], ACT.Ln).then_inc(root_step, 1)
                act.wait_ge(root_step, 2 * b + 1)
                nc.scalar.activation(rstd[:], rstd[:], ACT.Exp, scale=-0.5).then_inc(root_step, 1)
                act.preload_act_table_set("sigmoid_and_others")

            def features(b):
                for i in range(NT):
                    act.wait_ge(yn_turned, NT * b + i + 1)
                    act.wait_ge(up_done, SC * b)
                    nc.scalar.copy(y_t[:, :, i * P:(i + 1) * P],
                                   tr_ps[i % 2][:].rearrange("p (c t) -> p c t", c=DC)).then_inc(y_t_ready, 1)

            def router(b):
                act.wait_ge(logits_done, b + 1)
                act.wait_ge(route_step, ROUTE_STEPS * b)
                nc.scalar.activation(score[:], lg_ps[:], ACT.Sigmoid).then_inc(score_ready, 1)

            def head(b):
                root(b)
                features(b)
                router(b)

            def sequence(b, last):
                for f in range(SC):
                    m = SC * b + f
                    act.wait_ge(gate_done, m + 1)
                    act.wait_ge(h_step, 2 * (SC * b + (f - 1 if f >= 2 else 0)))
                    nc.scalar.activation(sig[:, f % 2, :], gate_ps[f % 2][:], ACT.Sigmoid).then_inc(sig_ready, 1)
                    if f == 1 and not last:
                        root(b + 1)
                if not last:
                    features(b + 1)
                    router(b + 1)
            each_sequence(act, head, sequence)

        @block.tensor
        def _(pe):
            pe.wait_ge(loaded, ALL_LOADS)
            pe.wait_ge(cast, 3)
            for d in range(DC):
                ins = nc.tensor.transpose(tr_ps[0][:, d * E_:(d + 1) * E_], rw[:, d * P:(d + 1) * P], ident[0:E_, 0:E_])
            ins.then_inc(rw_turned, 1)
            pe.wait_ge(rw_ready, 1)
            pe.wait_ge(shared_loaded, 16 * 3)
            for n in range(3):
                for q in range(4):
                    m = 4 * n + q
                    if m >= 2:
                        pe.wait_ge(w_ready, m - 1)
                    for d in range(4):
                        ins = nc.tensor.transpose(gate_ps[m % 2][:, d * P:(d + 1) * P], raw[n][:, q, d * P:(d + 1) * P], ident[:])
                    ins.then_inc(w_turned, 1)
            pe.wait_ge(w_ready, 12)

            def turn(b):
                for i in range(NT):
                    pe.wait_ge(yn_ready, NT * b + i + 1)
                    pe.wait_ge(y_t_ready, NT * b + (i - 1 if i >= 2 else 0))
                    for d in range(DC):
                        ins = nc.tensor.transpose(tr_ps[i % 2][:, d * P:(d + 1) * P], yn[:, i, d * P:(d + 1) * P], ident[:])
                    ins.then_inc(yn_turned, 1)

            def logits(b):
                pe.wait_ge(y_t_ready, NT * (b + 1))
                pe.wait_ge(score_ready, b)
                for i in range(NT):
                    for d in range(DC):
                        ins = nc.tensor.matmul(lg_ps[:, i, :], y_t[:, d, i * P:(i + 1) * P], rw_t[:, d, :],
                                               start=(d == 0), stop=(d == DC - 1))
                ins.then_inc(logits_done, 1)

            def places(b):
                pe.wait_ge(picks_ready, b + 1)
                for i in range(NT):
                    nc.tensor.matmul(pos_ps[:, i, :], before_b[:], picked[:, i, :], start=True, stop=False)
                    ins = nc.tensor.matmul(pos_ps[:, i, :], ones_b[:], seen_b[:, i, :], start=False, stop=True)
                ins.then_inc(places_done, 1)

            def down(b, tiles):
                for i in tiles:
                    pe.wait_ge(h_step, 2 * SC * (b + 1))
                    pe.wait_ge(summed, NT * b + (i - 1 if i >= 2 else 0))
                    for f in range(SC):
                        ins = nc.tensor.matmul(down_ps[i % 2][:], h[:, f, i * P:(i + 1) * P], sd[:, f, :],
                                               start=(f == 0), stop=(f == SC - 1))
                    ins.then_inc(down_done, 1)

            def head(b):
                turn(b)
                logits(b)

            def sequence(b, last):
                for f in range(SC):
                    pe.wait_ge(summed, NT * b)
                    pe.wait_ge(h_step, 2 * (SC * b + (f - 1 if f >= 2 else 0)))
                    for w, ps, done in ((sg, gate_ps, gate_done), (su, up_ps, up_done)):
                        for d in range(DC):
                            ins = nc.tensor.matmul(ps[f % 2][:], w[:, d, f * P:(f + 1) * P], y_t[:, d, :],
                                                   start=(d == 0), stop=(d == DC - 1))
                        ins.then_inc(done, 1)
                if not last:
                    turn(b + 1)
                down(b, (0, 1, 2))
                places(b)
                down(b, (3,))
                if not last:
                    logits(b + 1)
            each_sequence(pe, head, sequence)

        @block.vector
        def _(dve):
            dve.wait_ge(loaded, ALL_LOADS)
            nc.vector.tensor_copy(before_b[:], before[:]).then_inc(cast, 1)
            nc.vector.memset(ones_b[:], 1.0).then_inc(cast, 1)
            nc.vector.memset(seen[:], 0.0).then_inc(cast, 1)
            dve.wait_ge(cast, 3)
            def statistics(b):
                base = (2 * NT + 1) * b
                dve.wait_ge(x_loaded, 16 * (b + 1))
                for i in range(NT):
                    nc.vector.bn_stats(bn[:, i, :], xb[:, i, :]).then_inc(stats_step, 1)
                dve.wait_ge(stats_step, base + NT)
                nc.vector.memset(newton[:], 0.0)
                for i in range(NT):
                    nc.vector.bn_aggr(mv[:, i, :], bn[:, i, :]).then_inc(stats_step, 1)
                dve.wait_ge(stats_step, base + 2 * NT)
                nc.vector.tensor_scalar(vpe[:], mv[:, :, 1], EPS, None, ALU.add).then_inc(stats_step, 1)

            def normalise(b):
                dve.wait_ge(root_step, 2 * b + 2)
                dve.wait_ge(stats_step, (2 * NT + 1) * (b + 1))
                for r in range(2):
                    n = 8 * b + 4 * r
                    dve.wait_ge(newton_step, n)
                    nc.vector.tensor_tensor(newton[:], rstd[:], rstd[:], ALU.mult).then_inc(newton_step, 1)
                    dve.wait_ge(newton_step, n + 1)
                    nc.vector.tensor_tensor(newton[:], newton[:], vpe[:], ALU.mult).then_inc(newton_step, 1)
                    dve.wait_ge(newton_step, n + 2)
                    nc.vector.tensor_scalar(newton[:], newton[:], -0.5, 1.5, ALU.mult, ALU.add).then_inc(newton_step, 1)
                    dve.wait_ge(newton_step, n + 3)
                    nc.vector.tensor_tensor(rstd[:], rstd[:], newton[:], ALU.mult).then_inc(newton_step, 1)
                dve.wait_ge(newton_step, 8 * b + 8)
                dve.wait_ge(y_stored, 16 * b)
                dve.wait_ge(yn_turned, NT * b)
                for i in range(NT):
                    nc.vector.tensor_scalar(yn[:, i, :], xb[:, i, :], mv[:, i, 0:1], rstd[:, i:i + 1],
                                            ALU.subtract, ALU.mult).then_inc(yn_ready, 1)

            now, steps = 0, 0

            def step(ins):
                nonlocal steps
                steps += 1
                ins.then_inc(route_step, 1)
                dve.wait_ge(route_step, ROUTE_STEPS * now + steps)

            def tt(out, a, c, op):
                return nc.vector.tensor_tensor(out, a, c, op)

            def over_experts(t):
                return t.unsqueeze(2).to_broadcast([P, NT, E_])

            def over_tiles(t):
                return t.unsqueeze(1).to_broadcast([P, NT, E_])

            def group_scores(b):
                nonlocal now, steps
                now, steps = b, 0
                dve.wait_ge(score_ready, b + 1)
                step(tt(biased[:], score[:], over_tiles(bias[:]), ALU.add))
                pairs = biased[:].rearrange("p i (g q r) -> p (i g) q r", q=GE // 2, r=2)
                step(tt(hi[:], pairs[:, :, :, 0], pairs[:, :, :, 1], ALU.max))
                step(tt(lo[:], pairs[:, :, :, 0], pairs[:, :, :, 1], ALU.min))
                gsf = gs[:].rearrange("p i g -> p (i g)")
                step(tt(gsf, hi[:, :, 0], hi[:, :, 1], ALU.max))
                step(tt(g2[:], hi[:, :, 0], hi[:, :, 1], ALU.min))
                step(tt(g3[:], lo[:, :, 0], lo[:, :, 1], ALU.max))
                step(tt(g2[:], g2[:], g3[:], ALU.max))
                step(tt(gsf, gsf, g2[:], ALU.add))

            def best_groups(b):
                for i in range(NT):
                    r = slice(i * GROUPS, (i + 1) * GROUPS)
                    other = gs[:, i, :].unsqueeze(1).to_broadcast([P, GROUPS, GROUPS])
                    own = gs[:, i, :].unsqueeze(2).to_broadcast([P, GROUPS, GROUPS])
                    tt(beats[:, r, :], other, own, ALU.is_gt)
                    ins = tt(ties[:, r, :], other, own, ALU.is_equal)
                step(ins)
                for i in range(NT):
                    r = slice(i * GROUPS, (i + 1) * GROUPS)
                    ins = tt(ties[:, r, :], ties[:, r, :], lower[:], ALU.mult)
                step(ins)
                step(tt(beats[:], beats[:], ties[:], ALU.add))
                step(nc.vector.tensor_reduce(rank[:], beats[:], AX_X, ALU.add))
                step(nc.vector.tensor_scalar(rank[:], rank[:], float(TOP_GROUPS), None, ALU.is_lt))
                step(tt(v[:].rearrange("p i (g q) -> p (i g) q", q=GE), biased[:].rearrange("p i (g q) -> p (i g) q", q=GE),
                        rank[:].unsqueeze(2).to_broadcast([P, NT * GROUPS, GE]), ALU.mult))

            def picks(ks):
                for k in ks:
                    step(nc.vector.tensor_reduce(top[:], v[:], AX_X, ALU.max))
                    step(tt(cand[:], v[:], over_experts(top[:]), ALU.is_equal))
                    step(tt(cand[:], cand[:], over_tiles(order[:]), ALU.mult))
                    step(nc.vector.tensor_reduce(top[:], cand[:], AX_X, ALU.max))
                    step(tt(hot[:, :, k, :], cand[:], over_experts(top[:]), ALU.is_equal))
                    step(nc.vector.scalar_tensor_tensor(out=v[:], in0=hot[:, :, k, :], scalar=PICKED, in1=v[:],
                                                        op0=ALU.mult, op1=ALU.add))

            def count_picks(b):
                dve.wait_ge(places_done, b)
                step(nc.vector.tensor_scalar(cand[:], v[:], 0.5 * PICKED, None, ALU.is_lt))
                for i in range(NT):
                    nc.vector.tensor_copy(seen_b[:, i, :], seen[:])
                    step(tt(seen[:], seen[:], cand[:, i, :], ALU.add))
                nc.vector.tensor_copy(picked[:], cand[:]).then_inc(picks_ready, 1)

            def pick_weights(b):
                dve.wait_ge(slots_stored, 32 * b)
                dve.wait_ge(scattered, 16 * NT * K * b)
                step(tt(prod[:], hot[:], score[:].unsqueeze(2).to_broadcast([P, NT, K, E_]), ALU.mult))
                step(nc.vector.tensor_reduce(wk[:], prod[:], AX_X, ALU.add))
                step(nc.vector.tensor_reduce(wsum[:], wk[:], AX_X, ALU.add))
                step(nc.vector.tensor_scalar(wsum[:], wsum[:], 1e-20, None, ALU.add))
                step(nc.vector.reciprocal(wsum[:], wsum[:]))
                step(tt(wk[:], wk[:], wsum[:].unsqueeze(2).to_broadcast([P, NT, K]), ALU.mult))

            def pick_slots(b):
                dve.wait_ge(places_done, b + 1)
                step(nc.vector.tensor_scalar(over[:], pos_ps[:], float(cap), FAR, ALU.is_ge, ALU.mult))
                step(tt(slot[:], pos_ps[:], over_tiles(first[:]), ALU.add))
                step(tt(slot[:], slot[:], over[:], ALU.add))
                step(tt(prod[:], hot[:], slot[:].unsqueeze(2).to_broadcast([P, NT, K, E_]), ALU.mult))
                step(nc.vector.tensor_reduce(sk[:], prod[:], AX_X, ALU.add))
                step(nc.vector.tensor_scalar(ok[:], sk[:], FAR, ROUTE_SCALE, ALU.is_lt, ALU.mult))
                step(tt(wk[:], wk[:], ok[:], ALU.mult))
                nc.vector.tensor_copy(sk_i[:], sk[:]).then_inc(slots_ready, 1)
                assert steps == ROUTE_STEPS, steps

            def silu_product(b, f):
                m = SC * b + f
                dve.wait_ge(sig_ready, m + 1)
                nc.vector.tensor_tensor(sig[:, f % 2, :], sig[:, f % 2, :], gate_ps[f % 2][:], ALU.mult).then_inc(h_step, 1)
                dve.wait_ge(h_step, 2 * m + 1)
                dve.wait_ge(up_done, m + 1)
                dve.wait_ge(down_done, NT * b)
                nc.vector.tensor_tensor(h[:, f, :], sig[:, f % 2, :], up_ps[f % 2][:], ALU.mult).then_inc(h_step, 1)

            def residual(b, i):
                dve.wait_ge(xr_loaded, 16 * (b + 1))
                dve.wait_ge(down_done, NT * b + i + 1)
                nc.vector.tensor_tensor(xr[:, i, :], down_ps[i % 2][:], xr[:, i, :], ALU.add).then_inc(summed, 1)

            def head(b):
                statistics(b)
                normalise(b)

            def sequence(b, last):
                group_scores(b)
                silu_product(b, 0)
                if not last:
                    statistics(b + 1)
                best_groups(b)
                silu_product(b, 1)
                if not last:
                    normalise(b + 1)
                picks((0,))
                silu_product(b, 2)
                picks((1, 2))
                silu_product(b, 3)
                picks((3,))
                count_picks(b)
                residual(b, 0)
                residual(b, 1)
                pick_weights(b)
                residual(b, 2)
                pick_slots(b)
                residual(b, 3)
            each_sequence(dve, head, sequence)


def expert_phase(nc, y, w_gate, w_up, w_down, consts, tokens_dram, y_out):
    T = y.shape[0] * SEQ
    cap = capacity(T)
    n_ct, ct = slot_tiles(cap)
    UNROLL = 4
    ROUNDS = E_ // UNROLL
    yf = y.rearrange("b t d -> (b t) d")
    with ExitStack() as ctx:
        def sb(name, shape, dt=F32):
            return ctx.enter_context(nc.sbuf_tensor("e_" + name, shape, dt))

        def sem(name):
            return ctx.enter_context(nc.semaphore("e_" + name))

        def sems(name, n):
            return [sem(f"{name}{i}") for i in range(n)]

        def banks(name):
            return [ctx.enter_context(nc.psum_tensor(f"e_{name}{n}", [P, 512], F32)) for n in range(2)]

        ident = sb("ident", [P, P])
        spare = sb("spare", [P, 1 + UNROLL])
        who = sb("who", [E_, cap])
        who_i = sb("who_i", [ct, n_ct, E_], I32)
        now = [sb(f"now{n}", [ct, n_ct], I32) for n in range(UNROLL)]
        wg = [sb(f"wg{n}", [P, DC, FF]) for n in range(UNROLL)]
        wu = [sb(f"wu{n}", [P, DC, FF]) for n in range(UNROLL)]
        wd = [sb(f"wd{n}", [P, FC, DM]) for n in range(UNROLL)]
        xg = [[sb(f"xg{n}_{j}", [ct, DM]) for j in range(n_ct)] for n in range(UNROLL)]
        xp_t = [sb(f"xp_t{n}", [P, DC, cap]) for n in range(2)]
        sig = [sb(f"sig{n}", [P, FC, cap]) for n in range(2)]
        h = [sb(f"h{n}", [P, FC, cap]) for n in range(2)]
        yo = [sb(f"yo{n}", [ct, n_ct, DM]) for n in range(UNROLL)]
        tr_ps, gate_ps, up_ps, down_ps = banks("tr_ps"), banks("gate_ps"), banks("up_ps"), banks("down_ps")

        def by_chunk(bank):
            return bank[:, 0:FC * cap].rearrange("p (c t) -> p c t", c=FC)

        loaded = sem("loaded")
        cleared = sem("cleared")
        who_turned = sem("who_turned")
        who_ready = sem("who_ready")
        now_ready = sems("now_ready", UNROLL)
        up_loaded = sems("up_loaded", UNROLL)
        down_loaded = sems("down_loaded", UNROLL)
        gathered = sems("gathered", UNROLL)
        stored = sems("stored", UNROLL)
        turned = sem("turned")
        xp_ready = sem("xp_ready")
        gate_done = sem("gate_done")
        up_done = sem("up_done")
        sig_ready = sem("sig_ready")
        h_step = sem("h_step")
        down_done = sem("down_done")
        yo_ready = sem("yo_ready")

        def before(r, n):
            return (r, n - 1) if n else (r - 1, UNROLL - 1)

        def after(r, n):
            return (r, n + 1) if n < UNROLL - 1 else (r + 1, 0)

        def each_expert(eng, expert):
            def in_round(r, first, last):
                for n in range(UNROLL):
                    expert(r, n, first and n == 0, last and n == UNROLL - 1)
            in_round(0, True, False)
            with eng.Fori(1, ROUNDS - 1) as r:
                in_round(r, False, False)
            in_round(ROUNDS - 1, False, True)

        block = ctx.enter_context(nc.Block())

        @block.sync
        def _(sp):
            sp.dma_start(who[:], tokens_dram.rearrange("(e c) o -> e (c o)", e=E_)).then_inc(loaded, 16)
            sp.dma_start(ident[:], consts["ident"]).then_inc(loaded, 16)

            def load(r, n, first):
                e = UNROLL * r + n
                if not first:
                    sp.wait_ge(up_done, e - UNROLL + 1)
                sp.dma_start(wg[n][:], w_gate[e].rearrange("(c p) i -> p c i", p=P)).then_inc(up_loaded[n], 16)
                sp.dma_start(wu[n][:], w_up[e].rearrange("(c p) i -> p c i", p=P)).then_inc(up_loaded[n], 16)
                if not first:
                    sp.wait_ge(down_done, n_ct * (e - UNROLL + 1))
                sp.dma_start(wd[n][:], w_down[e].rearrange("(c p) d -> p c d", p=P)).then_inc(down_loaded[n], 16)

            for n in range(UNROLL):
                load(0, n, True)
            with sp.Fori(1, ROUNDS) as r:
                for n in range(UNROLL):
                    load(r, n, False)

        @block.gpsimd
        def _(pool):
            for n in range(UNROLL):
                for j in range(n_ct):
                    nc.gpsimd.memset(xg[n][j][:], 0.0)
            nc.gpsimd.memset(spare[:], 0.0).then_inc(cleared, 1)
            pool.wait_ge(cleared, 1)
            pool.wait_ge(who_ready, 1)

            def gather(r, n, first):
                pool.wait_ge(gathered[n], 16 * n_ct * r)
                pool.wait_ge(who_ready, 1)
                nc.gpsimd.tensor_copy(now[n][:], who_i[:, :, bass.ds(UNROLL * r + n, 1)].rearrange("p j e -> p (j e)")).then_inc(now_ready[n], 1)
                pool.wait_ge(now_ready[n], r + 1)
                if not first:
                    pool.wait_ge(turned, n_ct * (UNROLL * (r - 1) + n + 1))
                nc.gpsimd.tensor_tensor(spare[:, 1 + n:2 + n], spare[:, 0:1], spare[:, 0:1], ALU.add)
                for j in range(n_ct):
                    pool.indirect_dma_start(xg[n][j][:], None, yf, bass.IndirectOffsetOnAxis(ap=now[n][:, j:j + 1], axis=0),
                                            bounds_check=T - 1, oob_is_err=False).then_inc(gathered[n], 16)

            for n in range(UNROLL):
                gather(0, n, True)
            with pool.Fori(1, ROUNDS) as r:
                for n in range(UNROLL):
                    gather(r, n, False)

        @block.scalar
        def _(act):
            act.preload_act_table_set("sigmoid_and_others")

            def copy_turned(e, p):
                for j in range(n_ct):
                    act.wait_ge(turned, n_ct * e + j + 1)
                    nc.scalar.copy(xp_t[p][:, :, j * ct:(j + 1) * ct],
                                   tr_ps[j % 2][:, 0:DC * ct].rearrange("p (c t) -> p c t", c=DC)).then_inc(xp_ready, 1)

            def copy_down(r, n):
                e = UNROLL * r + n
                act.wait_ge(stored[n], 16 * r)
                for j in range(n_ct):
                    act.wait_ge(down_done, n_ct * e + j + 1)
                    nc.scalar.copy(yo[n][:, j, :], down_ps[j % 2][0:ct, :]).then_inc(yo_ready, 1)
                act.wait_ge(yo_ready, n_ct * (e + 1))
                act.dma_start(y_out[e].rearrange("(j p) d -> p j d", p=ct), yo[n][:]).then_inc(stored[n], 16)

            def expert(r, n, first, last):
                e = UNROLL * r + n
                act.wait_ge(gate_done, e + 1)
                if not first:
                    act.wait_ge(h_step, 2 * (e - 1))
                nc.scalar.activation(sig[n % 2][:], by_chunk(gate_ps[n % 2]), ACT.Sigmoid).then_inc(sig_ready, 1)
                if not last:
                    copy_turned(e + 1, (n + 1) % 2)
                if not first:
                    copy_down(*before(r, n))

            copy_turned(0, 0)
            each_expert(act, expert)
            copy_down(ROUNDS - 1, UNROLL - 1)
            for n in range(UNROLL):
                act.wait_ge(stored[n], 16 * ROUNDS)

        @block.vector
        def _(dve):
            dve.wait_ge(who_turned, 1)
            nc.vector.tensor_copy(who_i[:], gate_ps[0][0:ct, 0:n_ct * E_].rearrange("p (j e) -> p j e", e=E_)).then_inc(who_ready, 1)
            with dve.Fori(0, E_ // 2) as r:
                for n in range(2):
                    e = 2 * r + n
                    dve.wait_ge(sig_ready, e + 1)
                    nc.vector.tensor_tensor(sig[n][:], sig[n][:], by_chunk(gate_ps[n]), ALU.mult).then_inc(h_step, 1)
                    dve.wait_ge(h_step, 2 * e + 1)
                    dve.wait_ge(up_done, e + 1)
                    dve.wait_ge(down_done, 2 * n_ct * r)
                    nc.vector.tensor_tensor(h[n][:], sig[n][:], by_chunk(up_ps[n]), ALU.mult).then_inc(h_step, 1)

        @block.tensor
        def _(pe):
            pe.wait_ge(loaded, 32)
            for j in range(n_ct):
                ins = nc.tensor.transpose(gate_ps[0][0:ct, j * E_:(j + 1) * E_], who[:, j * ct:(j + 1) * ct], ident[0:E_, 0:E_])
            ins.then_inc(who_turned, 1)
            pe.wait_ge(who_ready, 1)

            def turn(r, n):
                e = UNROLL * r + n
                pe.wait_ge(gathered[n], 16 * n_ct * (r + 1))
                for j in range(n_ct):
                    pe.wait_ge(xp_ready, n_ct * e + max(j - 1, 0))
                    for d in range(DC):
                        ins = nc.tensor.transpose(tr_ps[j % 2][:, d * ct:(d + 1) * ct], xg[n][j][:, d * P:(d + 1) * P],
                                                  ident[0:ct, 0:ct])
                    ins.then_inc(turned, 1)

            def down(r, n):
                e = UNROLL * r + n
                pe.wait_ge(h_step, 2 * (e + 1))
                pe.wait_ge(down_loaded[n], 16 * (r + 1))
                for j in range(n_ct):
                    pe.wait_ge(yo_ready, n_ct * e + max(j - 1, 0))
                    for f in range(FC):
                        ins = nc.tensor.matmul(down_ps[j % 2][0:ct, :], h[n % 2][:, f, j * ct:(j + 1) * ct], wd[n][:, f, :],
                                               start=(f == 0), stop=(f == FC - 1))
                    ins.then_inc(down_done, 1)

            def expert(r, n, first, last):
                e = UNROLL * r + n
                pe.wait_ge(xp_ready, n_ct * (e + 1))
                pe.wait_ge(up_loaded[n], 32 * (r + 1))
                if not first:
                    pe.wait_ge(h_step, 2 * (e - 1))
                for w, ps, done in ((wg, gate_ps, gate_done), (wu, up_ps, up_done)):
                    for f in range(FC):
                        for d in range(DC):
                            ins = nc.tensor.matmul(ps[n % 2][:, f * cap:(f + 1) * cap], w[n][:, d, f * P:(f + 1) * P],
                                                   xp_t[n % 2][:, d, :], start=(d == 0), stop=(d == DC - 1))
                    ins.then_inc(done, 1)
                if not last:
                    turn(*after(r, n))
                if not first:
                    down(*before(r, n))

            turn(0, 0)
            each_expert(pe, expert)
            down(ROUNDS - 1, UNROLL - 1)


def combine_phase(nc, base_dram, consts, slots_dram, weights_dram, y_out, out):
    B = base_dram.shape[0]
    cap = capacity(B * SEQ)
    rows = y_out.rearrange("e c d -> (e c) d")
    with ExitStack() as ctx:
        def sb(name, shape, dt=F32):
            return ctx.enter_context(nc.sbuf_tensor("c_" + name, shape, dt))

        def sem(name):
            return ctx.enter_context(nc.semaphore("c_" + name))

        def sems(name):
            return [sem(f"{name}{i}") for i in range(NT)]

        acc = sb("acc", [P, NT, DM])
        part = sb("part", [P, NT, K, DM])
        spare = sb("spare", [P, 1 + NT])
        all_slots = sb("all_slots", [P, B, NT * K], I32)
        all_weights = sb("all_weights", [P, B, NT * K])
        slots = sb("slots", [P, NT, K], I32)
        wk = sb("wk", [P, NT, K])

        tables_loaded = sem("tables_loaded")
        cleared = sem("cleared")
        base_loaded = sems("base_loaded")
        slots_copied = sems("slots_copied")
        gathered = sems("gathered")
        summed = sems("summed")
        stored = sems("stored")
        block = ctx.enter_context(nc.Block())

        @block.sync
        def _(sp):
            sp.dma_start(all_slots[:], slots_dram.rearrange("b p k -> p b k")).then_inc(tables_loaded, 16)
            sp.dma_start(all_weights[:], weights_dram.rearrange("b p k -> p b k")).then_inc(tables_loaded, 16)
            with sp.Fori(0, B) as b:
                for i in range(NT):
                    sp.wait_ge(stored[i], 16 * b)
                    sp.dma_start(acc[:, i, :], base_dram[b, i * P:(i + 1) * P, :]).then_inc(base_loaded[i], 16)

        @block.gpsimd
        def _(pool):
            nc.gpsimd.memset(part[:], 0.0)
            nc.gpsimd.memset(spare[:], 0.0).then_inc(cleared, 1)
            pool.wait_ge(cleared, 1)
            with pool.Fori(0, B) as b:
                for i in range(NT):
                    pool.wait_ge(gathered[i], 16 * K * b)
                    pool.wait_ge(summed[i], K * b)
                    pool.wait_ge(tables_loaded, 32)
                    nc.gpsimd.tensor_copy(slots[:, i, :], all_slots[:, bass.ds(b, 1), K * i:K * (i + 1)].rearrange("p b k -> p (b k)")).then_inc(slots_copied[i], 1)
                    nc.gpsimd.tensor_copy(wk[:, i, :], all_weights[:, bass.ds(b, 1), K * i:K * (i + 1)].rearrange("p b k -> p (b k)")).then_inc(slots_copied[i], 1)
                    pool.wait_ge(slots_copied[i], 2 * (b + 1))
                    nc.gpsimd.tensor_tensor(spare[:, 1 + i:2 + i], spare[:, 0:1], spare[:, 0:1], ALU.add)
                    for k in range(K):
                        pool.indirect_dma_start(part[:, i, k, :], None, rows, bass.IndirectOffsetOnAxis(ap=slots[:, i, k:k + 1], axis=0),
                                                bounds_check=E_ * cap - 1, oob_is_err=False).then_inc(gathered[i], 16)

        @block.scalar
        def _(act):
            with act.Fori(0, B) as b:
                for i in range(NT):
                    act.wait_ge(summed[i], K * (b + 1))
                    act.dma_start(out[b, i * P:(i + 1) * P, :], acc[:, i, :]).then_inc(stored[i], 16)
            for i in range(NT):
                act.wait_ge(stored[i], 16 * B)

        @block.vector
        def _(dve):
            with dve.Fori(0, B) as b:
                for i in range(NT):
                    dve.wait_ge(base_loaded[i], 16 * (b + 1))
                    dve.wait_ge(slots_copied[i], 2 * (b + 1))
                    dve.wait_ge(gathered[i], 16 * K * (b + 1))
                    for k in range(K):
                        dve.wait_ge(summed[i], K * b + k)
                        nc.vector.scalar_tensor_tensor(out=acc[:, i, :], in0=part[:, i, k, :], scalar=wk[:, i, k:k + 1],
                                                       in1=acc[:, i, :], op0=ALU.mult, op1=ALU.add).then_inc(summed[i], 1)


def host_constants():
    inv = (1.0 / np.float32(ROPE_THETA) ** (np.arange(0, DH, 2, dtype=np.float32) / np.float32(DH))).astype(np.float32)
    ang = (np.arange(SEQ, dtype=np.float32)[:, None] * inv[None, :]).astype(np.float32)
    at = np.arange(P)
    return {
        "rope": np.stack([np.cos(ang), np.sin(ang)], 1).astype(np.float32),
        "ident": np.eye(P, dtype=np.float32),
        "upto": (at[:, None] <= at[None, :]).astype(np.float32) / np.float32(GATE_NORM),
        "beyond": (at[:, None] > at[None, :]).astype(np.float32) / np.float32(GATE_NORM),
        "keep": (at[:, None] <= at[None, :]).astype(np.float32),
    }


def host_constants2(T):
    cap = capacity(T)
    at = np.arange(P)
    c = host_constants()
    c["before"] = (at[:, None] < at[None, :]).astype(np.float32)
    c["first"] = (np.arange(E_) * cap).astype(np.float32)
    c["order"] = (E_ - np.arange(E_)).astype(np.float32)
    g = np.arange(GROUPS)
    c["lower"] = (g[None, :] < g[:, None]).astype(np.float32)
    c["token"] = np.repeat((np.arange(T // P)[None, :] * P + at[:, None])[:, :, None], K, 2).astype(np.float32)
    c["no_token"] = np.full((E_, cap), T, np.float32)
    return c


def block_kernel(nc, a, consts, out):
    x = a["L0_attn_hidden_states"]
    B = x.shape[0]
    cap = capacity(B * SEQ)

    def scratch(name, shape, dt=F32):
        return nc.dram_tensor(name, shape, dt, kind="Internal").ap()

    x2 = scratch("x2", [B, SEQ, DM])
    y = scratch("y", [B, SEQ, DM])
    base = scratch("base", [B, SEQ, DM])
    slots = scratch("slots", [B, P, NT * K], I32)
    weights = scratch("weights", [B, P, NT * K])
    tokens = scratch("tokens", [E_ * cap, 1])
    y_out = scratch("y_out", [E_, cap, DM])
    attention_phase(nc, x, a["L0_attn_Wq"], a["L0_attn_Wk"], a["L0_attn_Wv"], a["L0_attn_Wo"], consts, x2)
    routing_phase(nc, x2, a["L0_ffn_router_w"], a["L0_ffn_e_bias"], a["L0_ffn_shared_gate"], a["L0_ffn_shared_up"],
                  a["L0_ffn_shared_down"], consts, y, base, slots, weights, tokens)
    expert_phase(nc, y, a["L0_ffn_W_gate"], a["L0_ffn_W_up"], a["L0_ffn_W_down"], consts, tokens, y_out)
    combine_phase(nc, base, consts, slots, weights, y_out, out)


_INS = ["L0_attn_hidden_states", "L0_attn_Wq", "L0_attn_Wk", "L0_attn_Wv", "L0_attn_Wo", "L0_ffn_router_w",
        "L0_ffn_e_bias", "L0_ffn_W_gate", "L0_ffn_W_up", "L0_ffn_W_down", "L0_ffn_shared_gate", "L0_ffn_shared_up",
        "L0_ffn_shared_down"]


def kernel(**inputs):
    import concourse.bacc as _bacc
    from concourse.bass_utils import run_bass_kernel_spmd as _run

    nc = _bacc.Bacc("TRN2", target_bir_lowering=False, num_devices=1)
    arrays, ins, consts = {}, {}, {}
    for name in _INS:
        a = np.ascontiguousarray(inputs[name])
        arrays[f"in_{name}_dram"] = a
        ins[name] = nc.dram_tensor(f"in_{name}_dram", a.shape, mybir.dt.from_np(a.dtype), kind="ExternalInput").ap()
    shape = inputs["L0_attn_hidden_states"].shape
    for name, a in host_constants2(shape[0] * shape[1]).items():
        arrays[f"const_{name}_dram"] = a
        consts[name] = nc.dram_tensor(f"const_{name}_dram", a.shape, mybir.dt.from_np(a.dtype), kind="ExternalInput").ap()
    out = nc.dram_tensor("out_0_dram", shape, F32, kind="ExternalOutput").ap()
    block_kernel(nc, ins, consts, out)
    r = _run(nc, [arrays], core_ids=[0])
    return r.results[0]["out_0_dram"]
```

```python
from contextlib import ExitStack

import concourse.bass as bass
import numpy as np
from concourse import mybir

P = 128
F32 = mybir.dt.float32
BF16 = mybir.dt.bfloat16
FP16 = mybir.dt.float16
I32 = mybir.dt.int32
ALU = mybir.AluOpType
ACT = mybir.ActivationFunctionType
AX_X = mybir.AxisListType.X

DM = 512
DC = DM // P
HEADS = 16
KV = 4
G = HEADS // KV
DH = 128
HALF = DH // 2
SEQ = 512
NT = SEQ // P
SUB = 32
NSUB = P // SUB
EPS = 1e-5
GATE_NORM = 16.0
ROPE_THETA = 10000.0
HUGE = 3.0e38
NEG = -1.0e30
THREE = ((0, 0), (0, 1), (1, 0))
X_SCALE = 2.0 ** 10
W_SCALE = 2.0 ** 10
O_SCALE = 2.0 ** 8


def attention_phase(nc, x, w_q, w_k, w_v, w_o, consts, x2):
    B = x.shape[0]
    QK = (G + 1) * DH
    with ExitStack() as ctx:
        def sb(name, shape, dt=F32):
            return ctx.enter_context(nc.sbuf_tensor(name, shape, dt))

        def sem(name):
            return ctx.enter_context(nc.semaphore(name))

        wq = [sb(f"wq_{n}", [P, DC, HEADS * DH], FP16) for n in ("high", "low")]
        wkv = [sb(f"wkv_{n}", [P, DC, KV, 2 * DH], FP16) for n in ("high", "low")]
        wo = [sb(f"wo_{n}", [P, HEADS, DM], FP16) for n in ("high", "low")]
        rope = sb("rope", [P, NT, 2, HALF])
        ident = sb("ident", [P, P])
        upto = sb("upto", [P, P])
        beyond = sb("beyond", [P, P])
        keep = sb("keep", [P, P])
        ident_b = sb("ident_b", [P, P], BF16)
        future_b = sb("future_b", [P, P], BF16)
        qr_t = [sb(f"qr_t{n}", [P, G, SEQ]) for n in range(2)]
        kr_t = [sb(f"kr_t{n}", [P, SEQ]) for n in range(2)]
        val = [sb(f"val{n}", [P, NT, DH]) for n in range(2)]
        q_in = [sb(f"q_in{n}", [P, G, SEQ - P]) for n in range(2)]
        local = [sb(f"local{n}", [P, NT, G, P]) for n in range(2)]
        state = [sb(f"state{n}", [P, NT - 1, DH]) for n in range(2)]
        o_t = [sb(f"o_t_{n}", [P, G, SEQ], FP16) for n in ("high", "low")]
        x_in = sb("x_in", [P, NT, DM])
        x_acc = sb("x_acc", [P, NT, DM])
        x_t = [sb(f"x_t_{n}", [P, DC, SEQ], FP16) for n in ("high", "low")]
        parts = sb("parts", [P, 2, QK])
        xn = [parts[:, n, 0:DM] for n in range(2)]
        qk = sb("qk", [P, QK])
        rot = sb("rot", [P, QK])
        soft = sb("soft", [P, QK])
        neg_top = sb("neg_top", [P, G + 1])
        tot = sb("tot", [P, G + 1])
        inv_tot = sb("inv_tot", [P, G + 1])
        logs = sb("logs", [P, DH])
        gate = sb("gate", [P, DH])
        decay = sb("decay", [P, (NSUB + 1) * P])
        keys = sb("keys", [P, 4 * P])
        span = sb("span", [P, 2 * P])
        k_dec = sb("k_dec", [P, NSUB, P])
        q_dec = sb("q_dec", [P, G, P])
        k_rest = sb("k_rest", [P, DH])
        prob = sb("prob", [P, 2, SEQ])
        prob_t = sb("prob_t", [P, NT, SEQ])
        neg_max = sb("neg_max", [P, G * NT])
        row_sum = sb("row_sum", [P, G * NT])
        inv_sum = sb("inv_sum", [P, G * NT])
        bn = sb("bn", [P, NT, 6])
        mv = sb("mv", [P, NT, 2])
        vpe = sb("vpe", [P, NT])
        rstd = sb("rstd", [P, NT])
        newton = sb("newton", [P, NT])

        qkv_ps = ctx.enter_context(nc.psum_tensor("qkv_ps", [P, 2 * 512], F32))
        tr_ps = [ctx.enter_context(nc.psum_tensor(f"tr_ps{n}", [P, 512], F32)) for n in range(2)]
        score_ps = [ctx.enter_context(nc.psum_tensor(f"score_ps{n}", [P, 512], F32)) for n in range(2)]
        out_ps = ctx.enter_context(nc.psum_tensor("out_ps", [P, 512], F32))
        prob_ps = [out_ps, ctx.enter_context(nc.psum_tensor("prob_ps", [P, 512], F32))]

        loaded = sem("constants_loaded")
        stage_loaded = [sem(f"stage_loaded{n}") for n in range(DC + 2)]
        w_high = sem("w_high")
        w_low = sem("w_low")
        masks_cast = sem("masks_cast")
        x_loaded = sem("x_loaded")
        x2_stored = sem("x2_stored")
        stats_step = sem("stats_step")
        root_step = sem("root_step")
        newton_step = sem("newton_step")
        xn_ready = sem("xn_ready")
        xn_turned = sem("xn_turned")
        x_high_ready = sem("x_high_ready")
        x_t_ready = sem("x_t_ready")
        q_done = sem("q_done")
        kv_done = sem("kv_done")
        tops_ready = sem("tops_ready")
        cosines_ready = sem("cosines_ready")
        sines_ready = sem("sines_ready")
        logs_step = sem("logs_step")
        gate_ready = sem("gate_ready")
        qk_ready = sem("qk_ready")
        val_ready = sem("val_ready")
        exps_ready = sem("exps_ready")
        inv_ready = sem("inv_ready")
        rot_ready = sem("rot_ready")
        soft_ready = sem("soft_ready")
        keys_turned = sem("keys_turned")
        kr_t_ready = sem("kr_t_ready")
        keys_copied = sem("keys_copied")
        span_ready = sem("span_ready")
        diffs_ready = sem("diffs_ready")
        decay_ready = sem("decay_ready")
        queries_turned = sem("queries_turned")
        qr_t_ready = sem("qr_t_ready")
        soft_turned = sem("soft_turned")
        k_dec_ready = sem("k_dec_ready")
        q_dec_ready = sem("q_dec_ready")
        q_in_ready = sem("q_in_ready")
        k_rest_ready = sem("k_rest_ready")
        update_done = sem("update_done")
        state_ready = sem("state_ready")
        local_done = sem("local_done")
        local_ready = sem("local_ready")
        scores_done = sem("scores_done")
        max_ready = sem("max_ready")
        exp_ready = [sem(f"exp_ready{n}") for n in range(2)]
        inv_sum_ready = sem("inv_sum_ready")
        prob_ready = sem("prob_ready")
        prob_turned = [sem(f"prob_turned{n}") for n in range(2)]
        past_copied = sem("past_copied")
        diag_ready = sem("diag_ready")
        attended = sem("attended")
        o_high_ready = sem("o_high_ready")
        o_t_ready = sem("o_t_ready")
        projected = sem("projected")
        x2_added = [sem(f"x2_added{n}") for n in range(2)]

        PROJECTION = (0, 1, 3, 2)
        ALL_LOADS = 16 * 5

        def flat(t):
            return t.rearrange("p a b c -> p (a b c)") if len(t.shape) == 4 else t.rearrange("p a b -> p (a b)")

        stage = [flat(t[:]) for t in (local[0], local[1], prob_t, x_acc, qr_t[1], qr_t[0])]
        wo_stage = stage[1:5]
        STAGES = len(stage)

        def weight_parts(n):
            if n < DC:
                return stage[n], [w[:, n, :] for w in wq]
            if n < STAGES:
                m = n - DC
                return (stage[n].rearrange("p (c g d) -> p c g d", g=KV, d=DH), [w[:, :, :, m * DH:(m + 1) * DH] for w in wkv])
            m = n - STAGES
            return wo_stage[m], [w[:, G * m:G * (m + 1), :].rearrange("p h d -> p (h d)") for w in wo]

        def each_sequence(eng, head, unit):
            head()
            unit(None, 0, 0, True, False)

            def sequence(b, last):
                for g in range(KV):
                    unit(KV * b + g, b, g, not (g == KV - 1 and last), not last)
            if B > 1:
                with eng.Fori(0, B - 1) as b:
                    sequence(b, False)
            sequence(B - 1, True)

        def block_index(c, h, i):
            return G * NT * c + NT * h + NT - 1 - i

        def use_index(c, h, i):
            return G * NT // 2 * c + NT // 2 * h + (NT - 1 - i) // 2

        block = ctx.enter_context(nc.Block())

        @block.sync
        def _(sp):
            sp.dma_start(x_in[:], x[0].rearrange("(i p) d -> p i d", p=P)).then_inc(x_loaded, 16)
            sp.dma_start(rope[:], consts["rope"].rearrange("(i p) a d -> p i a d", p=P)).then_inc(loaded, 16)
            for to, name in ((ident, "ident"), (upto, "upto"), (beyond, "beyond"), (keep, "keep")):
                sp.dma_start(to[:], consts[name]).then_inc(loaded, 16)
            for n in range(DC):
                sp.dma_start(stage[n], w_q[n * P:(n + 1) * P, :]).then_inc(stage_loaded[n], 16)
            for n, w in ((DC, w_k), (DC + 1, w_v)):
                sp.dma_start(stage[n].rearrange("p (c n) -> p c n", c=DC), w.rearrange("(c p) n -> p c n", p=P)).then_inc(stage_loaded[n], 16)
            for n in range(DC):
                sp.wait_ge(w_low, min(n + 2, DC + 1))
                sp.dma_start(wo_stage[n].rearrange("p (h n) -> p h n", h=G),
                             w_o[n * G * DH:(n + 1) * G * DH, :].rearrange("(h p) n -> p h n", p=P)).then_inc(stage_loaded[n + 1], 16)
            if B > 1:
                with sp.Fori(0, B - 1) as b:
                    for n in range(2):
                        sp.wait_ge(x2_added[n], KV * (NT // 2) * b + NT // 2)
                    sp.dma_start(x_in[:], x[b + 1].rearrange("(i p) d -> p i d", p=P)).then_inc(x_loaded, 16)
                    for n in range(2):
                        sp.wait_ge(x2_added[n], KV * (NT // 2) * (b + 1))
                    sp.dma_start(x2[b].rearrange("(i p) d -> p i d", p=P), x_acc[:]).then_inc(x2_stored, 16)
            for n in range(2):
                sp.wait_ge(x2_added[n], KV * (NT // 2) * B)
            sp.dma_start(x2[B - 1].rearrange("(i p) d -> p i d", p=P), x_acc[:]).then_inc(x2_stored, 16)
            sp.wait_ge(x2_stored, 16 * B)

        @block.gpsimd
        def _(pool):
            pool.wait_ge(loaded, ALL_LOADS)

            def rope_sines(a, i):
                pool.wait_ge(qk_ready, a + 1)
                pool.wait_ge(rot_ready, a)
                nc.gpsimd.tensor_tensor(parts[:, 1, :].rearrange("p (h d) -> p h d", d=HALF),
                                        qk[:].rearrange("p (h d) -> p h d", d=HALF),
                                        rope[:, i, 1:2, :].to_broadcast([P, 2 * (G + 1), HALF]), ALU.mult).then_inc(sines_ready, 1)

            def rotate(a):
                pool.wait_ge(cosines_ready, a + 1)
                pool.wait_ge(sines_ready, a + 1)
                pool.wait_ge(keys_turned, a)
                pool.wait_ge(queries_turned, a)
                xc = parts[:, 0, :].rearrange("p (h s d) -> p h s d", s=2, d=HALF)
                xs = parts[:, 1, :].rearrange("p (h s d) -> p h s d", s=2, d=HALF)
                r = rot[:].rearrange("p (h s d) -> p h s d", s=2, d=HALF)
                nc.gpsimd.tensor_tensor(r[:, :, 0, :], xc[:, :, 0, :], xs[:, :, 1, :], ALU.subtract)
                nc.gpsimd.tensor_tensor(r[:, :, 1, :], xc[:, :, 1, :], xs[:, :, 0, :], ALU.add).then_inc(rot_ready, 1)

            def differences(a):
                pool.wait_ge(keys_copied, a + 1)
                pool.wait_ge(q_dec_ready, a)
                run = keys[:, 2 * P:3 * P]
                runs = run.rearrange("p (c s) -> p c s", s=SUB)
                mid = runs[:, :, SUB // 2 - 1:SUB // 2]
                nc.gpsimd.tensor_tensor(decay[:, 0:NSUB * P].rearrange("p (c s) -> p c s", s=P),
                                        mid.to_broadcast([P, NSUB, P]),
                                        run.unsqueeze(1).to_broadcast([P, NSUB, P]), ALU.subtract)
                nc.gpsimd.tensor_tensor(decay[:, NSUB * P:(NSUB + 1) * P].rearrange("p (c s) -> p c s", s=SUB),
                                        runs, mid.to_broadcast([P, NSUB, SUB]), ALU.subtract).then_inc(diffs_ready, 1)

            def scaled_keys(a, p, i):
                nc.gpsimd.tensor_scalar(kr_t[p][:, i * P:(i + 1) * P], keys[:, 0:P], float(DH) ** -0.5, None,
                                        ALU.mult).then_inc(kr_t_ready, 1)

            def key_rest(ua, i):
                a, n = NT * ua + i, (NT - 1) * ua + i
                pool.wait_ge(span_ready, a + 1)
                pool.wait_ge(update_done, n)
                pool.wait_ge(soft_ready, a + 1)
                nc.gpsimd.tensor_tensor(k_rest[:], span[:, P:2 * P], soft[:, G * DH:QK], ALU.mult).then_inc(k_rest_ready, 1)

            def unit(c, b, g, prepare, more):
                ua, p = (0, 0) if c is None else (c + 1, (g + 1) % 2)
                if prepare and c is not None:
                    pool.wait_ge(attended, G * c)
                for s in range(NT):
                    if prepare and s:
                        differences(NT * ua + s - 1)
                        key_rest(ua, s - 1)
                        scaled_keys(NT * ua + s - 1, p, s - 1)
                    if prepare:
                        if s == 0 and (c is None or more and g == KV - 1):
                            pool.wait_ge(xn_turned, NT if c is None else NT * (b + 2))
                        rope_sines(NT * ua + s, s)
                        rotate(NT * ua + s)
                if prepare:
                    differences(NT * ua + NT - 1)
                    scaled_keys(NT * ua + NT - 1, p, NT - 1)
            each_sequence(pool, lambda: None, unit)

        @block.scalar
        def _(act):
            act.preload_act_table_set("natural_log_exp_and_others")

            def split_high(n):
                if n < STAGES:
                    act.wait_ge(stage_loaded[n], 16)
                else:
                    act.wait_ge(stage_loaded[n - STAGES + 1], 32)
                whole, (high, low) = weight_parts(n)
                nc.scalar.activation(high, whole, ACT.Copy, scale=W_SCALE).then_inc(w_high, 1)

            def root(b):
                act.wait_ge(stats_step, (2 * NT + 1) * (b + 1))
                nc.scalar.activation(rstd[:], vpe[:], ACT.Ln).then_inc(root_step, 1)
                act.wait_ge(root_step, 2 * b + 1)
                nc.scalar.activation(rstd[:], rstd[:], ACT.Exp, scale=-0.5).then_inc(root_step, 1)

            def turned_x(b):
                act.wait_ge(kv_done, KV * NT * b)
                for i in range(NT):
                    act.wait_ge(xn_turned, NT * b + i + 1)
                    nc.scalar.activation(x_t[0][:, :, i * P:(i + 1) * P], tr_ps[i % 2][:].rearrange("p (c t) -> p c t", c=DC),
                                         ACT.Copy, scale=X_SCALE).then_inc(x_high_ready, 1)

            def head():
                root(0)
                turned_x(0)
                for n in range(STAGES):
                    split_high(n)
                act.wait_ge(w_low, STAGES)

            def exponent(c, h, i):
                n, k, j, w = block_index(c, h, i), use_index(c, h, i), NT * h + i, P * (i + 1)
                act.wait_ge(max_ready, n + 1)
                act.wait_ge(prob_turned[i % 2], k)
                nc.scalar.activation(prob[:, i % 2, 0:w], score_ps[i % 2][:, 0:w], ACT.Exp, bias=neg_max[:, j:j + 1],
                                     accum_out=row_sum[:, j:j + 1]).then_inc(exp_ready[i % 2], 1)

            def past(c, h, i):
                act.wait_ge(diag_ready, block_index(c, h, i) + 1)
                act.wait_ge(attended, G * c + h)
                nc.scalar.copy(prob_t[:, 0:i, i * P:(i + 1) * P],
                               prob_ps[i % 2][:, 0:i * P].rearrange("p (j t) -> p j t", t=P)).then_inc(past_copied, 1)

            def out_copy(c, h):
                act.wait_ge(attended, G * c + h + 1)
                act.wait_ge(projected, NT * c)
                nc.scalar.activation(o_t[0][:, h, :], out_ps[:], ACT.Copy, scale=O_SCALE).then_inc(o_high_ready, 1)

            def take_products(a, p, i):
                act.wait_ge(q_done, a + 1)
                act.wait_ge(kv_done, a + 1)
                act.wait_ge(cosines_ready, a)
                act.wait_ge(sines_ready, a)
                act.wait_ge(gate_ready, a)
                back = 1.0 / (X_SCALE * W_SCALE)
                nc.scalar.activation(qk[:], qkv_ps[:, 0:QK], ACT.Copy, scale=back).then_inc(qk_ready, 1)
                nc.scalar.activation(val[p][:, i, :], qkv_ps[:, QK:QK + DH], ACT.Copy, scale=back).then_inc(val_ready, 1)
                act.wait_ge(qk_ready, a + 1)
                nc.scalar.activation(logs[:], qk[:, G * DH:QK], ACT.Abs).then_inc(logs_step, 1)

            def gates(a):
                act.wait_ge(logs_step, 3 * a + 1)
                nc.scalar.activation(logs[:], logs[:], ACT.Exp, scale=-1.0).then_inc(logs_step, 1)
                act.wait_ge(logs_step, 3 * a + 2)
                nc.scalar.activation(logs[:], logs[:], ACT.Ln, bias=1.0).then_inc(logs_step, 1)

            def feature_exps(a, ua, i):
                act.wait_ge(tops_ready, a + 1)
                act.wait_ge(soft_turned, a)
                act.wait_ge(k_rest_ready, (NT - 1) * ua + min(i, NT - 1))
                for h in range(G + 1):
                    ins = nc.scalar.activation(soft[:, h * DH:(h + 1) * DH], qk[:, h * DH:(h + 1) * DH], ACT.Exp,
                                               bias=neg_top[:, h:h + 1], accum_out=tot[:, h:h + 1])
                ins.then_inc(exps_ready, 1)

            def turned(a, ua, p, i):
                act.wait_ge(keys_copied, a + 1)
                act.wait_ge(k_rest_ready, (NT - 1) * ua + i)
                act.wait_ge(q_in_ready, (NT - 1) * ua + max(i - 1, 0))
                act.wait_ge(state_ready, (NT - 1) * ua + i)
                nc.scalar.activation(span[:], keys[:, 2 * P:4 * P], ACT.Exp).then_inc(span_ready, 1)
                act.wait_ge(queries_turned, a + 1)
                nc.scalar.copy(qr_t[p][:, :, i * P:(i + 1) * P],
                               tr_ps[1][:].rearrange("p (h t) -> p h t", t=P)).then_inc(qr_t_ready, 1)
                act.wait_ge(diffs_ready, a + 1)
                nc.scalar.activation(decay[:], decay[:], ACT.Exp).then_inc(decay_ready, 1)

            def unit(c, b, g, prepare, more):
                ua, p = (0, 0) if c is None else (c + 1, (g + 1) % 2)
                if prepare and c is not None:
                    act.wait_ge(attended, G * c)
                if c is not None:
                    exponent(c, 0, 3)
                    exponent(c, 0, 2)
                if more and g == KV - 1:
                    turned_x(b + 1)
                for s in range(NT):
                    if more and g == KV - 2 and s == 2:
                        root(b + 1)
                    if c is not None:
                        past(c, s, 3)
                        exponent(c, s, 1)
                        past(c, s, 2)
                        exponent(c, s, 0)
                    if prepare and s:
                        turned(NT * ua + s - 1, ua, p, s - 1)
                    if prepare:
                        take_products(NT * ua + s, p, s)
                    if c is not None:
                        if s < G - 1:
                            exponent(c, s + 1, 3)
                        past(c, s, 1)
                        if s < G - 1:
                            exponent(c, s + 1, 2)
                    if prepare:
                        gates(NT * ua + s)
                        feature_exps(NT * ua + s, ua, s)
                    if c is not None:
                        out_copy(c, s)
                    else:
                        split_high(STAGES + s)
                if prepare:
                    turned(NT * ua + NT - 1, ua, p, NT - 1)
                if c is None:
                    act.wait_ge(w_low, STAGES + DC)
            each_sequence(act, head, unit)

        @block.vector
        def _(dve):
            dve.wait_ge(loaded, ALL_LOADS)
            nc.vector.tensor_copy(ident_b[:], ident[:]).then_inc(masks_cast, 1)
            nc.vector.tensor_scalar(future_b[:], beyond[:], NEG * GATE_NORM, None, ALU.mult).then_inc(masks_cast, 1)

            def split_low(n):
                dve.wait_ge(w_high, n + 1)
                whole, (high, low) = weight_parts(n)
                nc.vector.scalar_tensor_tensor(out=low, in0=whole, scalar=W_SCALE, in1=high, op0=ALU.mult,
                                               op1=ALU.subtract).then_inc(w_low, 1)

            def statistics(b):
                base = (2 * NT + 1) * b
                dve.wait_ge(x_loaded, 16 * (b + 1))
                for i in range(NT):
                    nc.vector.bn_stats(bn[:, i, :], x_in[:, i, :]).then_inc(stats_step, 1)
                dve.wait_ge(stats_step, base + NT)
                nc.vector.memset(newton[:], 0.0)
                for i in range(NT):
                    nc.vector.bn_aggr(mv[:, i, :], bn[:, i, :]).then_inc(stats_step, 1)
                dve.wait_ge(stats_step, base + 2 * NT)
                nc.vector.tensor_scalar(vpe[:], mv[:, :, 1], EPS, None, ALU.add).then_inc(stats_step, 1)

            def refine(b):
                dve.wait_ge(root_step, 2 * b + 2)
                dve.wait_ge(stats_step, (2 * NT + 1) * (b + 1))
                for r in range(2):
                    n = 8 * b + 4 * r
                    if r:
                        dve.wait_ge(newton_step, n)
                    nc.vector.tensor_tensor(newton[:], rstd[:], rstd[:], ALU.mult).then_inc(newton_step, 1)
                    dve.wait_ge(newton_step, n + 1)
                    nc.vector.tensor_tensor(newton[:], newton[:], vpe[:], ALU.mult).then_inc(newton_step, 1)
                    dve.wait_ge(newton_step, n + 2)
                    nc.vector.tensor_scalar(newton[:], newton[:], -0.5, 1.5, ALU.mult, ALU.add).then_inc(newton_step, 1)
                    dve.wait_ge(newton_step, n + 3)
                    nc.vector.tensor_tensor(rstd[:], rstd[:], newton[:], ALU.mult).then_inc(newton_step, 1)

            def norm(b):
                dve.wait_ge(newton_step, 8 * b + 8)
                dve.wait_ge(rot_ready, KV * NT * b)
                for i in range(NT):
                    nc.vector.tensor_scalar(xn[i % 2], x_in[:, i, :], mv[:, i, 0:1], rstd[:, i:i + 1],
                                            ALU.subtract, ALU.mult).then_inc(xn_ready, 1)
                    if i:
                        x_low(b, i - 1)
                x_low(b, NT - 1)

            def x_low(b, i):
                dve.wait_ge(x_high_ready, NT * b + i + 1)
                nc.vector.scalar_tensor_tensor(out=x_t[1][:, :, i * P:(i + 1) * P],
                                               in0=tr_ps[i % 2][:].rearrange("p (c t) -> p c t", c=DC), scalar=X_SCALE,
                                               in1=x_t[0][:, :, i * P:(i + 1) * P], op0=ALU.mult,
                                               op1=ALU.subtract).then_inc(x_t_ready, 1)

            def head():
                statistics(0)
                refine(0)
                norm(0)
                for n in range(STAGES):
                    split_low(n)

            def row_max(c, h, i):
                n, j, w = block_index(c, h, i), NT * h + i, P * (i + 1)
                dve.wait_ge(scores_done, n + 1)
                nc.vector.tensor_reduce(neg_max[:, j:j + 1], score_ps[i % 2][:, 0:w], AX_X, ALU.max,
                                        negate=True).then_inc(max_ready, 1)

            def normalise(c, h, i):
                n, j, w = block_index(c, h, i), NT * h + i, P * (i + 1)
                dve.wait_ge(exp_ready[i % 2], use_index(c, h, i) + 1)
                nc.vector.reciprocal(inv_sum[:, j:j + 1], row_sum[:, j:j + 1]).then_inc(inv_sum_ready, 1)
                dve.wait_ge(inv_sum_ready, n + 1)
                nc.vector.tensor_scalar(prob[:, i % 2, 0:w], prob[:, i % 2, 0:w], inv_sum[:, j:j + 1], None,
                                        ALU.mult).then_inc(prob_ready, 1)

            def diagonal(c, h, i, p):
                dve.wait_ge(prob_turned[i % 2], use_index(c, h, i) + 1)
                dve.wait_ge(attended, G * c + h)
                dve.wait_ge(local_ready, NT * c + i + 1)
                nc.vector.tensor_tensor(prob_t[:, i, i * P:(i + 1) * P], prob_ps[i % 2][:, i * P:(i + 1) * P],
                                        local[p][:, i, h, :], ALU.add).then_inc(diag_ready, 1)

            def feature_max(a):
                dve.wait_ge(qk_ready, a + 1)
                dve.wait_ge(exps_ready, a)
                nc.vector.tensor_reduce(neg_top[:], qk[:].rearrange("p (h d) -> p h d", d=DH), AX_X, ALU.max,
                                        negate=True).then_inc(tops_ready, 1)

            def rope_cosines(a, i):
                dve.wait_ge(rot_ready, a)
                halves = qk[:].rearrange("p (h d) -> p h d", d=HALF)
                nc.vector.tensor_tensor(parts[:, 0, :].rearrange("p (h d) -> p h d", d=HALF), halves,
                                        rope[:, i, 0:1, :].to_broadcast([P, 2 * (G + 1), HALF]), ALU.mult).then_inc(cosines_ready, 1)

            def gate_logs(a):
                dve.wait_ge(logs_step, 3 * a + 3)
                dve.wait_ge(keys_turned, a)
                nc.vector.scalar_tensor_tensor(out=gate[:], in0=qk[:, G * DH:QK], scalar=0.0, in1=logs[:],
                                               op0=ALU.min, op1=ALU.subtract).then_inc(gate_ready, 1)

            def soften(a):
                dve.wait_ge(exps_ready, a + 1)
                nc.vector.reciprocal(inv_tot[:], tot[:]).then_inc(inv_ready, 1)
                dve.wait_ge(inv_ready, a + 1)
                s = soft[:].rearrange("p (h d) -> p h d", d=DH)
                nc.vector.tensor_tensor(s, s, inv_tot[:].unsqueeze(2).to_broadcast([P, G + 1, DH]),
                                        ALU.mult).then_inc(soft_ready, 1)

            def decays(a):
                dve.wait_ge(keys_turned, a + 1)
                dve.wait_ge(kr_t_ready, a)
                dve.wait_ge(span_ready, a)
                nc.vector.tensor_copy(keys[:], tr_ps[0][:]).then_inc(keys_copied, 1)

            def apply_decays(a, ua, i, p):
                dve.wait_ge(decay_ready, a + 1)
                dve.wait_ge(keys_copied, a + 1)
                dve.wait_ge(local_done, a)
                nc.vector.tensor_tensor(k_dec[:], decay[:, 0:NSUB * P].rearrange("p (c s) -> p c s", s=P),
                                        keys[:, P:2 * P].unsqueeze(1).to_broadcast([P, NSUB, P]), ALU.mult).then_inc(k_dec_ready, 1)
                dve.wait_ge(soft_turned, a + 1)
                qs = tr_ps[0][:].rearrange("p (h t) -> p h t", t=P)
                nc.vector.tensor_tensor(q_dec[:], qs, decay[:, NSUB * P:(NSUB + 1) * P].unsqueeze(1)
                                        .to_broadcast([P, G, P]), ALU.mult).then_inc(q_dec_ready, 1)
                dve.wait_ge(span_ready, a + 1)
                if i:
                    nc.vector.tensor_tensor(q_in[p][:, :, (i - 1) * P:i * P], qs, span[:, 0:P].unsqueeze(1)
                                            .to_broadcast([P, G, P]), ALU.mult).then_inc(q_in_ready, 1)
                if i < NT - 1:
                    n = (NT - 1) * ua + i
                    dve.wait_ge(update_done, n + 1)
                    if i:
                        dve.wait_ge(state_ready, n)
                        nc.vector.scalar_tensor_tensor(out=state[p][:, i, :], in0=state[p][:, i - 1, :],
                                                       scalar=span[:, P - 1:P],
                                                       in1=tr_ps[1][:, 0:DH], op0=ALU.mult, op1=ALU.add).then_inc(state_ready, 1)
                    else:
                        nc.vector.tensor_copy(state[p][:, 0, :], tr_ps[1][:, 0:DH]).then_inc(state_ready, 1)

            def keep_local(a, i, p):
                dve.wait_ge(local_done, a + 1)
                nc.vector.scalar_tensor_tensor(out=local[p][:, i, :, :], in0=tr_ps[0][:].rearrange("p (h t) -> p h t", t=P),
                                               scalar=HUGE, in1=keep[:].unsqueeze(1).to_broadcast([P, G, P]),
                                               op0=ALU.min, op1=ALU.mult).then_inc(local_ready, 1)

            def out_low(c, h):
                dve.wait_ge(o_high_ready, G * c + h + 1)
                nc.vector.scalar_tensor_tensor(out=o_t[1][:, h, :], in0=out_ps[:], scalar=O_SCALE, in1=o_t[0][:, h, :],
                                               op0=ALU.mult, op1=ALU.subtract).then_inc(o_t_ready, 1)

            def residual(c, b, g, tiles):
                for i in tiles:
                    dve.wait_ge(projected, NT * c + PROJECTION.index(i) + 1)
                    if g:
                        dve.wait_ge(x2_added[i % 2], NT // 2 * c)
                        base = x_acc
                    else:
                        dve.wait_ge(x2_stored, 16 * b)
                        base = x_in
                    nc.vector.scalar_tensor_tensor(out=x_acc[:, i, :], in0=score_ps[i % 2][:], scalar=0.5 / (O_SCALE * W_SCALE),
                                                   in1=base[:, i, :], op0=ALU.mult, op1=ALU.add).then_inc(x2_added[i % 2], 1)

            def unit(c, b, g, prepare, more):
                ua, p = (0, 0) if c is None else (c + 1, (g + 1) % 2)
                if prepare and c is not None:
                    dve.wait_ge(attended, G * c)
                if c is not None:
                    row_max(c, 0, 3)
                    row_max(c, 0, 2)
                if more and g == KV - 1:
                    norm(b + 1)
                if c is not None:
                    normalise(c, 0, 3)
                    normalise(c, 0, 2)
                for s in range(NT):
                    if more and g == KV - 2 and s == 2:
                        statistics(b + 1)
                    if more and g == KV - 2 and s == 3:
                        refine(b + 1)
                    if c is not None:
                        diagonal(c, s, 3, g % 2)
                        if s:
                            out_low(c, s - 1)
                        row_max(c, s, 1)
                        normalise(c, s, 1)
                        diagonal(c, s, 2, g % 2)
                        row_max(c, s, 0)
                        normalise(c, s, 0)
                    if prepare and s:
                        decays(NT * ua + s - 1)
                        apply_decays(NT * ua + s - 1, ua, s - 1, p)
                    if c is not None:
                        if s < G - 1:
                            row_max(c, s + 1, 3)
                            row_max(c, s + 1, 2)
                        diagonal(c, s, 1, g % 2)
                        diagonal(c, s, 0, g % 2)
                    if prepare:
                        feature_max(NT * ua + s)
                        rope_cosines(NT * ua + s, s)
                    if prepare and s:
                        keep_local(NT * ua + s - 1, s - 1, p)
                    if c is not None and s < G - 1:
                        normalise(c, s + 1, 3)
                        normalise(c, s + 1, 2)
                    if prepare:
                        gate_logs(NT * ua + s)
                        soften(NT * ua + s)
                    if c is None:
                        split_low(STAGES + s)
                if c is not None:
                    out_low(c, G - 1)
                if prepare:
                    decays(NT * ua + NT - 1)
                if c is not None:
                    residual(c, b, g, PROJECTION[:2])
                if prepare:
                    apply_decays(NT * ua + NT - 1, ua, NT - 1, p)
                if c is not None:
                    residual(c, b, g, PROJECTION[2:3])
                if prepare:
                    keep_local(NT * ua + NT - 1, NT - 1, p)
                if c is not None:
                    residual(c, b, g, PROJECTION[3:])
            each_sequence(dve, head, unit)

        @block.tensor
        def _(pe):
            pe.wait_ge(loaded, ALL_LOADS)
            pe.wait_ge(masks_cast, 2)

            def turn_x(b):
                pe.wait_ge(local_ready, KV * NT * b)
                pe.wait_ge(qr_t_ready, KV * NT * b)
                for i in range(NT):
                    pe.wait_ge(xn_ready, NT * b + i + 1)
                    if i >= 2:
                        pe.wait_ge(x_t_ready, NT * b + i - 1)
                    for d in range(DC):
                        ins = nc.tensor.transpose(tr_ps[i % 2][:, d * P:(d + 1) * P], xn[i % 2][:, d * P:(d + 1) * P], ident[:])
                    ins.then_inc(xn_turned, 1)

            def head():
                turn_x(0)

            def scores(c, h, i, p):
                k, w = use_index(c, h, i), P * (i + 1)
                pe.wait_ge(exp_ready[i % 2], k)
                pe.wait_ge(x2_added[i % 2], NT // 2 * c)
                nc.tensor.matmul(score_ps[i % 2][:, 0:w], qr_t[p][:, h, i * P:(i + 1) * P], kr_t[p][:, 0:w],
                                 start=True, stop=False)
                nc.tensor.matmul(score_ps[i % 2][:, i * P:w], future_b[:], ident_b[:], start=False,
                                 stop=True).then_inc(scores_done, 1)

            def turn_probs(c, h, i):
                n = block_index(c, h, i)
                pe.wait_ge(prob_ready, n + 1)
                if i == 2:
                    pe.wait_ge(o_t_ready, G * c + h)
                else:
                    pe.wait_ge(past_copied, (NT - 1) * (G * c + h) + max(NT - 2 - i, 0))
                for j in range(i + 1):
                    ins = nc.tensor.transpose(prob_ps[i % 2][:, j * P:(j + 1) * P], prob[:, i % 2, j * P:(j + 1) * P], ident[:])
                ins.then_inc(prob_turned[i % 2], 1)

            def attend(c, h, p):
                pe.wait_ge(past_copied, (NT - 1) * (G * c + h + 1))
                pe.wait_ge(diag_ready, NT * (G * c + h + 1))
                pe.wait_ge(o_t_ready, G * c + h)
                pe.wait_ge(val_ready, NT * (c + 1))
                pe.wait_ge(q_in_ready, (NT - 1) * (c + 1))
                pe.wait_ge(state_ready, (NT - 1) * (c + 1))
                for j in range(NT):
                    nc.tensor.matmul(out_ps[:, j * P:SEQ], val[p][:, j, :], prob_t[:, j, j * P:SEQ],
                                     start=(j == 0), stop=False, skip_group_check=True)
                for i in range(1, NT):
                    ins = nc.tensor.matmul(out_ps[:, i * P:(i + 1) * P], state[p][:, i - 1, :],
                                           q_in[p][:, h, (i - 1) * P:i * P], start=False, stop=(i == NT - 1),
                                           skip_group_check=True)
                ins.then_inc(attended, 1)

            def project_first(c, g, tiles):
                for i in tiles:
                    pe.wait_ge(o_t_ready, G * (c + 1) - 1)
                    pe.wait_ge(exp_ready[i % 2], G * NT // 2 * (c + 1))
                    pe.wait_ge(x2_added[i % 2], NT // 2 * c + i // 2)
                    for h in range(G - 1):
                        for m, (o, w) in enumerate(THREE):
                            nc.tensor.matmul(score_ps[i % 2][:], o_t[o][:, h, i * P:(i + 1) * P], wo[w][:, G * g + h, :],
                                             start=(h == 0 and m == 0), stop=False)

            def project_last(c, g, tiles):
                for i in tiles:
                    pe.wait_ge(o_t_ready, G * (c + 1))
                    for m, (o, w) in enumerate(THREE):
                        ins = nc.tensor.matmul(score_ps[i % 2][:], o_t[o][:, G - 1, i * P:(i + 1) * P],
                                               wo[w][:, G * g + G - 1, :], start=False, stop=(m == 2))
                    ins.then_inc(projected, 1)

            def products(a, ub, i, gn):
                pe.wait_ge(x_t_ready, NT * (ub + 1))
                pe.wait_ge(val_ready, a)
                for d in range(DC):
                    for m, (x_part, w) in enumerate(THREE):
                        ins = nc.tensor.matmul(qkv_ps[:, 0:G * DH], x_t[x_part][:, d, i * P:(i + 1) * P],
                                               wq[w][:, d, gn * G * DH:(gn + 1) * G * DH],
                                               start=(d == 0 and m == 0), stop=(d == DC - 1 and m == 2))
                ins.then_inc(q_done, 1)
                for d in range(DC):
                    for m, (x_part, w) in enumerate(THREE):
                        ins = nc.tensor.matmul(qkv_ps[:, G * DH:G * DH + 2 * DH], x_t[x_part][:, d, i * P:(i + 1) * P],
                                               wkv[w][:, d, gn, :], start=(d == 0 and m == 0),
                                               stop=(d == DC - 1 and m == 2))
                ins.then_inc(kv_done, 1)

            def turn_features(a):
                pe.wait_ge(rot_ready, a + 1)
                pe.wait_ge(soft_ready, a + 1)
                pe.wait_ge(gate_ready, a + 1)
                pe.wait_ge(local_ready, a)
                nc.tensor.transpose(tr_ps[0][:, 0:P], rot[:, G * DH:QK], ident[:])
                nc.tensor.transpose(tr_ps[0][:, P:2 * P], soft[:, G * DH:QK], ident[:])
                nc.tensor.matmul(tr_ps[0][:, 2 * P:3 * P], gate[:], upto[:], start=True, stop=True)
                nc.tensor.matmul(tr_ps[0][:, 3 * P:4 * P], beyond[:], gate[:], start=True, stop=True).then_inc(keys_turned, 1)

            def turn_queries(a, ua, i):
                pe.wait_ge(state_ready, (NT - 1) * ua + min(i, NT - 1))
                pe.wait_ge(qr_t_ready, a)
                for h in range(G):
                    ins = nc.tensor.transpose(tr_ps[1][:, h * P:(h + 1) * P], rot[:, h * P:(h + 1) * P], ident[:])
                ins.then_inc(queries_turned, 1)

            def linear(a, ua, i, p):
                pe.wait_ge(keys_copied, a + 1)
                for h in range(G):
                    ins = nc.tensor.transpose(tr_ps[0][:, h * P:(h + 1) * P], soft[:, h * P:(h + 1) * P], ident[:])
                ins.then_inc(soft_turned, 1)
                if i < NT - 1:
                    pe.wait_ge(qr_t_ready, a + 1)
                    pe.wait_ge(k_rest_ready, (NT - 1) * ua + i + 1)
                    pe.wait_ge(val_ready, a + 1)
                    nc.tensor.matmul(tr_ps[1][:, 0:DH], k_rest[:], val[p][:, i, :], start=True, stop=True).then_inc(update_done, 1)

            def chunk_local(a, ua, i):
                pe.wait_ge(k_dec_ready, a + 1)
                pe.wait_ge(q_dec_ready, a + 1)
                pe.wait_ge(q_in_ready, (NT - 1) * ua + i)
                for s in range(NSUB):
                    m = SUB * (s + 1)
                    ins = nc.tensor.matmul(tr_ps[0][0:m, :].rearrange("p (h t) -> p h t", t=P)[:, :, m - SUB:m],
                                           k_dec[:, s, 0:m], q_dec[:, :, m - SUB:m], start=True, stop=True)
                ins.then_inc(local_done, 1)

            def unit(c, b, g, prepare, more):
                ua, p = (0, 0) if c is None else (c + 1, (g + 1) % 2)
                gn = 0 if c is None else (g + 1) % KV
                ub = 0 if c is None else b + (g + 1) // KV
                if c is None:
                    pe.wait_ge(w_low, STAGES)
                if c is not None:
                    pe.wait_ge(kr_t_ready, NT * (c + 1))
                    pe.wait_ge(qr_t_ready, NT * (c + 1))
                if c is not None:
                    scores(c, 0, 3, g % 2)
                    scores(c, 0, 2, g % 2)
                if more and g == KV - 1:
                    turn_x(b + 1)
                for s in range(NT):
                    if prepare and s == 0:
                        products(NT * ua, ub, 0, gn)
                    if c is not None:
                        turn_probs(c, s, 3)
                        scores(c, s, 1, g % 2)
                    if prepare and s:
                        turn_features(NT * ua + s - 1)
                        turn_queries(NT * ua + s - 1, ua, s - 1)
                    if c is not None:
                        turn_probs(c, s, 2)
                        scores(c, s, 0, g % 2)
                    if prepare and s:
                        products(NT * ua + s, ub, s, gn)
                        linear(NT * ua + s - 1, ua, s - 1, p)
                    if c is not None:
                        if s < G - 1:
                            scores(c, s + 1, 3, g % 2)
                            scores(c, s + 1, 2, g % 2)
                        turn_probs(c, s, 1)
                        turn_probs(c, s, 0)
                        if s == G - 1:
                            project_first(c, g, PROJECTION[:1])
                    if prepare and s:
                        chunk_local(NT * ua + s - 1, ua, s - 1)
                    if c is not None:
                        attend(c, s, g % 2)
                if prepare:
                    turn_features(NT * ua + NT - 1)
                    turn_queries(NT * ua + NT - 1, ua, NT - 1)
                if c is not None:
                    project_first(c, g, PROJECTION[1:2])
                    project_last(c, g, PROJECTION[:2])
                if prepare:
                    linear(NT * ua + NT - 1, ua, NT - 1, p)
                if c is not None:
                    project_first(c, g, PROJECTION[2:3])
                    project_last(c, g, PROJECTION[2:3])
                if prepare:
                    chunk_local(NT * ua + NT - 1, ua, NT - 1)
                if c is not None:
                    project_first(c, g, PROJECTION[3:])
                    project_last(c, g, PROJECTION[3:])
                else:
                    pe.wait_ge(w_low, STAGES + DC)
            each_sequence(pe, head, unit)


E_ = 32
GROUPS = 8
TOP_GROUPS = 3
K = 4
FF = 256
FC = FF // P
SH = 512
SC = SH // P
ROUTE_SCALE = 2.5
FAR = 1.0e6
PICKED = -1.0e30


H_SCALE = 2.0 ** 6


def capacity(tokens):
    return -(-5 * tokens // (4 * E_))


def slot_tiles(cap):
    n = -(-cap // P)
    assert cap % n == 0
    return n, cap // n


def routing_phase(nc, x2, router_w, e_bias, shared_gate, shared_up, shared_down, consts, y, base_dram, slots_dram,
                  weights_dram, tokens_dram):
    B = x2.shape[0]
    T = B * SEQ
    cap = capacity(T)
    ROUTE_STEPS = 56
    GE = E_ // GROUPS
    with ExitStack() as ctx:
        def sb(name, shape, dt=F32):
            return ctx.enter_context(nc.sbuf_tensor("r_" + name, shape, dt))

        def sem(name):
            return ctx.enter_context(nc.semaphore("r_" + name))

        ident = sb("ident", [P, P])
        before = sb("before", [P, P])
        before_b = sb("before_b", [P, P], BF16)
        ones_b = sb("ones_b", [P, P], BF16)
        rw = sb("rw", [E_, DM])
        rw_t = sb("rw_t", [P, DC, E_])
        bias = sb("bias", [P, E_])
        first = sb("first", [P, E_])
        order = sb("order", [P, E_])
        lower = sb("lower", [P, GROUPS, GROUPS])
        token = sb("token", [P, T // P, K])
        no_token = sb("no_token", [E_, cap])
        raw = [sb(f"raw{n}", [P, 4, DM]) for n in range(3)]
        turned_w = [[sb(f"w_t{n}_{part}", [P, 4, DM], FP16) for part in ("high", "low")] for n in range(3)]
        sg, su, sd = turned_w
        xb = sb("xb", [P, NT, DM])
        xr = sb("xr", [P, NT, DM])
        sig = sb("sig", [P, 2, SEQ])
        h = sb("h", [P, SC, SEQ])
        h_part = [sb(f"h_{part}", [P, SC, SEQ], FP16) for part in ("high", "low")]
        yn = sb("yn", [P, NT, DM])
        y_t = sb("y_t", [P, DC, SEQ])
        y_part = [sb(f"y_{part}", [P, DC, SEQ], FP16) for part in ("high", "low")]
        bn = sb("bn", [P, NT, 6])
        mv = sb("mv", [P, NT, 2])
        vpe = sb("vpe", [P, NT])
        rstd = sb("rstd", [P, NT])
        newton = sb("newton", [P, NT])
        score = sb("score", [P, NT, E_])
        biased = sb("biased", [P, NT, E_])
        hi = sb("hi", [P, NT * GROUPS, 2])
        lo = sb("lo", [P, NT * GROUPS, 2])
        gs = sb("gs", [P, NT, GROUPS])
        g2 = sb("g2", [P, NT * GROUPS])
        g3 = sb("g3", [P, NT * GROUPS])
        beats = sb("beats", [P, NT * GROUPS, GROUPS])
        ties = sb("ties", [P, NT * GROUPS, GROUPS])
        rank = sb("rank", [P, NT * GROUPS])
        v = sb("v", [P, NT, E_])
        cand = sb("cand", [P, NT, E_])
        top = sb("top", [P, NT])
        hot = sb("hot", [P, NT, K, E_])
        picked = sb("picked", [P, NT, E_], BF16)
        seen = sb("seen", [P, E_])
        seen_b = sb("seen_b", [P, NT, E_], BF16)
        over = sb("over", [P, NT, E_])
        slot = sb("slot", [P, NT, E_])
        prod = sb("prod", [P, NT, K, E_])
        wk = sb("wk", [P, NT, K])
        sk = sb("sk", [P, NT, K])
        ok = sb("ok", [P, NT, K])
        token_now = sb("token_now", [P, NT, K])
        sk_i = sb("sk_i", [P, NT, K], I32)
        wsum = sb("wsum", [P, NT])
        tr_ps = [ctx.enter_context(nc.psum_tensor(f"r_tr_ps{n}", [P, 512], F32)) for n in range(2)]
        gate_ps = [ctx.enter_context(nc.psum_tensor(f"r_gate_ps{n}", [P, 512], F32)) for n in range(2)]
        up_ps = [ctx.enter_context(nc.psum_tensor(f"r_up_ps{n}", [P, 512], F32)) for n in range(2)]
        down_ps = gate_ps
        lg_ps = ctx.enter_context(nc.psum_tensor("r_lg_ps", [P, NT, E_], F32))
        pos_ps = ctx.enter_context(nc.psum_tensor("r_pos_ps", [P, NT, E_], F32))

        loaded = sem("loaded")
        table_cleared = sem("table_cleared")
        cast = sem("cast")
        rw_turned = sem("rw_turned")
        rw_ready = sem("rw_ready")
        shared_loaded = sem("shared_loaded")
        w_turned = sem("w_turned")
        w_high_ready = sem("w_high_ready")
        w_ready = sem("w_ready")
        x_loaded = sem("x_loaded")
        xr_loaded = sem("xr_loaded")
        gate_done = sem("gate_done")
        up_done = sem("up_done")
        sig_ready = sem("sig_ready")
        h_step = sem("h_step")
        h_high_ready = sem("h_high_ready")
        h_low_ready = sem("h_low_ready")
        down_done = sem("down_done")
        summed = sem("summed")
        base_stored = sem("base_stored")
        y_stored = sem("y_stored")
        stats_step = sem("stats_step")
        root_step = sem("root_step")
        newton_step = sem("newton_step")
        yn_ready = sem("yn_ready")
        yn_turned = sem("yn_turned")
        y_t_ready = sem("y_t_ready")
        y_high_ready = sem("y_high_ready")
        y_low_ready = sem("y_low_ready")
        logits_done = sem("logits_done")
        score_ready = sem("score_ready")
        route_step = sem("route_step")
        picks_ready = sem("picks_ready")
        places_done = sem("places_done")
        slots_ready = sem("slots_ready")
        token_copied = sem("token_copied")
        slots_stored = sem("slots_stored")
        scattered = sem("scattered")
        ALL_LOADS = 16 * 9

        def each_sequence(eng, head, sequence):
            if head is not None:
                head(0)
            if B > 1:
                with eng.Fori(0, B - 1) as b:
                    sequence(b, False)
            sequence(B - 1, True)

        block = ctx.enter_context(nc.Block())

        @block.sync
        def _(sp):
            sp.dma_start(xb[:], x2[0].rearrange("(i p) d -> p i d", p=P)).then_inc(x_loaded, 16)
            sp.dma_start(no_token[:], consts["no_token"]).then_inc(loaded, 16)
            for to, name in ((ident, "ident"), (before, "before")):
                sp.dma_start(to[:], consts[name]).then_inc(loaded, 16)
            sp.dma_start(rw[:], router_w).then_inc(loaded, 16)
            sp.dma_start(bias[:], e_bias.partition_broadcast(P)).then_inc(loaded, 16)
            sp.dma_start(first[:], consts["first"].partition_broadcast(P)).then_inc(loaded, 16)
            sp.dma_start(order[:], consts["order"].partition_broadcast(P)).then_inc(loaded, 16)
            sp.dma_start(lower[:], consts["lower"].partition_broadcast(P)).then_inc(loaded, 16)
            sp.dma_start(token[:], consts["token"]).then_inc(loaded, 16)
            for to, w in zip(raw, (shared_gate, shared_up, shared_down)):
                sp.dma_start(to[:], w.rearrange("(r p) n -> p r n", p=P)).then_inc(shared_loaded, 16)
            sp.dma_start(xr[:], x2[0].rearrange("(i p) d -> p i d", p=P)).then_inc(xr_loaded, 16)
            sp.wait_ge(loaded, ALL_LOADS)
            sp.dma_start(tokens_dram.rearrange("(e c) o -> e (c o)", e=E_), no_token[:]).then_inc(table_cleared, 16)

            def sequence(b, last):
                sp.wait_ge(yn_ready, NT * (b + 1))
                if not last:
                    sp.dma_start(xb[:], x2[b + 1].rearrange("(i p) d -> p i d", p=P)).then_inc(x_loaded, 16)
                sp.dma_start(y[b].rearrange("(i p) d -> p i d", p=P), yn[:]).then_inc(y_stored, 16)
                sp.wait_ge(summed, NT * (b + 1))
                sp.dma_start(base_dram[b].rearrange("(i p) d -> p i d", p=P), xr[:]).then_inc(base_stored, 16)
                if not last:
                    sp.wait_ge(base_stored, 16 * (b + 1))
                    sp.dma_start(xr[:], x2[b + 1].rearrange("(i p) d -> p i d", p=P)).then_inc(xr_loaded, 16)
            each_sequence(sp, None, sequence)
            sp.wait_ge(y_stored, 16 * B)
            sp.wait_ge(base_stored, 16 * B)

        @block.gpsimd
        def _(pool):
            pool.wait_ge(loaded, ALL_LOADS)
            pool.wait_ge(table_cleared, 16)
            def y_low(b):
                for i in range(NT):
                    t = slice(i * P, (i + 1) * P)
                    pool.wait_ge(up_done, SC * b)
                    pool.wait_ge(y_high_ready, NT * b + i + 1)
                    nc.gpsimd.tensor_tensor(y_part[1][:, :, t], y_t[:, :, t], y_part[0][:, :, t], ALU.subtract).then_inc(y_low_ready, 1)

            def sequence(b, last):
                for f in range(SC):
                    pool.wait_ge(down_done, NT * b)
                    pool.wait_ge(h_high_ready, SC * b + f + 1)
                    nc.gpsimd.tensor_tensor(h_part[1][:, f, :], h[:, f, :], h_part[0][:, f, :], ALU.subtract).then_inc(h_low_ready, 1)
                if not last:
                    y_low(b + 1)
                pool.wait_ge(loaded, ALL_LOADS)
                pool.wait_ge(scattered, 16 * NT * K * b)
                nc.gpsimd.tensor_copy(token_now[:], token[:, bass.ts(b, NT), :]).then_inc(token_copied, 1)
                pool.wait_ge(token_copied, b + 1)
                pool.wait_ge(slots_ready, b + 1)
                pool.dma_start(slots_dram[b], sk_i[:].rearrange("p i k -> p (i k)")).then_inc(slots_stored, 16)
                pool.dma_start(weights_dram[b], wk[:].rearrange("p i k -> p (i k)")).then_inc(slots_stored, 16)
                for i in range(NT):
                    for k in range(K):
                        pool.indirect_dma_start(tokens_dram, bass.IndirectOffsetOnAxis(ap=sk_i[:, i, k:k + 1], axis=0),
                                                token_now[:, i, k:k + 1], None, bounds_check=E_ * cap - 1,
                                                oob_is_err=False).then_inc(scattered, 16)
            each_sequence(pool, y_low, sequence)
            pool.wait_ge(slots_stored, 32 * B)
            pool.wait_ge(scattered, 16 * NT * K * B)

        @block.scalar
        def _(act):
            act.preload_act_table_set("sigmoid_and_others")
            act.wait_ge(rw_turned, 1)
            nc.scalar.copy(rw_t[:], tr_ps[0][:, 0:DC * E_].rearrange("p (c e) -> p c e", e=E_)).then_inc(rw_ready, 1)
            def root(b):
                act.preload_act_table_set("natural_log_exp_and_others")
                act.wait_ge(stats_step, (2 * NT + 1) * (b + 1))
                nc.scalar.activation(rstd[:], vpe[:], ACT.Ln).then_inc(root_step, 1)
                act.wait_ge(root_step, 2 * b + 1)
                nc.scalar.activation(rstd[:], rstd[:], ACT.Exp, scale=-0.5).then_inc(root_step, 1)
                act.preload_act_table_set("sigmoid_and_others")

            def weights_high():
                for n in range(3):
                    for q in range(4):
                        m = 4 * n + q
                        act.wait_ge(w_turned, m + 1)
                        nc.scalar.activation(turned_w[n][0][:, :, q * P:(q + 1) * P], gate_ps[m % 2][:].rearrange("p (c t) -> p c t", c=4),
                                             ACT.Copy, scale=W_SCALE).then_inc(w_high_ready, 1)

            def features(b):
                for i in range(NT):
                    act.wait_ge(yn_turned, NT * b + i + 1)
                    act.wait_ge(logits_done, b)
                    act.wait_ge(y_low_ready, NT * b)
                    turned = tr_ps[i % 2][:].rearrange("p (c t) -> p c t", c=DC)
                    nc.scalar.activation(y_t[:, :, i * P:(i + 1) * P], turned, ACT.Copy, scale=X_SCALE).then_inc(y_t_ready, 1)
                    act.wait_ge(up_done, SC * b)
                    nc.scalar.activation(y_part[0][:, :, i * P:(i + 1) * P], turned, ACT.Copy, scale=X_SCALE).then_inc(y_high_ready, 1)

            def h_high(b, f):
                act.wait_ge(h_step, 2 * (SC * b + f + 1))
                act.wait_ge(down_done, NT * b)
                nc.scalar.copy(h_part[0][:, f, :], h[:, f, :]).then_inc(h_high_ready, 1)

            def router(b):
                act.wait_ge(logits_done, b + 1)
                act.wait_ge(route_step, ROUTE_STEPS * b)
                nc.scalar.activation(score[:], lg_ps[:], ACT.Sigmoid, scale=1.0 / X_SCALE).then_inc(score_ready, 1)

            def head(b):
                root(b)
                weights_high()
                features(b)
                router(b)

            def sequence(b, last):
                for f in range(SC):
                    m = SC * b + f
                    act.wait_ge(gate_done, m + 1)
                    act.wait_ge(h_step, 2 * (SC * b + (f - 1 if f >= 2 else 0)))
                    nc.scalar.activation(sig[:, f % 2, :], gate_ps[f % 2][:], ACT.Sigmoid, scale=1.0 / (X_SCALE * W_SCALE)).then_inc(sig_ready, 1)
                    if f:
                        h_high(b, f - 1)
                    if f == 2 and not last:
                        root(b + 1)
                h_high(b, SC - 1)
                if not last:
                    features(b + 1)
                    router(b + 1)
            each_sequence(act, head, sequence)

        @block.tensor
        def _(pe):
            pe.wait_ge(loaded, ALL_LOADS)
            pe.wait_ge(cast, 3)
            for d in range(DC):
                ins = nc.tensor.transpose(tr_ps[0][:, d * E_:(d + 1) * E_], rw[:, d * P:(d + 1) * P], ident[0:E_, 0:E_])
            ins.then_inc(rw_turned, 1)
            pe.wait_ge(rw_ready, 1)
            pe.wait_ge(shared_loaded, 16 * 3)
            for n in range(3):
                for q in range(4):
                    m = 4 * n + q
                    if m >= 2:
                        pe.wait_ge(w_ready, m - 1)
                    for d in range(4):
                        ins = nc.tensor.transpose(gate_ps[m % 2][:, d * P:(d + 1) * P], raw[n][:, q, d * P:(d + 1) * P], ident[:])
                    ins.then_inc(w_turned, 1)
            pe.wait_ge(w_ready, 12)

            def turn(b):
                for i in range(NT):
                    pe.wait_ge(yn_ready, NT * b + i + 1)
                    pe.wait_ge(y_high_ready, NT * b + (i - 1 if i >= 2 else 0))
                    for d in range(DC):
                        ins = nc.tensor.transpose(tr_ps[i % 2][:, d * P:(d + 1) * P], yn[:, i, d * P:(d + 1) * P], ident[:])
                    ins.then_inc(yn_turned, 1)

            def logits(b):
                pe.wait_ge(y_t_ready, NT * (b + 1))
                pe.wait_ge(score_ready, b)
                for i in range(NT):
                    for d in range(DC):
                        ins = nc.tensor.matmul(lg_ps[:, i, :], y_t[:, d, i * P:(i + 1) * P], rw_t[:, d, :],
                                               start=(d == 0), stop=(d == DC - 1))
                ins.then_inc(logits_done, 1)

            def places(b):
                pe.wait_ge(picks_ready, b + 1)
                for i in range(NT):
                    nc.tensor.matmul(pos_ps[:, i, :], before_b[:], picked[:, i, :], start=True, stop=False)
                    ins = nc.tensor.matmul(pos_ps[:, i, :], ones_b[:], seen_b[:, i, :], start=False, stop=True)
                ins.then_inc(places_done, 1)

            def down(b, tiles):
                for i in tiles:
                    pe.wait_ge(h_step, 2 * SC * (b + 1))
                    pe.wait_ge(h_low_ready, SC * (b + 1))
                    pe.wait_ge(summed, NT * b + (i - 1 if i >= 2 else 0))
                    for f in range(SC):
                        for m, (h_, w_) in enumerate(THREE):
                            ins = nc.tensor.matmul(down_ps[i % 2][:], h_part[h_][:, f, i * P:(i + 1) * P], sd[w_][:, f, :],
                                                   start=(f == 0 and m == 0), stop=(f == SC - 1 and m == 2))
                    ins.then_inc(down_done, 1)

            def head(b):
                turn(b)
                logits(b)

            def sequence(b, last):
                for f in range(SC):
                    pe.wait_ge(summed, NT * b)
                    pe.wait_ge(h_step, 2 * (SC * b + (f - 1 if f >= 2 else 0)))
                    pe.wait_ge(y_low_ready, NT * (b + 1))
                    for w, ps, done in ((sg, gate_ps, gate_done), (su, up_ps, up_done)):
                        for d in range(DC):
                            for m, (y_, w_) in enumerate(THREE):
                                ins = nc.tensor.matmul(ps[f % 2][:], w[w_][:, d, f * P:(f + 1) * P], y_part[y_][:, d, :],
                                                       start=(d == 0 and m == 0), stop=(d == DC - 1 and m == 2))
                        ins.then_inc(done, 1)
                if not last:
                    turn(b + 1)
                down(b, (0, 1, 2))
                places(b)
                down(b, (3,))
                if not last:
                    logits(b + 1)
            each_sequence(pe, head, sequence)

        @block.vector
        def _(dve):
            dve.wait_ge(loaded, ALL_LOADS)
            nc.vector.tensor_copy(before_b[:], before[:]).then_inc(cast, 1)
            nc.vector.memset(ones_b[:], 1.0).then_inc(cast, 1)
            nc.vector.memset(seen[:], 0.0).then_inc(cast, 1)
            dve.wait_ge(cast, 3)
            def statistics(b):
                base = (2 * NT + 1) * b
                dve.wait_ge(x_loaded, 16 * (b + 1))
                for i in range(NT):
                    nc.vector.bn_stats(bn[:, i, :], xb[:, i, :]).then_inc(stats_step, 1)
                dve.wait_ge(stats_step, base + NT)
                nc.vector.memset(newton[:], 0.0)
                for i in range(NT):
                    nc.vector.bn_aggr(mv[:, i, :], bn[:, i, :]).then_inc(stats_step, 1)
                dve.wait_ge(stats_step, base + 2 * NT)
                nc.vector.tensor_scalar(vpe[:], mv[:, :, 1], EPS, None, ALU.add).then_inc(stats_step, 1)

            def normalise(b):
                dve.wait_ge(root_step, 2 * b + 2)
                dve.wait_ge(stats_step, (2 * NT + 1) * (b + 1))
                for r in range(2):
                    n = 8 * b + 4 * r
                    dve.wait_ge(newton_step, n)
                    nc.vector.tensor_tensor(newton[:], rstd[:], rstd[:], ALU.mult).then_inc(newton_step, 1)
                    dve.wait_ge(newton_step, n + 1)
                    nc.vector.tensor_tensor(newton[:], newton[:], vpe[:], ALU.mult).then_inc(newton_step, 1)
                    dve.wait_ge(newton_step, n + 2)
                    nc.vector.tensor_scalar(newton[:], newton[:], -0.5, 1.5, ALU.mult, ALU.add).then_inc(newton_step, 1)
                    dve.wait_ge(newton_step, n + 3)
                    nc.vector.tensor_tensor(rstd[:], rstd[:], newton[:], ALU.mult).then_inc(newton_step, 1)
                dve.wait_ge(newton_step, 8 * b + 8)
                dve.wait_ge(y_stored, 16 * b)
                dve.wait_ge(yn_turned, NT * b)
                for i in range(NT):
                    nc.vector.tensor_scalar(yn[:, i, :], xb[:, i, :], mv[:, i, 0:1], rstd[:, i:i + 1],
                                            ALU.subtract, ALU.mult).then_inc(yn_ready, 1)

            now, steps = 0, 0

            def step(ins):
                nonlocal steps
                steps += 1
                ins.then_inc(route_step, 1)
                dve.wait_ge(route_step, ROUTE_STEPS * now + steps)

            def tt(out, a, c, op):
                return nc.vector.tensor_tensor(out, a, c, op)

            def over_experts(t):
                return t.unsqueeze(2).to_broadcast([P, NT, E_])

            def over_tiles(t):
                return t.unsqueeze(1).to_broadcast([P, NT, E_])

            def group_scores(b):
                nonlocal now, steps
                now, steps = b, 0
                dve.wait_ge(score_ready, b + 1)
                step(tt(biased[:], score[:], over_tiles(bias[:]), ALU.add))
                pairs = biased[:].rearrange("p i (g q r) -> p (i g) q r", q=GE // 2, r=2)
                step(tt(hi[:], pairs[:, :, :, 0], pairs[:, :, :, 1], ALU.max))
                step(tt(lo[:], pairs[:, :, :, 0], pairs[:, :, :, 1], ALU.min))
                gsf = gs[:].rearrange("p i g -> p (i g)")
                step(tt(gsf, hi[:, :, 0], hi[:, :, 1], ALU.max))
                step(tt(g2[:], hi[:, :, 0], hi[:, :, 1], ALU.min))
                step(tt(g3[:], lo[:, :, 0], lo[:, :, 1], ALU.max))
                step(tt(g2[:], g2[:], g3[:], ALU.max))
                step(tt(gsf, gsf, g2[:], ALU.add))

            def best_groups(b):
                for i in range(NT):
                    r = slice(i * GROUPS, (i + 1) * GROUPS)
                    other = gs[:, i, :].unsqueeze(1).to_broadcast([P, GROUPS, GROUPS])
                    own = gs[:, i, :].unsqueeze(2).to_broadcast([P, GROUPS, GROUPS])
                    tt(beats[:, r, :], other, own, ALU.is_gt)
                    ins = tt(ties[:, r, :], other, own, ALU.is_equal)
                step(ins)
                for i in range(NT):
                    r = slice(i * GROUPS, (i + 1) * GROUPS)
                    ins = tt(ties[:, r, :], ties[:, r, :], lower[:], ALU.mult)
                step(ins)
                step(tt(beats[:], beats[:], ties[:], ALU.add))
                step(nc.vector.tensor_reduce(rank[:], beats[:], AX_X, ALU.add))
                step(nc.vector.tensor_scalar(rank[:], rank[:], float(TOP_GROUPS), None, ALU.is_lt))
                step(tt(v[:].rearrange("p i (g q) -> p (i g) q", q=GE), biased[:].rearrange("p i (g q) -> p (i g) q", q=GE),
                        rank[:].unsqueeze(2).to_broadcast([P, NT * GROUPS, GE]), ALU.mult))

            def picks(ks):
                for k in ks:
                    step(nc.vector.tensor_reduce(top[:], v[:], AX_X, ALU.max))
                    step(tt(cand[:], v[:], over_experts(top[:]), ALU.is_equal))
                    step(tt(cand[:], cand[:], over_tiles(order[:]), ALU.mult))
                    step(nc.vector.tensor_reduce(top[:], cand[:], AX_X, ALU.max))
                    step(tt(hot[:, :, k, :], cand[:], over_experts(top[:]), ALU.is_equal))
                    step(nc.vector.scalar_tensor_tensor(out=v[:], in0=hot[:, :, k, :], scalar=PICKED, in1=v[:],
                                                        op0=ALU.mult, op1=ALU.add))

            def count_picks(b):
                dve.wait_ge(places_done, b)
                step(nc.vector.tensor_scalar(cand[:], v[:], 0.5 * PICKED, None, ALU.is_lt))
                for i in range(NT):
                    nc.vector.tensor_copy(seen_b[:, i, :], seen[:])
                    step(tt(seen[:], seen[:], cand[:, i, :], ALU.add))
                nc.vector.tensor_copy(picked[:], cand[:]).then_inc(picks_ready, 1)

            def pick_weights(b):
                dve.wait_ge(slots_stored, 32 * b)
                dve.wait_ge(scattered, 16 * NT * K * b)
                step(tt(prod[:], hot[:], score[:].unsqueeze(2).to_broadcast([P, NT, K, E_]), ALU.mult))
                step(nc.vector.tensor_reduce(wk[:], prod[:], AX_X, ALU.add))
                step(nc.vector.tensor_reduce(wsum[:], wk[:], AX_X, ALU.add))
                step(nc.vector.tensor_scalar(wsum[:], wsum[:], 1e-20, None, ALU.add))
                step(nc.vector.reciprocal(wsum[:], wsum[:]))
                step(tt(wk[:], wk[:], wsum[:].unsqueeze(2).to_broadcast([P, NT, K]), ALU.mult))

            def pick_slots(b):
                dve.wait_ge(places_done, b + 1)
                step(nc.vector.tensor_scalar(over[:], pos_ps[:], float(cap), FAR, ALU.is_ge, ALU.mult))
                step(tt(slot[:], pos_ps[:], over_tiles(first[:]), ALU.add))
                step(tt(slot[:], slot[:], over[:], ALU.add))
                step(tt(prod[:], hot[:], slot[:].unsqueeze(2).to_broadcast([P, NT, K, E_]), ALU.mult))
                step(nc.vector.tensor_reduce(sk[:], prod[:], AX_X, ALU.add))
                step(nc.vector.tensor_scalar(ok[:], sk[:], FAR, ROUTE_SCALE, ALU.is_lt, ALU.mult))
                step(tt(wk[:], wk[:], ok[:], ALU.mult))
                nc.vector.tensor_copy(sk_i[:], sk[:]).then_inc(slots_ready, 1)
                assert steps == ROUTE_STEPS, steps

            def silu_product(b, f):
                m = SC * b + f
                dve.wait_ge(sig_ready, m + 1)
                nc.vector.tensor_tensor(sig[:, f % 2, :], sig[:, f % 2, :], gate_ps[f % 2][:], ALU.mult).then_inc(h_step, 1)
                dve.wait_ge(h_step, 2 * m + 1)
                dve.wait_ge(up_done, m + 1)
                dve.wait_ge(h_low_ready, SC * b)
                nc.vector.scalar_tensor_tensor(out=h[:, f, :], in0=sig[:, f % 2, :], scalar=O_SCALE / (X_SCALE * W_SCALE) ** 2,
                                               in1=up_ps[f % 2][:], op0=ALU.mult, op1=ALU.mult).then_inc(h_step, 1)

            def residual(b, i):
                dve.wait_ge(xr_loaded, 16 * (b + 1))
                dve.wait_ge(down_done, NT * b + i + 1)
                nc.vector.scalar_tensor_tensor(out=xr[:, i, :], in0=down_ps[i % 2][:], scalar=1.0 / (O_SCALE * W_SCALE),
                                               in1=xr[:, i, :], op0=ALU.mult, op1=ALU.add).then_inc(summed, 1)

            def head(b):
                statistics(b)
                normalise(b)
                for n in range(3):
                    for q in range(4):
                        m = 4 * n + q
                        dve.wait_ge(w_high_ready, m + 1)
                        c = slice(q * P, (q + 1) * P)
                        nc.vector.scalar_tensor_tensor(out=turned_w[n][1][:, :, c], in0=gate_ps[m % 2][:].rearrange("p (c t) -> p c t", c=4),
                                                       scalar=W_SCALE, in1=turned_w[n][0][:, :, c], op0=ALU.mult,
                                                       op1=ALU.subtract).then_inc(w_ready, 1)

            def sequence(b, last):
                group_scores(b)
                silu_product(b, 0)
                best_groups(b)
                silu_product(b, 1)
                if not last:
                    statistics(b + 1)
                picks((0,))
                silu_product(b, 2)
                if not last:
                    normalise(b + 1)
                silu_product(b, 3)
                picks((1, 2, 3))
                count_picks(b)
                residual(b, 0)
                residual(b, 1)
                pick_weights(b)
                residual(b, 2)
                pick_slots(b)
                residual(b, 3)
            each_sequence(dve, head, sequence)


def expert_phase(nc, y, w_gate, w_up, w_down, consts, tokens_dram, y_out):
    T = y.shape[0] * SEQ
    cap = capacity(T)
    n_ct, ct = slot_tiles(cap)
    UNROLL = 4
    ROUNDS = E_ // UNROLL
    yf = y.rearrange("b t d -> (b t) d")
    with ExitStack() as ctx:
        def sb(name, shape, dt=F32):
            return ctx.enter_context(nc.sbuf_tensor("e_" + name, shape, dt))

        def sem(name):
            return ctx.enter_context(nc.semaphore("e_" + name))

        def sems(name, n):
            return [sem(f"{name}{i}") for i in range(n)]

        def banks(name):
            return [ctx.enter_context(nc.psum_tensor(f"e_{name}{n}", [P, 512], F32)) for n in range(2)]

        ident = sb("ident", [P, P])
        spare = sb("spare", [P, 1 + UNROLL])
        who = sb("who", [E_, cap])
        who_i = sb("who_i", [ct, n_ct, E_], I32)
        now = [sb(f"now{n}", [ct, n_ct], I32) for n in range(UNROLL)]
        wg = [sb(f"wg{n}", [P, DC, FF]) for n in range(UNROLL)]
        wu = [sb(f"wu{n}", [P, DC, FF]) for n in range(UNROLL)]
        wd = [sb(f"wd{n}", [P, FC, DM]) for n in range(UNROLL)]
        xg = [[sb(f"xg{n}_{j}", [ct, DM]) for j in range(n_ct)] for n in range(UNROLL)]
        wg_part, wu_part, wd_part = ([[sb(f"{name}{n}_{part}", shape, FP16) for part in ("high", "low")] for n in range(2)]
                                     for name, shape in (("wg", [P, DC, FF]), ("wu", [P, DC, FF]), ("wd", [P, FC, DM])))
        xp_t = [[sb(f"xp_t{n}_{part}", [P, DC, cap], FP16) for part in ("high", "low")] for n in range(2)]
        sig = [sb(f"sig{n}", [P, FC, cap]) for n in range(2)]
        h = [sb(f"h{n}", [P, FC, cap]) for n in range(2)]
        h_part = [[sb(f"h{n}_{part}", [P, FC, cap], FP16) for part in ("high", "low")] for n in range(2)]
        yo = [sb(f"yo{n}", [ct, n_ct, DM]) for n in range(UNROLL)]
        tr_ps, gate_ps, up_ps, down_ps = banks("tr_ps"), banks("gate_ps"), banks("up_ps"), banks("down_ps")

        def by_chunk(bank):
            return bank[:, 0:FC * cap].rearrange("p (c t) -> p c t", c=FC)

        loaded = sem("loaded")
        cleared = sem("cleared")
        who_turned = sem("who_turned")
        who_ready = sem("who_ready")
        now_ready = sem("now_ready")
        w_high = sem("w_high")
        w_low = sem("w_low")
        x_high_ready = sem("x_high_ready")
        h_high_ready = sem("h_high_ready")
        h_low_ready = sem("h_low_ready")
        up_loaded = sems("up_loaded", UNROLL)
        down_loaded = sems("down_loaded", UNROLL)
        gathered = sems("gathered", UNROLL)
        stored = sems("stored", UNROLL)
        turned = sem("turned")
        xp_ready = sem("xp_ready")
        gate_done = sem("gate_done")
        up_done = sem("up_done")
        sig_ready = sem("sig_ready")
        h_step = sem("h_step")
        down_done = sem("down_done")
        yo_ready = sem("yo_ready")

        def before(r, n):
            return (r, n - 1) if n else (r - 1, UNROLL - 1)

        def after(r, n):
            return (r, n + 1) if n < UNROLL - 1 else (r + 1, 0)

        def each_expert(eng, expert):
            def in_round(r, first, last):
                for n in range(UNROLL):
                    expert(r, n, first and n == 0, last and n == UNROLL - 1)
            in_round(0, True, False)
            with eng.Fori(1, ROUNDS - 1) as r:
                in_round(r, False, False)
            in_round(ROUNDS - 1, False, True)

        block = ctx.enter_context(nc.Block())

        @block.sync
        def _(sp):
            sp.dma_start(who[:], tokens_dram.rearrange("(e c) o -> e (c o)", e=E_)).then_inc(loaded, 16)
            sp.dma_start(ident[:], consts["ident"]).then_inc(loaded, 16)

            def load(r, n, first):
                e = UNROLL * r + n
                if not first:
                    sp.wait_ge(w_low, 3 * (e - UNROLL) + 2)
                sp.dma_start(wg[n][:], w_gate[e].rearrange("(c p) i -> p c i", p=P)).then_inc(up_loaded[n], 16)
                sp.dma_start(wu[n][:], w_up[e].rearrange("(c p) i -> p c i", p=P)).then_inc(up_loaded[n], 16)
                if not first:
                    sp.wait_ge(w_low, 3 * (e - UNROLL) + 3)
                sp.dma_start(wd[n][:], w_down[e].rearrange("(c p) d -> p c d", p=P)).then_inc(down_loaded[n], 16)

            load(0, 0, True)
            sp.wait_ge(gathered[0], 16 * n_ct)
            for n in range(1, UNROLL):
                load(0, n, True)
            with sp.Fori(1, ROUNDS) as r:
                for n in range(UNROLL):
                    load(r, n, False)

        @block.gpsimd
        def _(pool):
            for n in range(UNROLL):
                for j in range(n_ct):
                    nc.gpsimd.memset(xg[n][j][:], 0.0)
            nc.gpsimd.memset(spare[:], 0.0).then_inc(cleared, 1)
            pool.wait_ge(cleared, 1)
            pool.wait_ge(who_ready, 1)

            def gather(r, n, first):
                pool.wait_ge(gathered[n], 16 * n_ct * r)
                pool.wait_ge(who_ready, 1)
                nc.gpsimd.tensor_copy(now[n][:], who_i[:, :, bass.ds(UNROLL * r + n, 1)].rearrange("p j e -> p (j e)")).then_inc(now_ready, 1)
                pool.wait_ge(now_ready, UNROLL * r + n + 1)
                if not first:
                    pool.wait_ge(turned, n_ct * (UNROLL * (r - 1) + n + 1))
                nc.gpsimd.tensor_tensor(spare[:, 1 + n:2 + n], spare[:, 0:1], spare[:, 0:1], ALU.add)
                for j in range(n_ct):
                    pool.indirect_dma_start(xg[n][j][:], None, yf, bass.IndirectOffsetOnAxis(ap=now[n][:, j:j + 1], axis=0),
                                            bounds_check=T - 1, oob_is_err=False).then_inc(gathered[n], 16)

            for n in range(UNROLL):
                gather(0, n, True)
            with pool.Fori(1, ROUNDS) as r:
                for n in range(UNROLL):
                    gather(r, n, False)

        @block.scalar
        def _(act):
            act.preload_act_table_set("sigmoid_and_others")

            def copy_turned(e, p):
                for j in range(n_ct):
                    act.wait_ge(turned, n_ct * e + j + 1)
                    nc.scalar.activation(xp_t[p][0][:, :, j * ct:(j + 1) * ct],
                                         tr_ps[j % 2][:, 0:DC * ct].rearrange("p (c t) -> p c t", c=DC),
                                         ACT.Copy, scale=X_SCALE).then_inc(x_high_ready, 1)

            def copy_down(r, n):
                e = UNROLL * r + n
                act.wait_ge(stored[n], 16 * r)
                for j in range(n_ct):
                    act.wait_ge(down_done, n_ct * e + j + 1)
                    nc.scalar.activation(yo[n][:, j, :], down_ps[j % 2][0:ct, :], ACT.Copy,
                                         scale=1.0 / (H_SCALE * W_SCALE)).then_inc(yo_ready, 1)
                act.wait_ge(yo_ready, n_ct * (e + 1))
                act.dma_start(y_out[e].rearrange("(j p) d -> p j d", p=ct), yo[n][:]).then_inc(stored[n], 16)

            def up_high(r, n, fresh):
                act.wait_ge(up_loaded[n], 32 * (r + 1))
                if not fresh:
                    act.wait_ge(up_done, UNROLL * r + n - 1)
                for whole, part in ((wg, wg_part), (wu, wu_part)):
                    nc.scalar.activation(part[n % 2][0][:], whole[n][:], ACT.Copy, scale=W_SCALE).then_inc(w_high, 1)

            def down_high(r, n, first):
                act.wait_ge(down_loaded[n], 16 * (r + 1))
                if not first:
                    act.wait_ge(down_done, n_ct * (UNROLL * r + n - 1))
                nc.scalar.activation(wd_part[n % 2][0][:], wd[n][:], ACT.Copy, scale=W_SCALE).then_inc(w_high, 1)

            def expert(r, n, first, last):
                e = UNROLL * r + n
                down_high(r, n, first)
                if not last:
                    up_high(*after(r, n), first)
                    copy_turned(e + 1, (n + 1) % 2)
                act.wait_ge(gate_done, e + 1)
                if not first:
                    act.wait_ge(h_step, 2 * (e - 1))
                nc.scalar.activation(sig[n % 2][:], by_chunk(gate_ps[n % 2]), ACT.Sigmoid,
                                     scale=1.0 / (X_SCALE * W_SCALE)).then_inc(sig_ready, 1)
                if not first:
                    copy_down(*before(r, n))
                act.wait_ge(h_step, 2 * (e + 1))
                nc.scalar.copy(h_part[n % 2][0][:], h[n % 2][:]).then_inc(h_high_ready, 1)

            up_high(0, 0, True)
            copy_turned(0, 0)
            each_expert(act, expert)
            copy_down(ROUNDS - 1, UNROLL - 1)
            for n in range(UNROLL):
                act.wait_ge(stored[n], 16 * ROUNDS)

        @block.vector
        def _(dve):
            dve.wait_ge(who_turned, 1)
            nc.vector.tensor_copy(who_i[:], gate_ps[0][0:ct, 0:n_ct * E_].rearrange("p (j e) -> p j e", e=E_)).then_inc(who_ready, 1)

            def low(part, whole, scale):
                return nc.vector.scalar_tensor_tensor(out=part[1], in0=whole, scalar=scale, in1=part[0], op0=ALU.mult,
                                                      op1=ALU.subtract)

            def up_low(r, n, fresh):
                e = UNROLL * r + n
                if not fresh:
                    dve.wait_ge(up_done, e - 1)
                for m, (whole, part) in enumerate(((wg, wg_part), (wu, wu_part))):
                    dve.wait_ge(w_high, 3 * e + m + 1)
                    low([t[:] for t in part[n % 2]], whole[n][:], W_SCALE).then_inc(w_low, 1)

            def down_low(r, n, first):
                e = UNROLL * r + n
                if not first:
                    dve.wait_ge(down_done, n_ct * (e - 1))
                dve.wait_ge(w_high, 3 * e + 3)
                low([t[:] for t in wd_part[n % 2]], wd[n][:], W_SCALE).then_inc(w_low, 1)

            def x_low(r, n):
                for j in range(n_ct):
                    dve.wait_ge(x_high_ready, n_ct * (UNROLL * r + n) + j + 1)
                    low([t[:, :, j * ct:(j + 1) * ct] for t in xp_t[n % 2]],
                        tr_ps[j % 2][:, 0:DC * ct].rearrange("p (c t) -> p c t", c=DC), X_SCALE).then_inc(xp_ready, 1)

            def expert(r, n, first, last):
                e = UNROLL * r + n
                down_low(r, n, first)
                if not last:
                    up_low(*after(r, n), first)
                    x_low(*after(r, n))
                dve.wait_ge(sig_ready, e + 1)
                nc.vector.tensor_tensor(sig[n % 2][:], sig[n % 2][:], by_chunk(gate_ps[n % 2]), ALU.mult).then_inc(h_step, 1)
                dve.wait_ge(h_step, 2 * e + 1)
                dve.wait_ge(up_done, e + 1)
                nc.vector.scalar_tensor_tensor(out=h[n % 2][:], in0=sig[n % 2][:], scalar=H_SCALE / (X_SCALE * W_SCALE) ** 2,
                                               in1=by_chunk(up_ps[n % 2]), op0=ALU.mult, op1=ALU.mult).then_inc(h_step, 1)
                dve.wait_ge(h_high_ready, e + 1)
                nc.vector.tensor_tensor(h_part[n % 2][1][:], h[n % 2][:], h_part[n % 2][0][:], ALU.subtract).then_inc(h_low_ready, 1)

            up_low(0, 0, True)
            x_low(0, 0)
            each_expert(dve, expert)

        @block.tensor
        def _(pe):
            pe.wait_ge(loaded, 32)
            for j in range(n_ct):
                ins = nc.tensor.transpose(gate_ps[0][0:ct, j * E_:(j + 1) * E_], who[:, j * ct:(j + 1) * ct], ident[0:E_, 0:E_])
            ins.then_inc(who_turned, 1)
            pe.wait_ge(who_ready, 1)

            def turn(r, n):
                e = UNROLL * r + n
                pe.wait_ge(gathered[n], 16 * n_ct * (r + 1))
                for j in range(n_ct):
                    pe.wait_ge(xp_ready, n_ct * e + max(j - 1, 0))
                    for d in range(DC):
                        ins = nc.tensor.transpose(tr_ps[j % 2][:, d * ct:(d + 1) * ct], xg[n][j][:, d * P:(d + 1) * P],
                                                  ident[0:ct, 0:ct])
                    ins.then_inc(turned, 1)

            def down(r, n):
                e = UNROLL * r + n
                pe.wait_ge(h_low_ready, e + 1)
                pe.wait_ge(w_low, 3 * e + 3)
                for j in range(n_ct):
                    pe.wait_ge(yo_ready, n_ct * e + max(j - 1, 0))
                    for f in range(FC):
                        for m, (h_, w_) in enumerate(THREE):
                            ins = nc.tensor.matmul(down_ps[j % 2][0:ct, :], h_part[n % 2][h_][:, f, j * ct:(j + 1) * ct],
                                                   wd_part[n % 2][w_][:, f, :], start=(f == 0 and m == 0),
                                                   stop=(f == FC - 1 and m == 2))
                    ins.then_inc(down_done, 1)

            def expert(r, n, first, last):
                e = UNROLL * r + n
                pe.wait_ge(xp_ready, n_ct * (e + 1))
                pe.wait_ge(w_low, 3 * e + 2)
                if not first:
                    pe.wait_ge(h_step, 2 * (e - 1))
                for w, ps, done in ((wg_part, gate_ps, gate_done), (wu_part, up_ps, up_done)):
                    for f in range(FC):
                        for d in range(DC):
                            for m, (x_, w_) in enumerate(THREE):
                                ins = nc.tensor.matmul(ps[n % 2][:, f * cap:(f + 1) * cap], w[n % 2][w_][:, d, f * P:(f + 1) * P],
                                                       xp_t[n % 2][x_][:, d, :], start=(d == 0 and m == 0),
                                                       stop=(d == DC - 1 and m == 2))
                    ins.then_inc(done, 1)
                if not last:
                    turn(*after(r, n))
                if not first:
                    down(*before(r, n))

            turn(0, 0)
            each_expert(pe, expert)
            down(ROUNDS - 1, UNROLL - 1)


def combine_phase(nc, base_dram, consts, slots_dram, weights_dram, y_out, out):
    B = base_dram.shape[0]
    cap = capacity(B * SEQ)
    rows = y_out.rearrange("e c d -> (e c) d")
    with ExitStack() as ctx:
        def sb(name, shape, dt=F32):
            return ctx.enter_context(nc.sbuf_tensor("c_" + name, shape, dt))

        def sem(name):
            return ctx.enter_context(nc.semaphore("c_" + name))

        def sems(name):
            return [sem(f"{name}{i}") for i in range(NT)]

        acc = sb("acc", [P, NT, DM])
        part = sb("part", [P, NT, K, DM])
        spare = sb("spare", [P, 1 + NT])
        all_slots = sb("all_slots", [P, B, NT * K], I32)
        all_weights = sb("all_weights", [P, B, NT * K])
        slots = sb("slots", [P, NT, K], I32)
        wk = sb("wk", [P, NT, K])

        tables_loaded = sem("tables_loaded")
        cleared = sem("cleared")
        slots_copied = sem("slots_copied")
        base_loaded = sems("base_loaded")
        gathered = sems("gathered")
        summed = sems("summed")
        stored = sems("stored")
        block = ctx.enter_context(nc.Block())

        @block.sync
        def _(sp):
            sp.dma_start(all_slots[:], slots_dram.rearrange("b p k -> p b k")).then_inc(tables_loaded, 16)
            sp.dma_start(all_weights[:], weights_dram.rearrange("b p k -> p b k")).then_inc(tables_loaded, 16)
            with sp.Fori(0, B) as b:
                for i in range(NT):
                    sp.wait_ge(base_loaded[i], 16 * b)
                    sp.wait_ge(stored[i], 16 * b)
                    sp.dma_start(acc[:, i, :], base_dram[b, i * P:(i + 1) * P, :]).then_inc(base_loaded[i], 16)

        @block.gpsimd
        def _(pool):
            nc.gpsimd.memset(part[:], 0.0)
            nc.gpsimd.memset(spare[:], 0.0).then_inc(cleared, 1)
            pool.wait_ge(cleared, 1)
            with pool.Fori(0, B) as b:
                for i in range(NT):
                    pool.wait_ge(gathered[i], 16 * K * b)
                    pool.wait_ge(summed[i], K * b)
                    pool.wait_ge(tables_loaded, 32)
                    nc.gpsimd.tensor_copy(slots[:, i, :], all_slots[:, bass.ds(b, 1), K * i:K * (i + 1)].rearrange("p b k -> p (b k)")).then_inc(slots_copied, 1)
                    nc.gpsimd.tensor_copy(wk[:, i, :], all_weights[:, bass.ds(b, 1), K * i:K * (i + 1)].rearrange("p b k -> p (b k)")).then_inc(slots_copied, 1)
                    pool.wait_ge(slots_copied, 2 * (NT * b + i + 1))
                    nc.gpsimd.tensor_tensor(spare[:, 1 + i:2 + i], spare[:, 0:1], spare[:, 0:1], ALU.add)
                    for k in range(K):
                        pool.indirect_dma_start(part[:, i, k, :], None, rows, bass.IndirectOffsetOnAxis(ap=slots[:, i, k:k + 1], axis=0),
                                                bounds_check=E_ * cap - 1, oob_is_err=False).then_inc(gathered[i], 16)

        @block.scalar
        def _(act):
            with act.Fori(0, B) as b:
                for i in range(NT):
                    act.wait_ge(summed[i], K * (b + 1))
                    act.dma_start(out[b, i * P:(i + 1) * P, :], acc[:, i, :]).then_inc(stored[i], 16)
            for i in range(NT):
                act.wait_ge(stored[i], 16 * B)

        @block.vector
        def _(dve):
            with dve.Fori(0, B) as b:
                for i in range(NT):
                    dve.wait_ge(base_loaded[i], 16 * (b + 1))
                    dve.wait_ge(slots_copied, 2 * (NT * b + i + 1))
                    dve.wait_ge(gathered[i], 16 * K * (b + 1))
                    for k in range(K):
                        dve.wait_ge(summed[i], K * b + k)
                        nc.vector.scalar_tensor_tensor(out=acc[:, i, :], in0=part[:, i, k, :], scalar=wk[:, i, k:k + 1],
                                                       in1=acc[:, i, :], op0=ALU.mult, op1=ALU.add).then_inc(summed[i], 1)


def host_constants():
    inv = (1.0 / np.float32(ROPE_THETA) ** (np.arange(0, DH, 2, dtype=np.float32) / np.float32(DH))).astype(np.float32)
    ang = (np.arange(SEQ, dtype=np.float32)[:, None] * inv[None, :]).astype(np.float32)
    at = np.arange(P)
    return {
        "rope": np.stack([np.cos(ang), np.sin(ang)], 1).astype(np.float32),
        "ident": np.eye(P, dtype=np.float32),
        "upto": (at[:, None] <= at[None, :]).astype(np.float32) / np.float32(GATE_NORM),
        "beyond": (at[:, None] > at[None, :]).astype(np.float32) / np.float32(GATE_NORM),
        "keep": (at[:, None] <= at[None, :]).astype(np.float32),
    }


def host_constants2(T):
    cap = capacity(T)
    at = np.arange(P)
    c = host_constants()
    c["before"] = (at[:, None] < at[None, :]).astype(np.float32)
    c["first"] = (np.arange(E_) * cap).astype(np.float32)
    c["order"] = (E_ - np.arange(E_)).astype(np.float32)
    g = np.arange(GROUPS)
    c["lower"] = (g[None, :] < g[:, None]).astype(np.float32)
    c["token"] = np.repeat((np.arange(T // P)[None, :] * P + at[:, None])[:, :, None], K, 2).astype(np.float32)
    c["no_token"] = np.full((E_, cap), T, np.float32)
    return c


def block_kernel(nc, a, consts, out):
    x = a["L0_attn_hidden_states"]
    B = x.shape[0]
    cap = capacity(B * SEQ)

    def scratch(name, shape, dt=F32):
        return nc.dram_tensor(name, shape, dt, kind="Internal").ap()

    x2 = scratch("x2", [B, SEQ, DM])
    y = scratch("y", [B, SEQ, DM])
    base = scratch("base", [B, SEQ, DM])
    slots = scratch("slots", [B, P, NT * K], I32)
    weights = scratch("weights", [B, P, NT * K])
    tokens = scratch("tokens", [E_ * cap, 1])
    y_out = scratch("y_out", [E_, cap, DM])
    attention_phase(nc, x, a["L0_attn_Wq"], a["L0_attn_Wk"], a["L0_attn_Wv"], a["L0_attn_Wo"], consts, x2)
    routing_phase(nc, x2, a["L0_ffn_router_w"], a["L0_ffn_e_bias"], a["L0_ffn_shared_gate"], a["L0_ffn_shared_up"],
                  a["L0_ffn_shared_down"], consts, y, base, slots, weights, tokens)
    expert_phase(nc, y, a["L0_ffn_W_gate"], a["L0_ffn_W_up"], a["L0_ffn_W_down"], consts, tokens, y_out)
    combine_phase(nc, base, consts, slots, weights, y_out, out)


_INS = ["L0_attn_hidden_states", "L0_attn_Wq", "L0_attn_Wk", "L0_attn_Wv", "L0_attn_Wo", "L0_ffn_router_w",
        "L0_ffn_e_bias", "L0_ffn_W_gate", "L0_ffn_W_up", "L0_ffn_W_down", "L0_ffn_shared_gate", "L0_ffn_shared_up",
        "L0_ffn_shared_down"]


def kernel(**inputs):
    import concourse.bacc as _bacc
    from concourse.bass_utils import run_bass_kernel_spmd as _run

    nc = _bacc.Bacc("TRN2", target_bir_lowering=False, num_devices=1)
    arrays, ins, consts = {}, {}, {}
    for name in _INS:
        a = np.ascontiguousarray(inputs[name])
        arrays[f"in_{name}_dram"] = a
        ins[name] = nc.dram_tensor(f"in_{name}_dram", a.shape, mybir.dt.from_np(a.dtype), kind="ExternalInput").ap()
    shape = inputs["L0_attn_hidden_states"].shape
    for name, a in host_constants2(shape[0] * shape[1]).items():
        arrays[f"const_{name}_dram"] = a
        consts[name] = nc.dram_tensor(f"const_{name}_dram", a.shape, mybir.dt.from_np(a.dtype), kind="ExternalInput").ap()
    out = nc.dram_tensor("out_0_dram", shape, F32, kind="ExternalOutput").ap()
    block_kernel(nc, ins, consts, out)
    r = _run(nc, [arrays], core_ids=[0])
    return r.results[0]["out_0_dram"]
```
